# Optimizing a Trainium2 kernel written in Bass

```python
import numpy as np
import jax
import jax.numpy as jnp

def _softmax(x, axis=-1):
    return jax.nn.softmax(x, axis=axis)

def _gelu(x):
    return jax.nn.gelu(x, approximate=True)

def _silu(x):
    return jax.nn.silu(x)

def _sigmoid(x):
    return jax.nn.sigmoid(x)

def _layernorm(x, axis=-1, eps=1e-05):
    m = jnp.mean(x, axis=axis, keepdims=True)
    v = jnp.var(x, axis=axis, keepdims=True)
    return (x - m) / jnp.sqrt(v + eps)

def _scatter_add(tgt, idx, src, axis=0):
    return tgt.at[idx].add(src)

def _segment_sum(src, seg, n):
    return jax.ops.segment_sum(src, seg, n)
kernel_name = 'mk_lm_tower_d1_tok_ids512_r4_dcf1d0'

def setup_inputs(seed: int=0):
    np.random.seed(seed)
    _w = jnp.asarray

    def _rec_inputs():
        import jax
        import jax.numpy as jnp
        _rk = jax.random.key(seed)
        x = jax.random.randint(jax.random.fold_in(_rk, 1), (64, 96), 0, 31983, jnp.int32)
        return x
    x = _rec_inputs()

    def _L0_tok_setup():
        import jax, jax.numpy as jnp
        import numpy as np
        D_MODEL = 128
        D_FF = 512
        VOCAB = 8000
        B, N = (2, 96)
        EPS = 1e-06

        def positional_encoding(n, d):
            pos = np.arange(n)[:, None].astype(np.float64)
            i = np.arange(d)[None, :]
            ang = pos / np.power(10000.0, 2 * (i // 2) / np.float32(d))
            ang[:, 0::2] = np.sin(ang[:, 0::2])
            ang[:, 1::2] = np.cos(ang[:, 1::2])
            return jnp.asarray(ang, dtype=jnp.float32)

        def layer_norm(x, gamma, beta):
            mu = jnp.mean(x, axis=-1, keepdims=True)
            var = jnp.mean(jnp.square(x - mu), axis=-1, keepdims=True)
            return (x - mu) / jnp.sqrt(var + EPS) * gamma + beta
        key = jax.random.key(seed)
        ks = jax.random.split(key, 12)
        s = 0.02
        return {'tokens': jax.random.randint(ks[0], (B, N), 0, VOCAB, dtype=jnp.int32), 'emb': jax.random.normal(ks[1], (VOCAB, D_MODEL), jnp.float32) * s, 'Wq': jax.random.normal(ks[2], (D_MODEL, D_MODEL), jnp.float32) * s, 'bq': jnp.zeros((D_MODEL,), jnp.float32), 'Wk': jax.random.normal(ks[3], (D_MODEL, D_MODEL), jnp.float32) * s, 'bk': jnp.zeros((D_MODEL,), jnp.float32), 'Wv': jax.random.normal(ks[4], (D_MODEL, D_MODEL), jnp.float32) * s, 'bv': jnp.zeros((D_MODEL,), jnp.float32), 'attn_scale': jax.random.normal(ks[5], (D_MODEL,), jnp.float32) * 0.05, 'Wo': jax.random.normal(ks[6], (D_MODEL, D_MODEL), jnp.float32) * s, 'bo': jnp.zeros((D_MODEL,), jnp.float32), 'g1': jnp.ones((D_MODEL,), jnp.float32), 'beta1': jnp.zeros((D_MODEL,), jnp.float32), 'W1': jax.random.normal(ks[7], (D_MODEL, D_FF), jnp.float32) * s, 'bf1': jnp.zeros((D_FF,), jnp.float32), 'W2': jax.random.normal(ks[8], (D_FF, D_MODEL), jnp.float32) * s, 'bf2': jnp.zeros((D_MODEL,), jnp.float32), 'g2': jnp.ones((D_MODEL,), jnp.float32), 'beta2': jnp.zeros((D_MODEL,), jnp.float32)}
    _L0_tok_all = _L0_tok_setup()
    _L0_tok_in = {k: v for k, v in _L0_tok_all.items() if k in ('emb', 'Wq', 'bq', 'Wk', 'bk', 'Wv', 'bv', 'attn_scale', 'Wo', 'bo', 'g1', 'beta1', 'W1', 'bf1', 'W2', 'bf2', 'g2', 'beta2')}
    del _L0_tok_all

    def _L0_attn_setup():
        import jax, jax.numpy as jnp
        import numpy as np
        B, N, D, H, E = (4, 512, 128, 8, 8192)
        HD = D // H

        def _edge_col_bias(edge_index, edge_attr, eb_w, eb_b, n):
            eb = edge_attr @ eb_w.T + eb_b
            src, tgt = (edge_index[0], edge_index[1])
            valid = (src >= 0) & (src < n) & (tgt >= 0) & (tgt < n)
            order = jnp.where(valid, jnp.arange(edge_index.shape[1]), -1)
            tgt_safe = jnp.where(valid, tgt, 0)
            last = jnp.full((n,), -1, dtype=order.dtype).at[tgt_safe].max(order)
            hit = last >= 0
            gathered = eb[jnp.maximum(last, 0)]
            col_bias = jnp.where(hit[:, None], gathered, 0.0)
            return col_bias
        key = jax.random.key(seed)
        ks = jax.random.split(key, 12)
        s = 0.02
        inp = {'x': jax.random.normal(ks[0], (B, N, D), dtype=jnp.float32), 'edge_index': jax.random.randint(ks[1], (2, E), 0, N, dtype=jnp.int64), 'edge_attr': jax.random.normal(ks[2], (E, 3), dtype=jnp.float32), 'q_w': jax.random.normal(ks[3], (D, D), dtype=jnp.float32) * s, 'q_b': jnp.zeros((D,), jnp.float32), 'k_w': jax.random.normal(ks[4], (D, D), dtype=jnp.float32) * s, 'k_b': jnp.zeros((D,), jnp.float32), 'v_w': jax.random.normal(ks[5], (D, D), dtype=jnp.float32) * s, 'v_b': jnp.zeros((D,), jnp.float32), 'o_w': jax.random.normal(ks[6], (D, D), dtype=jnp.float32) * s, 'o_b': jnp.zeros((D,), jnp.float32), 'eb_w': jax.random.normal(ks[7], (H, 3), dtype=jnp.float32) * s, 'eb_b': jnp.zeros((H,), jnp.float32)}
        return inp
    _L0_attn_all = _L0_attn_setup()
    _L0_attn_in = {k: v for k, v in _L0_attn_all.items() if k in ('edge_index', 'edge_attr', 'q_w', 'q_b', 'k_w', 'k_b', 'v_w', 'v_b', 'o_w', 'o_b', 'eb_w', 'eb_b')}
    del _L0_attn_all

    def _L0_ffn_setup():
        import jax, jax.numpy as jnp
        import numpy as np
        B, S, D = (8, 1024, 128)
        H = 512
        O = 128
        E = 8
        TOP_K = 1
        key = jax.random.key(seed)
        ks = jax.random.split(key, 8)
        sc = 0.02
        return {'x': jax.random.normal(ks[0], (B, S, D), dtype=jnp.float32), 'Wr': jax.random.normal(ks[1], (D, E), dtype=jnp.float32) * sc, 'br': jnp.zeros((E,), dtype=jnp.float32), 'W1': jax.random.normal(ks[2], (E, D, H), dtype=jnp.float32) * sc, 'b1': jnp.zeros((E, H), dtype=jnp.float32), 'W2': jax.random.normal(ks[3], (E, H, O), dtype=jnp.float32) * sc, 'b2': jnp.zeros((E, O), dtype=jnp.float32)}
    _L0_ffn_all = _L0_ffn_setup()
    _L0_ffn_in = {k: v for k, v in _L0_ffn_all.items() if k in ('Wr', 'br', 'W1', 'b1', 'W2', 'b2')}
    del _L0_ffn_all
    return {'x': x, 'L0_tok_emb': _L0_tok_in['emb'], 'L0_tok_Wq': _L0_tok_in['Wq'], 'L0_tok_bq': _L0_tok_in['bq'], 'L0_tok_Wk': _L0_tok_in['Wk'], 'L0_tok_bk': _L0_tok_in['bk'], 'L0_tok_Wv': _L0_tok_in['Wv'], 'L0_tok_bv': _L0_tok_in['bv'], 'L0_tok_attn_scale': _L0_tok_in['attn_scale'], 'L0_tok_Wo': _L0_tok_in['Wo'], 'L0_tok_bo': _L0_tok_in['bo'], 'L0_tok_g1': _L0_tok_in['g1'], 'L0_tok_beta1': _L0_tok_in['beta1'], 'L0_tok_W1': _L0_tok_in['W1'], 'L0_tok_bf1': _L0_tok_in['bf1'], 'L0_tok_W2': _L0_tok_in['W2'], 'L0_tok_bf2': _L0_tok_in['bf2'], 'L0_tok_g2': _L0_tok_in['g2'], 'L0_tok_beta2': _L0_tok_in['beta2'], 'L0_attn_edge_index': _L0_attn_in['edge_index'], 'L0_attn_edge_attr': _L0_attn_in['edge_attr'], 'L0_attn_q_w': _L0_attn_in['q_w'], 'L0_attn_q_b': _L0_attn_in['q_b'], 'L0_attn_k_w': _L0_attn_in['k_w'], 'L0_attn_k_b': _L0_attn_in['k_b'], 'L0_attn_v_w': _L0_attn_in['v_w'], 'L0_attn_v_b': _L0_attn_in['v_b'], 'L0_attn_o_w': _L0_attn_in['o_w'], 'L0_attn_o_b': _L0_attn_in['o_b'], 'L0_attn_eb_w': _L0_attn_in['eb_w'], 'L0_attn_eb_b': _L0_attn_in['eb_b'], 'L0_ffn_Wr': _L0_ffn_in['Wr'], 'L0_ffn_br': _L0_ffn_in['br'], 'L0_ffn_W1': _L0_ffn_in['W1'], 'L0_ffn_b1': _L0_ffn_in['b1'], 'L0_ffn_W2': _L0_ffn_in['W2'], 'L0_ffn_b2': _L0_ffn_in['b2']}

def reference(x, L0_tok_emb, L0_tok_Wq, L0_tok_bq, L0_tok_Wk, L0_tok_bk, L0_tok_Wv, L0_tok_bv, L0_tok_attn_scale, L0_tok_Wo, L0_tok_bo, L0_tok_g1, L0_tok_beta1, L0_tok_W1, L0_tok_bf1, L0_tok_W2, L0_tok_bf2, L0_tok_g2, L0_tok_beta2, L0_attn_edge_index, L0_attn_edge_attr, L0_attn_q_w, L0_attn_q_b, L0_attn_k_w, L0_attn_k_b, L0_attn_v_w, L0_attn_v_b, L0_attn_o_w, L0_attn_o_b, L0_attn_eb_w, L0_attn_eb_b, L0_ffn_Wr, L0_ffn_br, L0_ffn_W1, L0_ffn_b1, L0_ffn_W2, L0_ffn_b2):
    import jax
    import jax.numpy as jnp

    def _L0_tok_ref(tokens, emb, Wq, bq, Wk, bk, Wv, bv, attn_scale, Wo, bo, g1, beta1, W1, bf1, W2, bf2, g2, beta2):
        import jax, jax.numpy as jnp
        import numpy as np
        D_MODEL = 128
        D_FF = 512
        VOCAB = 8000
        B, N = (2, 96)
        EPS = 1e-06

        def positional_encoding(n, d):
            pos = np.arange(n)[:, None].astype(np.float64)
            i = np.arange(d)[None, :]
            ang = pos / np.power(10000.0, 2 * (i // 2) / np.float32(d))
            ang[:, 0::2] = np.sin(ang[:, 0::2])
            ang[:, 1::2] = np.cos(ang[:, 1::2])
            return jnp.asarray(ang, dtype=jnp.float32)

        def layer_norm(x, gamma, beta):
            mu = jnp.mean(x, axis=-1, keepdims=True)
            var = jnp.mean(jnp.square(x - mu), axis=-1, keepdims=True)
            return (x - mu) / jnp.sqrt(var + EPS) * gamma + beta
        x = emb[tokens] * jnp.sqrt(jnp.float32(D_MODEL))
        x = x + positional_encoding(N, D_MODEL)[None, :, :]
        q = x @ Wq + bq
        k = x @ Wk + bk
        v = x @ Wv + bv
        scores = jnp.einsum('d,bijd->bij', attn_scale, jnp.tanh(q[:, :, None, :] + k[:, None, :, :]))
        weights = jax.nn.softmax(scores, axis=-1)
        attn = jnp.einsum('bij,bjd->bid', weights, v)
        attn = attn @ Wo + bo
        x = layer_norm(x + attn, g1, beta1)
        h = jax.nn.relu(x @ W1 + bf1)
        y = h @ W2 + bf2
        return layer_norm(x + y, g2, beta2)

    def _L0_attn_ref(x, edge_index, edge_attr, q_w, q_b, k_w, k_b, v_w, v_b, o_w, o_b, eb_w, eb_b):
        import jax, jax.numpy as jnp
        import numpy as np
        B, N, D, H, E = (4, 512, 128, 8, 8192)
        HD = D // H

        def _edge_col_bias(edge_index, edge_attr, eb_w, eb_b, n):
            eb = edge_attr @ eb_w.T + eb_b
            src, tgt = (edge_index[0], edge_index[1])
            valid = (src >= 0) & (src < n) & (tgt >= 0) & (tgt < n)
            order = jnp.where(valid, jnp.arange(edge_index.shape[1]), -1)
            tgt_safe = jnp.where(valid, tgt, 0)
            last = jnp.full((n,), -1, dtype=order.dtype).at[tgt_safe].max(order)
            hit = last >= 0
            gathered = eb[jnp.maximum(last, 0)]
            col_bias = jnp.where(hit[:, None], gathered, 0.0)
            return col_bias
        b, n, d = x.shape
        q = (x @ q_w.T + q_b).reshape(b, n, H, HD)
        k = (x @ k_w.T + k_b).reshape(b, n, H, HD)
        v = (x @ v_w.T + v_b).reshape(b, n, H, HD)
        scores = jnp.einsum('bnhd,bmhd->bhnm', q, k) / jnp.sqrt(jnp.float32(HD))
        col_bias = _edge_col_bias(edge_index, edge_attr, eb_w, eb_b, n)
        scores = scores + col_bias.T[None, :, None, :]
        attn = jax.nn.softmax(scores, axis=-1)
        out = jnp.einsum('bhnm,bmhd->bnhd', attn, v).reshape(b, n, d)
        return out @ o_w.T + o_b

    def _L0_ffn_ref(x, Wr, br, W1, b1, W2, b2):
        import jax, jax.numpy as jnp
        import numpy as np
        B, S, D = (8, 1024, 128)
        H = 512
        O = 128
        E = 8
        TOP_K = 1
        b, s, d = x.shape
        xf = x.reshape(-1, d)
        router_logits = xf @ Wr + br
        topk_logits, topk_idx = jax.lax.top_k(router_logits, TOP_K)
        topk_gates = jax.nn.softmax(topk_logits, axis=1)
        out = jnp.zeros((xf.shape[0], O), dtype=x.dtype)
        for k in range(TOP_K):
            idx_k = topk_idx[:, k]
            gate_k = topk_gates[:, k:k + 1]
            for e in range(E):
                h = jax.nn.relu(xf @ W1[e] + b1[e])
                oe = h @ W2[e] + b2[e]
                mask = (idx_k == e)[:, None]
                out = out + jnp.where(mask, gate_k * oe, 0.0)
        return out.reshape(b, s, O)
    h = _L0_tok_ref(x, L0_tok_emb, L0_tok_Wq, L0_tok_bq, L0_tok_Wk, L0_tok_bk, L0_tok_Wv, L0_tok_bv, L0_tok_attn_scale, L0_tok_Wo, L0_tok_bo, L0_tok_g1, L0_tok_beta1, L0_tok_W1, L0_tok_bf1, L0_tok_W2, L0_tok_bf2, L0_tok_g2, L0_tok_beta2)
    h = h + _L0_attn_ref(_layernorm(h, axis=-1), L0_attn_edge_index, L0_attn_edge_attr, L0_attn_q_w, L0_attn_q_b, L0_attn_k_w, L0_attn_k_b, L0_attn_v_w, L0_attn_v_b, L0_attn_o_w, L0_attn_o_b, L0_attn_eb_w, L0_attn_eb_b)
    h = h + _L0_ffn_ref(_layernorm(h, axis=-1), L0_ffn_Wr, L0_ffn_br, L0_ffn_W1, L0_ffn_b1, L0_ffn_W2, L0_ffn_b2)
    return h

_drawn_inputs = setup_inputs


def setup_inputs(seed=0):
    import zlib

    import numpy as np

    out = dict(_drawn_inputs(seed))
    spreads = {'L0_tok_bq': (0.0, 2.0),
     'L0_tok_bk': (0.0, 2.0),
     'L0_tok_bv': (0.0, 0.1),
     'L0_tok_bo': (0.0, 0.1),
     'L0_tok_g1': (1.0, 0.2),
     'L0_tok_beta1': (0.0, 0.1),
     'L0_tok_bf1': (0.0, 0.1),
     'L0_tok_bf2': (0.0, 0.1),
     'L0_tok_g2': (1.0, 0.2),
     'L0_tok_beta2': (0.0, 0.1),
     'L0_attn_q_b': (0.0, 2.0),
     'L0_attn_k_b': (0.0, 2.0),
     'L0_attn_v_b': (0.0, 0.331),
     'L0_attn_o_b': (0.0, 0.1),
     'L0_attn_eb_b': (0.0, 2.0),
     'L0_ffn_br': (0.0, 0.1),
     'L0_ffn_b1': (0.0, 0.273),
     'L0_ffn_b2': (0.0, 0.1)}
    factors = {'L0_tok_Wq': 95.669,
     'L0_tok_Wk': 25.893,
     'L0_tok_attn_scale': 25.083,
     'L0_attn_edge_attr': 8.0,
     'L0_attn_q_w': 8.0,
     'L0_attn_k_w': 8.0,
     'L0_attn_eb_w': 27.692}
    for name, (base, spread) in spreads.items():
        noise = np.random.default_rng([zlib.crc32(name.encode()), seed]).standard_normal(out[name].shape)
        drawn = base * np.exp(spread * noise) if base else spread * noise
        out[name] = jnp.asarray(drawn.astype(out[name].dtype))
    for name, factor in factors.items():
        out[name] = (out[name] * factor).astype(out[name].dtype)
    return out
```

```python
from contextlib import ExitStack

import concourse.bass as bass
from concourse import mybir

F32 = mybir.dt.float32
BF16 = mybir.dt.bfloat16
I32 = mybir.dt.int32
U32 = mybir.dt.uint32
ALU = mybir.AluOpType
ACT = mybir.ActivationFunctionType
AX_X = mybir.AxisListType.X

B, N, D = 64, 96, 128
VOCAB = 8000
FF = 512
NC = FF // D
H, HD = 8, 16
E = 8
NE = 8192
GB = 4
G = B // GB
GT = GB * N
R = N // 4
RING = 8
UT = 4 * GT
POOL_UNITS = (1, 5, 9, 13, 17, 21)
DVE_UNITS = tuple(r for r in range(R) if r not in POOL_UNITS)
NP, NV = len(POOL_UNITS), len(DVE_UNITS)
EPS_TOK, EPS_LN = 1e-6, 1e-5
BLK = 128
NBLK = B * N // BLK + E
REG = B * N + BLK
ROW = 2 * D + 2
FAR = 1 << 20
EC = NE // 8

LAY_A, LAY_B = {}, {}
for _lay, _items in ((LAY_A, (("ident", D), ("pos", D), ("wq", D), ("wk", D), ("wv", D), ("bq", 1), ("bk", 1),
                              ("scale", 1), ("iotap", 1))),
                     (LAY_B, (("wo", D), ("w1", FF), ("w2", FF), ("qw", D), ("kw", D), ("vw", D), ("ow", D), ("wr", E),
                              ("bv", 1), ("g1", 1), ("beta1", 1), ("bf1", NC), ("bf2", 1), ("qb", 1), ("kb", 1),
                              ("vb", 1), ("b1", E * NC), ("hmask", H), ("mask24", H), ("base", E), ("wtab", E),
                              ("upper", N), ("id0", GB), ("jtab", NBLK), ("k128", B * N // BLK)))):
    _at = 0
    for _name, _n in _items:
        _lay[_name] = (_at, _n)
        _at += _n
    _lay["_"] = (_at, 0)
ROWS = {"bo": (0, D), "g2": (D, D), "beta2": (2 * D, D), "ob": (3 * D, D), "br": (4 * D, E), "ebb": (4 * D + E, H),
        "b2": (4 * D + E + H, E * D)}
ROWS_N = 4 * D + E + H + E * D


def tower(nc, tok, emb, pack_a, pack_b, rows, edges, attr, ebw, w1m, w2m, out):
    out_rows = out.rearrange("b n d -> (b n) d")
    sorted_rows = nc.dram_tensor("sorted_rows", (E * REG + E * BLK, ROW), F32, kind="Internal").ap()
    edge_keys = nc.dram_tensor("edge_keys", (128, NE // 128), F32, kind="Internal").ap()

    with ExitStack() as ctx:
        def sb(name, shape, dt=F32):
            return ctx.enter_context(nc.sbuf_tensor(name, shape, dt))

        def sem(name):
            return ctx.enter_context(nc.semaphore(name))

        ca = sb("pack_a_sb", [128, LAY_A["_"][0]])
        cb = sb("pack_b_sb", [128, LAY_B["_"][0]])
        rw = sb("rows_sb", [128, ROWS_N])

        def A(name, p=128):
            at, n = LAY_A[name]
            return ca[0:p, at:at + n]

        def Bc(name, p=128):
            at, n = LAY_B[name]
            return cb[0:p, at:at + n]

        def Rw(name, p=N):
            at, n = ROWS[name]
            return rw[0:p, at:at + n]

        ring = sb("ring", [128, RING, UT])
        tok_i = sb("tok_i", [N, B], I32)
        tok_f = sb("tok_f", [N, B])
        tok_n = sb("tok_n", [N, B])
        tok_u = sb("tok_u", [N, B], U32)
        tok_g = sb("tok_g", [N, GB], U32)
        bqk = sb("bqk", [128, 1])
        qb4 = sb("qb4", [128, 1])
        scale_win = sb("scale_win", [128, 63])
        emb_in = sb("emb_in", [N, GB, D])
        x0 = [sb(f"x0_{p}", [N, GB, D]) for p in range(2)]
        xT = sb("xT", [128, GT])
        qS = [sb(f"qS_{p}", [128, GT]) for p in range(2)]
        kS = [sb(f"kS_{p}", [128, GT]) for p in range(2)]
        vS = [sb(f"vS_{p}", [N, GB, D]) for p in range(2)]
        nmax = sb("nmax", [128, GB])
        sum1 = sb("sum1", [128, GB])
        rs1 = sb("rs1", [128, GB])
        p1 = sb("p1", [128, GB, N])
        p1n = sb("p1n", [128, GB, N])
        pT = sb("pT", [N, GB, N])
        aT = sb("aT", [128, GT])
        r1 = sb("r1", [N, GB, D])
        st = [sb(f"st{k}", [N, GB, 6]) for k in range(4)]
        mv = [sb(f"mv{k}", [N, GB, 2]) for k in range(4)]
        ve = [sb(f"ve{k}", [N, GB]) for k in range(4)]
        rstd = [sb(f"rstd{k}", [N, GB]) for k in range(4)]
        mhalf = sb("mhalf", [N, GB])
        n1 = sb("n1", [N, GB, D])
        x1T = sb("x1T", [128, GT])
        hT = sb("hT", [128, NC, GT])
        r2T = sb("r2T", [128, GT])
        n2 = sb("n2", [N, GB, D])
        n2g = sb("n2g", [N, GB, D])
        h = sb("h", [N, GB, D])
        hb = [sb(f"hb_{p}", [N, GB, D]) for p in range(2)]
        hn = sb("hn", [N, GB, D])
        hnT = sb("hnT", [128, GT])
        q2T = sb("q2T", [128, GT])
        k2T = sb("k2T", [128, GT])
        v2 = sb("v2", [N, GB, H, HD + 1])
        kx = sb("kx", [128, GB, H, N])
        nm2 = [sb(f"nm2_{i}", [N, H]) for i in range(2)]
        p2 = [sb(f"p2_{i}", [N, H, N]) for i in range(2)]
        p2T = sb("p2T", [N, H, N])
        rd2 = [sb(f"rd2_{i}", [N, H]) for i in range(2)]
        a2 = sb("a2", [N, GB, H, HD])
        a2T = sb("a2T", [128, GT])
        row = [sb(f"row_{p}", [N, GB, ROW]) for p in range(2)]
        xfT = sb("xfT", [128, GT])
        lg = sb("lg", [N, GB, E])
        lmax = sb("lmax", [N, GB])
        lzero = sb("lzero", [N, GB])
        gexp = sb("gexp", [N, GB])
        ginv = sb("ginv", [N, GB])
        eqm = sb("eqm", [N, GB, E])
        eqw = sb("eqw", [N, GB, E])
        wsel = sb("wsel", [N, GB])
        cum = sb("cum", [N, GB + 1, E], BF16)
        oneh = sb("oneh", [N, GB, E], BF16)
        upper16 = sb("upper16", [N, N], BF16)
        ones16 = sb("ones16", [N, 128], BF16)
        posv = sb("posv", [N, GB, E])
        posm = sb("posm", [N, GB, E])
        posf = sb("posf", [N, GB])
        posu = [sb(f"posu_{p}", [N, GB], U32) for p in range(2)]
        cnt = [sb(f"cnt_{p}", [128, E]) for p in range(2)]
        idf = [sb(f"idf_{p}", [N, GB]) for p in range(2)]
        key_e = sb("key_e", [128, 2, NE // 128], I32)
        key_f = sb("key_f", [128, 2, NE // 128])
        key_v = sb("key_v", [128, 2, NE // 128])
        key_w = sb("key_w", [128, 2, NE // 128])
        key_t = sb("key_t", [128, NE // 128])
        key_1 = sb("key_1", [128, NE // 128])
        cmax = sb("cmax", [N, 8])
        cpos = sb("cpos", [N, 8])
        coff = sb("coff", [N, 8])
        last1 = sb("last1", [N, 1])
        hit = sb("hit", [N, 1])
        last_f = sb("last_f", [N, 1])
        last_u = sb("last_u", [N, 1], U32)
        at_rows = sb("at_rows", [N, 3])
        atT = sb("atT", [3, N])
        ebw_sb = sb("ebw_sb", [3, H])
        cbias = sb("cbias", [N, H])
        cbh = sb("cbh", [N, H])
        cb16 = sb("cb16", [N, 3, H], BF16)
        cb32 = sb("cb32", [N, 3, H])
        crem = [sb(f"crem{i}", [N, H]) for i in range(2)]
        cbT = sb("cbT", [3 * H, N])
        cbx = sb("cbx", [3 * H, H, N], BF16)
        ones24 = sb("ones24", [3 * H, N], BF16)
        order = hT[0:N, :, :].rearrange("p c t -> p (c t)")[:, 0:EC]
        kx_flat = kx[0:N, :, :, :].rearrange("p b h n -> p (b h n)")
        ech = [kx_flat[:, i * EC:(i + 1) * EC] for i in range(2)]
        eprod = kx_flat[:, 2 * EC:3 * EC]
        w1s = ring[:, 0:RING // 2, :].rearrange("p a n -> p (a n)")[:, 0:E * FF]
        w2s = ring[:, RING // 2:RING, :].rearrange("p a n -> p (a n)")[:, 0:E * FF]
        padrow = sb("padrow", [BLK, ROW])
        padf = sb("padf", [BLK, E])
        padu = sb("padu", [BLK, E], U32)
        blk_n = sb("blk_n", [1, E])
        blk_g = sb("blk_g", [1, E, B * N // BLK])
        blk_c = sb("blk_c", [1, E])
        blk_end = sb("blk_end", [1, E])
        blk_ge = sb("blk_ge", [1, NBLK, E])
        blk_gn = sb("blk_gn", [1, NBLK, E])
        blk_e = sb("blk_e", [1, NBLK])
        blk_s = sb("blk_s", [1, NBLK])
        blk_t = sb("blk_t", [1, NBLK])
        blk_t2 = sb("blk_t2", [1, NBLK])
        blk_em = sb("blk_em", [1, NBLK])
        tab_e = sb("tab_e", [1, NBLK], I32)
        tab_r = sb("tab_r", [1, NBLK], I32)
        rin = [sb(f"rin{i}", [BLK, ROW]) for i in range(4)]
        yout = [sb(f"yout{i}", [BLK, D]) for i in range(4)]
        xbT = [sb(f"xbT{i}", [128, BLK]) for i in range(2)]
        hraw = [sb(f"hraw{i}", [BLK, FF]) for i in range(2)]
        hbT = [sb(f"hbT{i}", [128, NC, BLK]) for i in range(2)]
        ytmp = [sb(f"ytmp{i}", [BLK, D]) for i in range(2)]

        bank = [ctx.enter_context(nc.psum_tensor(f"bank{i}", [128, 512], F32)) for i in range(4)]
        s2b = ctx.enter_context(nc.psum_tensor("s2_banks", [128, 2, 512], F32))
        rbb = ctx.enter_context(nc.psum_tensor("rb_banks", [128, 2, 512], F32))
        QP, SC, RA0, RA1 = bank
        RB0, RB1 = rbb[:, 0, :], rbb[:, 1, :]

        def feat(b):
            return b[:, 0:GT]

        def tokv(b):
            return b[0:N, :].rearrange("p (b d) -> p b d", b=GB)

        def cols(t, b):
            return t[:, b * N:(b + 1) * N]

        names = """ld_a ld_b ld_rows ld_tok ld_edge ld_ebw ld_keys ld_attr key_out ld_moe
            consts tok_ok tok_g_ok x0_ok xT_ps xT_ok q_ps q_ok k_ps k_ok v_ps v_ok x0b_ok
            qp_ok sum_dve sum_pool tanh_ok unit_used
            nmax_ok exp1_ok rs1_ok p1n_ok p1T_ps pT_ok aT_ps aT_ok wo_ps r1_ok n1_ok n1T_ps x1T_ok
            f1_ps hT_ok f2_ps r2T_ok r2_ps n2_ok n2g_ok h_ok hb_ok hn_ok hnT_ps hnT_ok
            q2_ps q2_ok k2_ps k2_ok v2_ps v2_ok kx_ok s2_ps nm2_ok p2_ok e2_ok p2T_ps p2T_ok pv_ps
            rd2_ok a2_ok a2T_ps a2T_ok o_ps h2_ok xf_ok xfT_ps xfT_ok lg_ps lg_ok lmax_ok lzero_ok gexp_ok ginv_ok
            gate_ok eqm_ok eqw_ok wsel_ok oneh_ok cum1 cum2 cum3 cum4 rank_ps posv_ok posm_ok posf_ok pos_ok cnt_ok
            idf_ok id_ok
            passed dve_seq bias_ok scale_ok upper_ok init_ok key_ok edge_p last_ok edge_at_ps atT_ok edge_cb_ps cb32_ok
            edge_cbT_ps cb_ok iota_ok pad_ok pad_out tab_ok
            tr_ps xb_ok l1_ps hraw_ok htr_ps hb_relu y_ps ytmp_ok yo_ok"""
        S = {n: sem(n) for n in names.split()}
        st_ok = [sem(f"st{k}_ok") for k in range(4)]
        mv_ok = [sem(f"mv{k}_ok") for k in range(4)]
        ve_ok = [sem(f"ve{k}_ok") for k in range(4)]
        rstd_ok = [sem(f"rstd{k}_ok") for k in range(4)]
        gathered = [sem(f"gathered_{p}") for p in range(2)]
        scattered = [sem(f"scattered_{p}") for p in range(2)]
        blk_in = [sem(f"blk_in{i}") for i in range(4)]
        blk_out = [sem(f"blk_out{i}") for i in range(4)]

        block = ctx.enter_context(nc.Block())

        def wait_apart(eng, s, value):
            eng.wait_ge(s, value)
            eng.sem_inc(S["passed"], 1)

        def windows(eng, window):
            window(0, 0, 0, True, True, False, False)
            window(1, 1, 0, True, True, True, False)
            window(2, 0, 1, True, True, True, True)
            window(3, 1, 1, True, True, True, True)
            with eng.Fori(2, G // 2 - 1) as t:
                window(2 * t, 0, t, True, True, True, True)
                window(2 * t + 1, 1, t, True, True, True, True)
            window(G - 2, 0, G // 2 - 1, True, True, True, True)
            window(G - 1, 1, G // 2 - 1, False, True, True, True)
            window(G, 0, G // 2, False, False, True, True)
            window(G + 1, 1, G // 2, False, False, False, True)

        @block.sync
        def _(sp):
            sp.dma_start(tok_i[:, :], tok).then_inc(S["ld_tok"], 16)
            sp.dma_start(ca[:, :], pack_a).then_inc(S["ld_a"], 16)
            sp.dma_start(key_e[:, :, :], edges.rearrange("s (p f) -> p s f", p=128)).then_inc(S["ld_edge"], 16)
            sp.dma_start(cb[:, :], pack_b).then_inc(S["ld_b"], 16)
            sp.dma_start(rw[:, :], rows.to_broadcast([128, ROWS_N])).then_inc(S["ld_rows"], 16)
            sp.dma_start(ebw_sb[:, :], ebw).then_inc(S["ld_ebw"], 16)
            sp.wait_ge(S["key_ok"], 1)
            sp.dma_start(edge_keys, key_t[:, :]).then_inc(S["key_out"], 16)
            sp.wait_ge(S["key_out"], 16)
            flat = edge_keys.rearrange("p f -> (p f)").rearrange("(a n) -> a n", a=8)
            for c in range(8):
                if c >= 2:
                    sp.wait_ge(S["edge_p"], c - 1)
                sp.dma_start(ech[c % 2], flat[c:c + 1, :].to_broadcast([N, EC])).then_inc(S["ld_keys"], 16)
                sp.wait_ge(S["ld_keys"], 16 * (c + 1))
            sp.wait_ge(S["unit_used"], R * G)
            sp.dma_start(w1s.rearrange("p (e f) -> p e f", e=E), w1m.rearrange("e p f -> p e f")).then_inc(S["ld_moe"], 16)
            for e in range(E):
                sp.dma_start(w2s[:, e * FF:(e + 1) * FF].rearrange("p (c o) -> p c o", c=NC),
                             w2m[e].rearrange("(c p) o -> p c o", p=128)).then_inc(S["ld_moe"], 16)
            sp.wait_ge(S["tab_ok"], 2)
            sp.wait_ge(S["pad_out"], 16 * (E + 1))
            sp.wait_ge(scattered[0], 16 * GB * (G // 2))
            sp.wait_ge(scattered[1], 16 * GB * (G // 2))

            def load(j, i, first, t):
                if not first:
                    sp.wait_ge(blk_out[i], 16 * t)
                r = sp.value_load(tab_r[0:1, bass.ds(j, 1)], min_val=0, max_val=E * REG + (E - 1) * BLK)
                sp.dma_start(rin[i][:, :], sorted_rows[bass.ds(r, BLK), :]).then_inc(blk_in[i], 16)

            for i in range(4):
                load(i, i, True, 0)
            with sp.Fori(1, NBLK // 4) as t:
                for i in range(4):
                    load(4 * t + i, i, False, t)
            for i in range(4):
                sp.wait_ge(blk_out[i], 16 * (NBLK // 4))

        @block.gpsimd
        def _(pool):
            pool.memset(mhalf[:, :], -0.5).then_inc(S["consts"], 1)
            pool.memset(v2[:, :, :, HD:HD + 1], 1.0).then_inc(S["consts"], 1)
            pool.memset(ones24[:, :], 1.0).then_inc(S["consts"], 1)
            pool.memset(ones16[:, :], 1.0).then_inc(S["consts"], 1)
            pool.memset(cum[:, 0, :], 0.0).then_inc(S["consts"], 1)
            pool.memset(padrow[:, :], 0.0).then_inc(S["consts"], 1)
            pool.wait_ge(S["consts"], 6)
            pool.memset(padrow[:, 2 * D + 1:ROW].bitcast(I32), FAR).then_inc(S["consts"], 1)
            pool.iota(order, [[1, EC]], base=1, channel_multiplier=0,
                      allow_small_or_imprecise_dtypes=True).then_inc(S["iota_ok"], 1)
            pool.iota(coff[:, :], [[EC, 8]], base=0, channel_multiplier=0,
                      allow_small_or_imprecise_dtypes=True).then_inc(S["iota_ok"], 1)
            pool.wait_ge(S["tok_ok"], 1)
            pool.wait_ge(S["ld_a"], 16)
            pool.wait_ge(S["ld_b"], 16)
            pool.wait_ge(S["ld_rows"], 16)

            def gather(g, p, pair, first):
                if not first:
                    wait_apart(pool, S["x0_ok"], g)
                pool.tensor_copy(tok_g[:, :], tok_u[:, bass.ds(GB * g, GB)]).then_inc(S["tok_g_ok"], 1)
                wait_apart(pool, S["tok_g_ok"], g + 1)
                for b in range(GB):
                    pool.indirect_dma_start(
                        out=emb_in[:, b, :], out_offset=None, in_=emb,
                        in_offset=bass.IndirectOffsetOnAxis(ap=tok_g[:, b:b + 1], axis=0)).then_inc(gathered[p], 16)

            def add_bo(g, p):
                pool.wait_ge(S["xT_ok"], g + 1)
                pool.tensor_tensor(x0[p][:, :, :], x0[p][:, :, :],
                                   Rw("bo").unsqueeze(1).to_broadcast([N, GB, D]), ALU.add).then_inc(S["x0b_ok"], 1)

            def rsqrt(k, g1, eps):
                wait_apart(pool, mv_ok[k], g1)
                pool.tensor_scalar(ve[k][:, :], mv[k][:, :, 1], eps, None, ALU.add).then_inc(ve_ok[k], 1)
                pool.wait_ge(ve_ok[k], g1)
                pool.tensor_tensor(rstd[k][:, :], ve[k][:, :], mhalf[:, :], ALU.pow).then_inc(rstd_ok[k], 1)

            def normalise(k, g1, dst, src, done):
                wait_apart(pool, rstd_ok[k], g1)
                for b in range(GB):
                    ins = pool.tensor_scalar(dst[:, b, 0:D], src[:, b, 0:D], mv[k][:, b, 0:1], rstd[k][:, b:b + 1],
                                             ALU.subtract, ALU.mult)
                ins.then_inc(done, 1)

            gather(0, 0, 0, True)
            add_bo(0, 0)

            def window(w, p, pair, front, units, a, b):
                q = 1 - p
                for r in range(R):
                    if units and r in POOL_UNITS:
                        if r == POOL_UNITS[0]:
                            pool.wait_ge(S["q_ok"], w + 1)
                            pool.wait_ge(S["k_ok"], w + 1)
                        if not (isinstance(w, int) and w == 0 and r < RING):
                            pool.wait_ge(S["unit_used"], R * w + r - RING + 1)
                        pool.tensor_tensor(
                            ring[:, r % RING, :].rearrange("p (c b j) -> p c b j", c=4, b=GB),
                            kS[p][:, :].rearrange("p (b j) -> p b j", b=GB).unsqueeze(1).to_broadcast([128, 4, GB, N]),
                            qS[p][:, :].rearrange("p (b c r) -> p c b r", b=GB, c=4)[:, :, :, r].unsqueeze(3)
                            .to_broadcast([128, 4, GB, N]), ALU.add).then_inc(S["sum_pool"], 1)
                    if front and r == 0:
                        gather(w + 1, q, pair, False)
                    if isinstance(w, int) and w == 0 and r == 15:
                        pool.wait_ge(S["last_ok"], 1)
                        pool.indirect_dma_start(
                            out=at_rows[:, :], out_offset=None, in_=attr,
                            in_offset=bass.IndirectOffsetOnAxis(ap=last_u[:, :], axis=0)).then_inc(S["ld_attr"], 16)
                    if b and r == 1:
                        wait_apart(pool, S["k2_ok"], w - 1)
                        for hh in range(H):
                            ins = pool.tensor_scalar(
                                kx[:, :, hh, :], k2T[:, :].rearrange("p (b m) -> p b m", b=GB),
                                Bc("hmask")[:, hh:hh + 1], None, ALU.mult)
                        ins.then_inc(S["kx_ok"], 1)
                    if a and r == 3:
                        pool.wait_ge(S["rs1_ok"], w)
                        pool.tensor_tensor(p1n[:, :, :], p1[:, :, :],
                                           rs1[:, :].unsqueeze(2).to_broadcast([128, GB, N]), ALU.mult)\
                            .then_inc(S["p1n_ok"], 1)
                    if a and r == 8:
                        rsqrt(0, w, EPS_TOK)
                        normalise(0, w, n1, r1, S["n1_ok"])
                    if a and r == 14:
                        rsqrt(1, w, EPS_TOK)
                    if a and r == 16:
                        pool.wait_ge(S["n2_ok"], w)
                        pool.tensor_tensor(n2g[:, :, :], n2[:, :, :],
                                           Rw("g2").unsqueeze(1).to_broadcast([N, GB, D]), ALU.mult)\
                            .then_inc(S["n2g_ok"], 1)
                        pool.wait_ge(S["n2g_ok"], w)
                        pool.tensor_tensor(h[:, :, :], n2g[:, :, :],
                                           Rw("beta2").unsqueeze(1).to_broadcast([N, GB, D]), ALU.add)\
                            .then_inc(S["h_ok"], 1)
                        pool.wait_ge(S["h_ok"], w)
                        pool.tensor_tensor(hb[q][:, :, :], h[:, :, :],
                                           Rw("ob").unsqueeze(1).to_broadcast([N, GB, D]), ALU.add)\
                            .then_inc(S["hb_ok"], 1)
                    if a and r == 18:
                        rsqrt(2, w, EPS_LN)
                        normalise(2, w, hn, h, S["hn_ok"])
                    if front and r == 19:
                        add_bo(w + 1, q)
                    if b and r == 20:
                        rsqrt(3, w - 1, EPS_LN)
                        wait_apart(pool, rstd_ok[3], w - 1)
                        for bb in range(GB):
                            ins = pool.tensor_scalar(row[p][:, bb, D:2 * D], row[p][:, bb, 0:D], mv[3][:, bb, 0:1],
                                                     rstd[3][:, bb:bb + 1], ALU.subtract, ALU.mult)
                        ins.then_inc(S["xf_ok"], 1)
                    if b and r == 23:
                        pool.wait_ge(S["pos_ok"], w - 1)
                        pool.wait_ge(S["gate_ok"], w - 1)
                        wait_apart(pool, S["id_ok"], w - 1)
                        for bb in range(GB):
                            pool.indirect_dma_start(
                                out=sorted_rows, out_offset=bass.IndirectOffsetOnAxis(ap=posu[p][:, bb:bb + 1], axis=0),
                                in_=row[p][:, bb, :], in_offset=None).then_inc(scattered[p], 16)

            windows(pool, window)

            pool.wait_ge(S["pad_ok"], 1)
            pool.dma_start(sorted_rows[E * REG:E * REG + E * BLK, :].rearrange("(k p) c -> p k c", p=BLK),
                           padrow[:, :].unsqueeze(1).to_broadcast([BLK, E, ROW])).then_inc(S["pad_out"], 16)
            for e in range(E):
                pool.indirect_dma_start(
                    out=sorted_rows, out_offset=bass.IndirectOffsetOnAxis(ap=padu[:, e:e + 1], axis=0),
                    in_=padrow[:, :], in_offset=None).then_inc(S["pad_out"], 16)

            def store(j, i):
                wait_apart(pool, S["yo_ok"], j + 1)
                pool.indirect_dma_start(
                    out=out_rows, out_offset=bass.IndirectOffsetOnAxis(
                        ap=rin[i][:, 2 * D + 1:ROW].bitcast(U32), axis=0),
                    in_=yout[i][:, :], in_offset=None, bounds_check=B * N - 1, oob_is_err=False)\
                    .then_inc(blk_out[i], 16)

            with pool.Fori(0, NBLK // 4) as t:
                for i in range(4):
                    store(4 * t + i, i)

        @block.scalar
        def _(act):
            act.wait_ge(S["ld_a"], 16)
            act.wait_ge(S["ld_b"], 16)
            act.wait_ge(S["bias_ok"], 2)

            def xT_out(g):
                act.wait_ge(S["xT_ps"], g + 1)
                act.activation(xT[:, :], feat(RA1), ACT.Copy).then_inc(S["xT_ok"], 1)

            def q_out(g, p):
                act.wait_ge(S["q_ps"], g + 1)
                act.activation(qS[p][:, :], feat(RA0), ACT.Copy).then_inc(S["q_ok"], 1)

            def k_out(g, p):
                act.wait_ge(S["k_ps"], g + 1)
                act.activation(kS[p][:, :], feat(RA1), ACT.Identity, bias=bqk[:, 0:1]).then_inc(S["k_ok"], 1)

            def v_out(g, p):
                act.wait_ge(S["v_ps"], g + 1)
                act.activation(vS[p][:, :, :], tokv(RA1), ACT.Copy).then_inc(S["v_ok"], 1)

            xT_out(0)
            q_out(0, 0)
            k_out(0, 0)
            v_out(0, 0)

            def window(w, p, pair, front, units, a, b):
                q = 1 - p

                def exp2(bb):
                    act.wait_ge(S["p2_ok"], GB * (w - 2) + bb + 1)
                    act.activation(p2[bb % 2][:, :, :], p2[bb % 2][:, :, :], ACT.Exp).then_inc(S["e2_ok"], 1)

                def p2T_out(bb):
                    act.wait_ge(S["p2T_ps"], GB * (w - 2) + bb + 1)
                    act.activation(p2T[:, :, :].rearrange("p (u v) m -> p u (v m)", u=2), rbb[0:N, :, 0:4 * N],
                                   ACT.Copy).then_inc(S["p2T_ok"], 1)

                for r in range(R):
                    if units:
                        if r in POOL_UNITS:
                            act.wait_ge(S["sum_pool"], NP * w + POOL_UNITS.index(r) + 1)
                        else:
                            act.wait_ge(S["sum_dve"], NV * w + DVE_UNITS.index(r) + 1)
                        act.activation(ring[:, r % RING, :], ring[:, r % RING, :], ACT.Tanh).then_inc(S["tanh_ok"], 1)
                    if b and r == 0:
                        act.wait_ge(S["q2_ps"], w - 1)
                        act.activation(q2T[:, :], feat(RB0), ACT.Identity, bias=qb4[:, 0:1], scale=0.25)\
                            .then_inc(S["q2_ok"], 1)
                    if b and r == 1:
                        act.wait_ge(S["k2_ps"], w - 1)
                        act.activation(k2T[:, :], feat(RB1), ACT.Identity, bias=Bc("kb")).then_inc(S["k2_ok"], 1)
                    if b and r == 2:
                        act.wait_ge(S["v2_ps"], w - 1)
                        act.activation(v2[:, :, :, 0:HD], tokv(RB0).rearrange("p b (h d) -> p b h d", h=H), ACT.Copy)\
                            .then_inc(S["v2_ok"], 1)
                    if a and r == 2:
                        act.wait_ge(S["nmax_ok"], w)
                        for bb in range(GB):
                            act.activation(p1[:, bb, :], cols(SC, bb), ACT.Exp, bias=nmax[:, bb:bb + 1],
                                           accum_out=sum1[:, bb:bb + 1]).then_inc(S["exp1_ok"], 1)
                    for bb in range(GB):
                        if b and r == 4 + 4 * bb:
                            exp2(bb)
                        if b and r == 5 + 4 * bb:
                            p2T_out(bb)
                    if a and r == 6:
                        act.wait_ge(S["aT_ps"], w)
                        act.activation(aT[:, :], feat(RA1), ACT.Identity, bias=Bc("bv")).then_inc(S["aT_ok"], 1)
                    if a and r in (10, 11):
                        for c in ((0, 1) if r == 10 else (2, 3)):
                            act.wait_ge(S["f1_ps"], NC * (w - 1) + c + 1)
                            act.activation(hT[:, c, :], feat((RA0, RA1)[c % 2]), ACT.Relu,
                                           bias=Bc("bf1")[:, c:c + 1]).then_inc(S["hT_ok"], 1)
                    if front and r == 16:
                        xT_out(w + 1)
                    if front and r == 17:
                        q_out(w + 1, q)
                        k_out(w + 1, q)
                    if b and r == 18:
                        act.wait_ge(S["a2T_ps"], w - 1)
                        act.activation(a2T[:, :], feat(RB1), ACT.Identity, bias=Bc("vb")).then_inc(S["a2T_ok"], 1)
                    if a and r == 19:
                        act.wait_ge(S["hnT_ps"], w)
                        act.activation(hnT[:, :], feat(RA0), ACT.Copy).then_inc(S["hnT_ok"], 1)
                    if front and r == 19:
                        v_out(w + 1, q)
                    if b and r == 20:
                        act.wait_ge(S["xfT_ps"], w - 1)
                        act.activation(xfT[:, :], feat(RB1), ACT.Copy).then_inc(S["xfT_ok"], 1)
                    if b and r == 21:
                        act.wait_ge(S["lzero_ok"], w - 1)
                        act.activation(gexp[:, :], lzero[:, :], ACT.Exp).then_inc(S["gexp_ok"], 1)

            windows(act, window)

            act.wait_ge(S["tab_ok"], 2)

            def relu_block(j, i):
                e = act.value_load(tab_e[0:1, bass.ds(j, 1)], min_val=0, max_val=E - 1)
                act.wait_ge(S["htr_ps"], j + 1)
                for c in range(NC):
                    ins = act.activation(hbT[i % 2][:, c, :], bank[i % 2][:, c * BLK:(c + 1) * BLK], ACT.Relu,
                                         bias=Bc("b1")[:, bass.ds(NC * e + c, 1)])
                ins.then_inc(S["hb_relu"], 1)

            with act.Fori(0, NBLK // 4) as t:
                for i in range(4):
                    relu_block(4 * t + i, i)

        @block.tensor
        def _(pe):
            pe.wait_ge(S["ld_a"], 16)
            pe.wait_ge(S["scale_ok"], 1)
            pe.wait_ge(S["upper_ok"], 1)
            pe.wait_ge(S["consts"], 7)
            ident = A("ident")

            def x_tr(g, p):
                pe.wait_ge(S["x0_ok"], g + 1)
                for b in range(GB):
                    ins = pe.transpose(cols(RA1, b), x0[p][:, b, :], ident[0:N, 0:N])
                ins.then_inc(S["xT_ps"], 1)

            def q_mm(g):
                pe.wait_ge(S["xT_ok"], g + 1)
                pe.matmul(feat(RA0), A("wq"), xT[:, :], start=True, stop=True).then_inc(S["q_ps"], 1)

            def k_mm(g):
                pe.matmul(feat(RA1), A("wk"), xT[:, :], start=True, stop=True).then_inc(S["k_ps"], 1)

            def v_mm(g):
                pe.wait_ge(S["k_ok"], g + 1)
                for b in range(GB):
                    ins = pe.matmul(tokv(RA1)[:, b, :], cols(xT, b), A("wv"), start=True, stop=True)
                ins.then_inc(S["v_ps"], 1)

            x_tr(0, 0)
            q_mm(0)
            k_mm(0)
            v_mm(0)
            pe.wait_ge(S["ld_ebw"], 16)
            pe.wait_ge(S["ld_b"], 16)

            def window(w, p, pair, front, units, a, b):
                q = 1 - p

                def scores2(bb):
                    if bb == 0:
                        pe.wait_ge(S["kx_ok"], w - 1)
                        pe.wait_ge(S["cb_ok"], 1)
                    if not (isinstance(w, int) and w == 2 and bb == 0):
                        pe.wait_ge(S["p2_ok"], GB * (w - 2) + bb)
                    for u in range(2):
                        pe.matmul(s2b[0:N, u, 0:4 * N], cols(q2T, bb),
                                  kx[:, bb, 4 * u:4 * u + 4, :].rearrange("p h m -> p (h m)"), start=True, stop=False)
                        ins = pe.matmul(s2b[0:N, u, 0:4 * N], ones24[:, :],
                                        cbx[:, 4 * u:4 * u + 4, :].rearrange("p h m -> p (h m)"), start=False, stop=True)
                    ins.then_inc(S["s2_ps"], 1)

                def p2_tr(bb):
                    pe.wait_ge(S["e2_ok"], GB * (w - 2) + bb + 1)
                    if bb == 0:
                        pe.wait_ge(S["v2_ok"], w - 1)
                    else:
                        pe.wait_ge(S["a2_ok"], GB * (w - 2) + bb)
                    for hh in range(H):
                        ins = pe.transpose(rbb[0:N, hh // 4, (hh % 4) * N:(hh % 4 + 1) * N], p2[bb % 2][:, hh, :],
                                           ident[0:N, 0:N])
                    ins.then_inc(S["p2T_ps"], 1)

                def pv(bb):
                    pe.wait_ge(S["p2T_ok"], GB * (w - 2) + bb + 1)
                    for hh in range(H):
                        ins = pe.matmul(RB0[0:N, hh * (HD + 1):(hh + 1) * (HD + 1)], p2T[:, hh, :], v2[:, bb, hh, :],
                                        start=True, stop=True)
                    ins.then_inc(S["pv_ps"], 1)

                for r in range(R):
                    if b and r == 0:
                        pe.wait_ge(S["hnT_ok"], w - 1)
                        if isinstance(w, int) and w == 2:
                            pe.wait_ge(S["cb_ok"], 1)
                        else:
                            pe.wait_ge(S["cnt_ok"], w - 2)
                            pe.wait_ge(S["lg_ok"], w - 2)
                        pe.matmul(feat(RB0), Bc("qw"), hnT[:, :], start=True, stop=True).then_inc(S["q2_ps"], 1)
                        pe.matmul(feat(RB1), Bc("kw"), hnT[:, :], start=True, stop=True).then_inc(S["k2_ps"], 1)
                    if b and r == 0:
                        pe.wait_ge(S["q2_ok"], w - 1)
                        for bb in range(GB):
                            ins = pe.matmul(tokv(RB0)[:, bb, :], cols(hnT, bb), Bc("vw"), start=True, stop=True)
                        ins.then_inc(S["v2_ps"], 1)
                    if units:
                        if r == 0 and not (isinstance(w, int) and w == 0):
                            pe.wait_ge(S["exp1_ok"], GB * w)
                        pe.wait_ge(S["tanh_ok"], R * w + r + 1)
                        for c in range(4):
                            ins = pe.matmul(SC[32 * c:32 * c + 32, 0:GT], scale_win[:, 31 - r:63 - r],
                                            ring[:, r % RING, c * GT:(c + 1) * GT], start=(r == 0), stop=(r == R - 1))
                        ins.then_inc(S["unit_used"], 1)
                    if isinstance(w, int) and w == 0:
                        if r == 18:
                            pe.wait_ge(S["ld_attr"], 16)
                            pe.transpose(RB0[0:3, 0:N], at_rows[:, :], ident[0:N, 0:N]).then_inc(S["edge_at_ps"], 1)
                        if r == 20:
                            pe.wait_ge(S["atT_ok"], 1)
                            pe.matmul(RB1[0:N, 0:H], atT[:, :], ebw_sb[:, :], start=True, stop=True)\
                                .then_inc(S["edge_cb_ps"], 1)
                        if r == 22:
                            pe.wait_ge(S["cb32_ok"], 1)
                            pe.transpose(RB0[0:3 * H, 0:N], cb32[:, :, :].rearrange("p s h -> p (s h)"),
                                         ident[0:N, 0:N]).then_inc(S["edge_cbT_ps"], 1)
                    for bb in range(GB):
                        if b and r == 3 + 4 * bb:
                            scores2(bb)
                        if b and r == 5 + 4 * bb:
                            p2_tr(bb)
                        if b and r == 6 + 4 * bb:
                            pv(bb)
                    if a and r == 4:
                        pe.wait_ge(S["p1n_ok"], w)
                        if isinstance(w, int) and w == 1:
                            pe.wait_ge(S["q_ok"], 2)
                        else:
                            pe.wait_ge(S["hnT_ok"], w - 1)
                        for bb in range(GB):
                            ins = pe.transpose(RA0[0:N, bb * 128:(bb + 1) * 128], p1n[:, bb, :], ident)
                        ins.then_inc(S["p1T_ps"], 1)
                    if a and r == 5:
                        pe.wait_ge(S["pT_ok"], w)
                        if isinstance(w, int) and w == G:
                            pe.wait_ge(S["v_ok"], w)
                            pe.wait_ge(S["n2_ok"], w - 1)
                        else:
                            pe.wait_ge(S["v_ok"], w + 1)
                        for bb in range(GB):
                            ins = pe.matmul(cols(RA1, bb), vS[q][:, bb, :], pT[:, bb, :], start=True, stop=True)
                        ins.then_inc(S["aT_ps"], 1)
                    if a and r == 6:
                        pe.wait_ge(S["aT_ok"], w)
                        for bb in range(GB):
                            ins = pe.matmul(tokv(RA0)[:, bb, :], cols(aT, bb), Bc("wo"), start=True, stop=True)
                        ins.then_inc(S["wo_ps"], 1)
                    if a and r == 8:
                        pe.wait_ge(S["n1_ok"], w)
                        for bb in range(GB):
                            ins = pe.transpose(cols(RA1, bb), n1[:, bb, :], ident[0:N, 0:N])
                        ins.then_inc(S["n1T_ps"], 1)
                    if a and r in (9, 10):
                        for c in ((0, 1) if r == 9 else (2, 3)):
                            if c == 0:
                                pe.wait_ge(S["x1T_ok"], w)
                            if c >= 2:
                                pe.wait_ge(S["hT_ok"], NC * (w - 1) + c - 1)
                            pe.matmul(feat((RA0, RA1)[c % 2]), Bc("w1")[:, c * D:(c + 1) * D], x1T[:, :],
                                      start=True, stop=True).then_inc(S["f1_ps"], 1)
                    if a and r == 11:
                        pe.wait_ge(S["hT_ok"], NC * w)
                        for c in range(NC):
                            ins = pe.matmul(feat(RA0), Bc("w2")[:, c * D:(c + 1) * D], hT[:, c, :],
                                            start=(c == 0), stop=(c == NC - 1))
                        ins.then_inc(S["f2_ps"], 1)
                    if a and r == 13:
                        pe.wait_ge(S["r2T_ok"], w)
                        for bb in range(GB):
                            ins = pe.transpose(tokv(RA1)[:, bb, :], cols(r2T, bb), ident)
                        ins.then_inc(S["r2_ps"], 1)
                    if front and r == 16:
                        if a:
                            pe.wait_ge(S["n2_ok"], w)
                        else:
                            pe.wait_ge(S["v_ok"], w + 1)
                        x_tr(w + 1, q)
                    if front and r == 17:
                        q_mm(w + 1)
                        k_mm(w + 1)
                    if b and r == 18:
                        pe.wait_ge(S["a2_ok"], GB * (w - 1))
                        for bb in range(GB):
                            ins = pe.transpose(cols(RB1, bb), a2[:, bb, :, :].rearrange("p h d -> p (h d)"),
                                               ident[0:N, 0:N])
                        ins.then_inc(S["a2T_ps"], 1)
                    if front and r == 18:
                        v_mm(w + 1)
                    if a and r == 19:
                        pe.wait_ge(S["hn_ok"], w)
                        if front:
                            pe.wait_ge(S["q_ok"], w + 2)
                        for bb in range(GB):
                            ins = pe.transpose(cols(RA0, bb), hn[:, bb, :], ident[0:N, 0:N])
                        ins.then_inc(S["hnT_ps"], 1)
                    if b and r == 19:
                        pe.wait_ge(S["a2T_ok"], w - 1)
                        for bb in range(GB):
                            ins = pe.matmul(tokv(RB0)[:, bb, :], cols(a2T, bb), Bc("ow"), start=True, stop=True)
                        ins.then_inc(S["o_ps"], 1)
                    if b and r == 20:
                        pe.wait_ge(S["xf_ok"], w - 1)
                        for bb in range(GB):
                            ins = pe.transpose(cols(RB1, bb), row[p][:, bb, D:2 * D], ident[0:N, 0:N])
                        ins.then_inc(S["xfT_ps"], 1)
                    if b and r == 21:
                        pe.wait_ge(S["xfT_ok"], w - 1)
                        for bb in range(GB):
                            ins = pe.matmul(RB0[0:N, bb * E:(bb + 1) * E], cols(xfT, bb), Bc("wr"), start=True, stop=True)
                        ins.then_inc(S["lg_ps"], 1)
                    if b and r == 22:
                        pe.wait_ge(S["cum4"], w - 1)
                        pe.matmul(RB1[0:N, 0:GB * E], upper16[:, :], oneh[:, :, :].rearrange("p b e -> p (b e)"),
                                  start=True, stop=False)
                        pe.matmul(RB1[0:N, 0:GB * E], ones16[:, 0:N], cum[:, 0:GB, :].rearrange("p b e -> p (b e)"),
                                  start=False, stop=True)
                        pe.matmul(RB1[:, GB * E:GB * E + E], ones16[:, :], cum[:, GB, :], start=True, stop=True)\
                            .then_inc(S["rank_ps"], 1)

            windows(pe, window)

            pe.wait_ge(S["tab_ok"], 2)
            pe.wait_ge(S["ld_moe"], 16 * (E + 1))

            def step(j, i, tr, l1, htr, l2, t=None, tr0=False):
                t = j // 4 if t is None else t
                if tr:
                    n = (i + 1) % 4
                    pe.wait_ge(blk_in[n], 16 * (t + (1 if i < 3 else 2)))
                    if not tr0:
                        pe.wait_ge(S["xb_ok"], j + 1)
                    pe.transpose(RB0[:, 0:BLK], rin[n][:, D:2 * D], ident).then_inc(S["tr_ps"], 1)
                if l1:
                    e = pe.value_load(tab_e[0:1, bass.ds(j, 1)], min_val=0, max_val=E - 1)
                    pe.wait_ge(S["xb_ok"], j + 1)
                    if l1 > 1:
                        pe.wait_ge(S["hraw_ok"], j - 1)
                    pe.matmul(s2b[:, i % 2, :], xbT[i % 2][:, :], w1s[:, bass.ds(FF * e, FF)], start=True, stop=True)\
                        .then_inc(S["l1_ps"], 1)
                if htr:
                    pe.wait_ge(S["hraw_ok"], j)
                    if htr > 1:
                        pe.wait_ge(S["hb_relu"], j - 2)
                    k = (i + 1) % 2
                    for c in range(NC):
                        ins = pe.transpose(bank[k][:, c * BLK:(c + 1) * BLK], hraw[k][:, c * BLK:(c + 1) * BLK], ident)
                    ins.then_inc(S["htr_ps"], 1)
                if l2:
                    k = i % 2
                    e = pe.value_load(tab_e[0:1, bass.ds(j - 2, 1)], min_val=0, max_val=E - 1)
                    pe.wait_ge(S["hb_relu"], j - 1)
                    if l2 > 1:
                        pe.wait_ge(S["ytmp_ok"], j - 3)
                    for c in range(NC):
                        ins = pe.matmul(bank[2 + k][:, 0:D], hbT[k][:, c, :], w2s[:, bass.ds(FF * e + c * D, D)],
                                        start=(c == 0), stop=(c == NC - 1))
                    ins.then_inc(S["y_ps"], 1)

            step(-1, 3, 1, 0, 0, 0, tr0=True)
            step(0, 0, 1, 1, 0, 0)
            step(1, 1, 1, 1, 1, 0)
            step(2, 2, 1, 2, 1, 1)
            step(3, 3, 1, 2, 2, 1)
            with pe.Fori(1, NBLK // 4 - 1) as t:
                for i in range(4):
                    step(4 * t + i, i, 1, 2, 2, 2, t)
            for j in range(NBLK - 4, NBLK + 2):
                step(j, j % 4, int(j + 1 < NBLK), 2 if j < NBLK else 0, 2 if j - 1 < NBLK else 0, 2)

        @block.vector
        def _(dve):
            linked = [0]

            def link(ins):
                linked[0] += 1
                ins.then_inc(S["dve_seq"], 1)
                dve.wait_ge(S["dve_seq"], linked[0])

            link(dve.memset(scale_win[:, :], 0.0))
            dve.wait_ge(S["ld_tok"], 16)
            link(dve.tensor_copy(tok_f[:, :], tok_i[:, :]))
            link(dve.tensor_scalar(tok_n[:, :], tok_f[:, :], 0.0, float(VOCAB), ALU.is_lt, ALU.mult))
            link(dve.tensor_tensor(tok_f[:, :], tok_n[:, :], tok_f[:, :], ALU.add))
            dve.tensor_scalar(tok_u[:, :], tok_f[:, :], float(VOCAB - 1), 0.0, ALU.min, ALU.max)\
                .then_inc(S["tok_ok"], 1)
            dve.wait_ge(S["ld_a"], 16)
            dve.tensor_tensor(bqk[:, :], A("bq"), A("bk"), ALU.add).then_inc(S["bias_ok"], 1)
            dve.tensor_copy(scale_win[:, 31:32], A("scale")).then_inc(S["scale_ok"], 1)
            dve.wait_ge(S["ld_b"], 16)
            dve.tensor_scalar(qb4[:, :], Bc("qb"), 0.25, None, ALU.mult).then_inc(S["bias_ok"], 1)
            dve.tensor_copy(upper16[:, :], Bc("upper", N)).then_inc(S["upper_ok"], 1)
            link(dve.tensor_copy(cnt[1][:, :], Bc("base")))
            link(dve.tensor_scalar(idf[1][:, :], Bc("id0", N), -float(GT), None, ALU.add))

            def x0_in(g, p, count):
                dve.wait_ge(gathered[p], 16 * GB * count)
                dve.scalar_tensor_tensor(x0[p][:, :, :], emb_in[:, :, :], float(D) ** 0.5,
                                         A("pos", N).unsqueeze(1).to_broadcast([N, GB, D]), ALU.mult, ALU.add)\
                    .then_inc(S["x0_ok"], 1)

            def stats(k, g1, src):
                for b in range(GB):
                    ins = dve.bn_stats(st[k][:, b, :], src[:, b, 0:D])
                ins.then_inc(st_ok[k], 1)
                wait_apart(dve, st_ok[k], g1)
                for b in range(GB):
                    ins = dve.bn_aggr(mv[k][:, b, :], st[k][:, b, :])
                ins.then_inc(mv_ok[k], 1)

            x0_in(0, 0, 1)
            dve.wait_ge(S["ld_edge"], 16)
            link(dve.tensor_copy(key_f[:, :, :], key_e[:, :, :]))
            link(dve.tensor_scalar(key_v[:, :, :], key_f[:, :, :], 0.0, None, ALU.is_ge))
            link(dve.scalar_tensor_tensor(key_w[:, :, :], key_f[:, :, :], float(N), key_v[:, :, :], ALU.is_lt, ALU.mult))
            link(dve.scalar_tensor_tensor(key_1[:, :], key_f[:, 1, :], 1.0, key_w[:, 0, :], ALU.add, ALU.mult))
            link(dve.tensor_tensor(key_v[:, 0, :], key_1[:, :], key_w[:, 1, :], ALU.mult))
            dve.tensor_scalar(key_t[:, :], key_v[:, 0, :], -1.0, None, ALU.add).then_inc(S["key_ok"], 1)

            def edges_in(r):
                if 4 <= r < 12:
                    c = r - 4
                    if c == 0:
                        dve.wait_ge(S["iota_ok"], 2)
                    dve.wait_ge(S["ld_keys"], 16 * (c + 1))
                    link(dve.scalar_tensor_tensor(eprod, ech[c % 2], A("iotap", N), order, ALU.is_equal, ALU.mult))
                    dve.tensor_reduce(cmax[:, c:c + 1], eprod, AX_X, ALU.max).then_inc(S["edge_p"], 1)
                    dve.wait_ge(S["edge_p"], c + 1)
                if r == 13:
                    link(dve.tensor_tensor(cpos[:, :], cmax[:, :], coff[:, :], ALU.add))
                    link(dve.scalar_tensor_tensor(coff[:, :], cmax[:, :], 0.0, cpos[:, :], ALU.is_gt, ALU.mult))
                    link(dve.tensor_reduce(last1[:, :], coff[:, :], AX_X, ALU.max))
                    link(dve.tensor_scalar(hit[:, :], last1[:, :], 0.0, None, ALU.is_gt))
                    dve.tensor_scalar(last_u[:, :], last1[:, :], -1.0, 0.0, ALU.add, ALU.max).then_inc(S["last_ok"], 1)
                if r == 19:
                    dve.wait_ge(S["edge_at_ps"], 1)
                    dve.tensor_copy(atT[:, :], RB0[0:3, 0:N]).then_inc(S["atT_ok"], 1)
                if r == 21:
                    dve.wait_ge(S["edge_cb_ps"], 1)
                    link(dve.tensor_tensor(cbias[:, :], RB1[0:N, 0:H], Rw("ebb"), ALU.add))
                    link(dve.tensor_scalar(cbh[:, :], cbias[:, :], hit[:, 0:1], None, ALU.mult))
                    link(dve.tensor_copy(cb16[:, 0, :], cbh[:, :]))
                    link(dve.tensor_tensor(crem[0][:, :], cbh[:, :], cb16[:, 0, :], ALU.subtract))
                    link(dve.tensor_copy(cb16[:, 1, :], crem[0][:, :]))
                    link(dve.tensor_tensor(crem[1][:, :], crem[0][:, :], cb16[:, 1, :], ALU.subtract))
                    link(dve.tensor_copy(cb16[:, 2, :], crem[1][:, :]))
                    dve.tensor_copy(cb32[:, :, :], cb16[:, :, :]).then_inc(S["cb32_ok"], 1)
                if r == 23:
                    dve.wait_ge(S["edge_cbT_ps"], 1)
                    link(dve.tensor_copy(cbT[:, :], RB0[0:3 * H, 0:N]))
                    dve.tensor_tensor(cbx[:, :, :], cbT[:, :].unsqueeze(1).to_broadcast([3 * H, H, N]),
                                      Bc("mask24", 3 * H).unsqueeze(2).to_broadcast([3 * H, H, N]), ALU.mult)\
                        .then_inc(S["cb_ok"], 1)

            dve.wait_ge(S["ld_rows"], 16)

            def window(w, p, pair, front, units, a, b):
                q = 1 - p
                first = isinstance(w, int) and w == 0

                def shifted(bb):
                    n = GB * (w - 2) + bb + 1
                    s = s2b[0:N, :, 0:4 * N].rearrange("p u (v m) -> p u v m", v=4)
                    dve.wait_ge(S["s2_ps"], n)
                    dve.tensor_reduce(nm2[bb % 2][:, :].rearrange("p (u v) -> p u v", u=2), s, AX_X, ALU.max, negate=True)\
                        .then_inc(S["nm2_ok"], 1)
                    dve.wait_ge(S["nm2_ok"], n)
                    dve.tensor_tensor(p2[bb % 2][:, :, :].rearrange("p (u v) m -> p u v m", u=2), s,
                                      nm2[bb % 2][:, :].rearrange("p (u v) -> p u v", u=2).unsqueeze(3)
                                      .to_broadcast([N, 2, 4, N]), ALU.add).then_inc(S["p2_ok"], 1)

                def divided(bb):
                    n = GB * (w - 2) + bb + 1
                    o = RB0[0:N, 0:H * (HD + 1)].rearrange("p (h d) -> p h d", h=H)
                    dve.wait_ge(S["pv_ps"], n)
                    dve.reciprocal(rd2[bb % 2][:, :], o[:, :, HD]).then_inc(S["rd2_ok"], 1)
                    dve.wait_ge(S["rd2_ok"], n)
                    dve.tensor_tensor(a2[:, bb, :, :], o[:, :, 0:HD],
                                      rd2[bb % 2][:, :].unsqueeze(2).to_broadcast([N, H, HD]), ALU.mult)\
                        .then_inc(S["a2_ok"], 1)

                for r in range(R):
                    if units and r == 0:
                        dve.wait_ge(S["q_ok"], w + 1)
                        dve.wait_ge(S["k_ok"], w + 1)
                        if not first:
                            dve.wait_ge(S["sum_dve"], NV * w)
                        dve.tensor_copy(feat(QP), qS[p][:, :]).then_inc(S["qp_ok"], 1)
                        dve.wait_ge(S["qp_ok"], w + 1)
                    if units and r in DVE_UNITS:
                        if not (first and r < RING):
                            dve.wait_ge(S["unit_used"], R * w + r - RING + 1)
                        dve.tensor_tensor(
                            ring[:, r % RING, :].rearrange("p (c b j) -> p c b j", c=4, b=GB),
                            kS[p][:, :].rearrange("p (b j) -> p b j", b=GB).unsqueeze(1).to_broadcast([128, 4, GB, N]),
                            feat(QP).rearrange("p (b c r) -> p c b r", b=GB, c=4)[:, :, :, r].unsqueeze(3)
                            .to_broadcast([128, 4, GB, N]), ALU.add).then_inc(S["sum_dve"], 1)
                    if first:
                        edges_in(r)
                    if a and r == 2:
                        dve.wait_ge(S["unit_used"], R * w)
                        dve.tensor_reduce(nmax[:, :], feat(SC).rearrange("p (b j) -> p b j", b=GB), AX_X, ALU.max,
                                          negate=True).then_inc(S["nmax_ok"], 1)
                    if a and r == 3:
                        dve.wait_ge(S["exp1_ok"], GB * w)
                        dve.reciprocal(rs1[:, :], sum1[:, :]).then_inc(S["rs1_ok"], 1)
                    for bb in range(GB):
                        if b and r == 4 + 4 * bb:
                            shifted(bb)
                        if b and r == 6 + 4 * bb:
                            divided(bb)
                    if a and r == 5:
                        dve.wait_ge(S["p1T_ps"], w)
                        dve.tensor_copy(pT[:, :, :].rearrange("p b (c r) -> p b c r", c=4),
                                        RA0[0:N, :].rearrange("p (b c r) -> p b c r", b=GB, c=4)[:, :, :, 0:R])\
                            .then_inc(S["pT_ok"], 1)
                    if a and r == 7:
                        dve.wait_ge(S["wo_ps"], w)
                        dve.wait_ge(S["x0b_ok"], w)
                        dve.tensor_tensor(r1[:, :, :], tokv(RA0), x0[q][:, :, :], ALU.add).then_inc(S["r1_ok"], 1)
                        dve.wait_ge(S["r1_ok"], w)
                        stats(0, w, r1)
                    if a and r == 9:
                        dve.wait_ge(S["n1T_ps"], w)
                        dve.tensor_scalar(x1T[:, :], feat(RA1), Bc("g1"), Bc("beta1"), ALU.mult, ALU.add)\
                            .then_inc(S["x1T_ok"], 1)
                    if front and r == 10:
                        x0_in(w + 1, q, pair + 1 + p)
                    if a and r == 13:
                        dve.wait_ge(S["f2_ps"], w)
                        dve.scalar_tensor_tensor(r2T[:, :], feat(RA0), Bc("bf2"), x1T[:, :], ALU.add, ALU.add)\
                            .then_inc(S["r2T_ok"], 1)
                    if a and r == 14:
                        dve.wait_ge(S["r2_ps"], w)
                        stats(1, w, tokv(RA1))
                    if a and r == 15:
                        dve.wait_ge(rstd_ok[1], w)
                        for bb in range(GB):
                            ins = dve.tensor_scalar(n2[:, bb, :], tokv(RA1)[:, bb, :], mv[1][:, bb, 0:1],
                                                    rstd[1][:, bb:bb + 1], ALU.subtract, ALU.mult)
                        ins.then_inc(S["n2_ok"], 1)
                    if a and r == 17:
                        dve.wait_ge(S["h_ok"], w)
                        stats(2, w, h)
                    if b and r == 19:
                        dve.wait_ge(S["o_ps"], w - 1)
                        dve.wait_ge(S["hb_ok"], w - 1)
                        if not (isinstance(w, int) and w < 4):
                            dve.wait_ge(scattered[p], 16 * GB * (pair - 1))
                        dve.tensor_tensor(row[p][:, :, 0:D], tokv(RB0), hb[p][:, :, :], ALU.add)\
                            .then_inc(S["h2_ok"], 1)
                        dve.wait_ge(S["h2_ok"], w - 1)
                        stats(3, w - 1, row[p])
                    if b and r == 21:
                        dve.wait_ge(S["lg_ps"], w - 1)
                        dve.tensor_tensor(lg[:, :, :], RB0[0:N, 0:GB * E].rearrange("p (b e) -> p b e", b=GB),
                                          Rw("br").unsqueeze(1).to_broadcast([N, GB, E]), ALU.add).then_inc(S["lg_ok"], 1)
                        dve.wait_ge(S["lg_ok"], w - 1)
                        dve.tensor_reduce(lmax[:, :], lg[:, :, :], AX_X, ALU.max).then_inc(S["lmax_ok"], 1)
                        dve.wait_ge(S["lmax_ok"], w - 1)
                        dve.tensor_tensor(lzero[:, :], lmax[:, :], lmax[:, :], ALU.subtract).then_inc(S["lzero_ok"], 1)
                        dve.tensor_tensor(eqm[:, :, :], lg[:, :, :], lmax[:, :].unsqueeze(2).to_broadcast([N, GB, E]),
                                          ALU.is_equal).then_inc(S["eqm_ok"], 1)
                        dve.wait_ge(S["eqm_ok"], w - 1)
                        dve.tensor_tensor(eqw[:, :, :], eqm[:, :, :],
                                          Bc("wtab", N).unsqueeze(1).to_broadcast([N, GB, E]), ALU.mult)\
                            .then_inc(S["eqw_ok"], 1)
                        dve.wait_ge(S["eqw_ok"], w - 1)
                        dve.tensor_reduce(wsel[:, :], eqw[:, :, :], AX_X, ALU.max).then_inc(S["wsel_ok"], 1)
                        dve.wait_ge(S["wsel_ok"], w - 1)
                        dve.tensor_tensor(oneh[:, :, :], Bc("wtab", N).unsqueeze(1).to_broadcast([N, GB, E]),
                                          wsel[:, :].unsqueeze(2).to_broadcast([N, GB, E]), ALU.is_equal)\
                            .then_inc(S["oneh_ok"], 1)
                        dve.wait_ge(S["oneh_ok"], w - 1)
                        for bb in range(GB):
                            done = S[f"cum{bb + 1}"]
                            dve.tensor_tensor(cum[:, bb + 1, :], cum[:, bb, :], oneh[:, bb, :], ALU.add).then_inc(done, 1)
                            dve.wait_ge(done, w - 1)
                    if b and r == 22:
                        dve.wait_ge(S["rank_ps"], w - 1)
                        dve.tensor_tensor(posv[:, :, :], RB1[0:N, 0:GB * E].rearrange("p (b e) -> p b e", b=GB),
                                          cnt[q][0:N, :].unsqueeze(1).to_broadcast([N, GB, E]), ALU.add)\
                            .then_inc(S["posv_ok"], 1)
                        dve.tensor_tensor(cnt[p][:, :], cnt[q][:, :], RB1[:, GB * E:GB * E + E], ALU.add)\
                            .then_inc(S["cnt_ok"], 1)
                        dve.wait_ge(S["posv_ok"], w - 1)
                        dve.tensor_tensor(posm[:, :, :], posv[:, :, :], oneh[:, :, :], ALU.mult).then_inc(S["posm_ok"], 1)
                        dve.tensor_scalar(idf[p][:, :], idf[q][:, :], float(GT), None, ALU.add).then_inc(S["idf_ok"], 1)
                        dve.wait_ge(S["posm_ok"], w - 1)
                        dve.tensor_reduce(posf[:, :], posm[:, :, :], AX_X, ALU.add).then_inc(S["posf_ok"], 1)
                        dve.wait_ge(S["gexp_ok"], w - 1)
                        dve.reciprocal(ginv[:, :], gexp[:, :]).then_inc(S["ginv_ok"], 1)
                        dve.wait_ge(S["posf_ok"], w - 1)
                        dve.tensor_copy(posu[p][:, :], posf[:, :]).then_inc(S["pos_ok"], 1)
                        dve.wait_ge(S["idf_ok"], w - 1)
                        dve.tensor_copy(row[p][:, :, 2 * D + 1].bitcast(I32), idf[p][:, :]).then_inc(S["id_ok"], 1)
                        dve.wait_ge(S["ginv_ok"], w - 1)
                        dve.tensor_tensor(row[p][:, :, 2 * D], gexp[:, :], ginv[:, :], ALU.mult).then_inc(S["gate_ok"], 1)
                        dve.wait_ge(S["cnt_ok"], w - 1)

            windows(dve, window)

            last = cnt[1]
            KB = B * N // BLK
            link(dve.tensor_scalar(padf[:, :], last[:, :], A("iotap"), None, ALU.add))
            dve.tensor_copy(padu[:, :], padf[:, :]).then_inc(S["pad_ok"], 1)
            link(dve.tensor_tensor(blk_c[:, :], last[0:1, :], Bc("base", 1), ALU.subtract))
            link(dve.tensor_tensor(blk_g[:, :, :], blk_c[:, :].unsqueeze(2).to_broadcast([1, E, KB]),
                                   Bc("k128", 1).unsqueeze(1).to_broadcast([1, E, KB]), ALU.is_gt))
            link(dve.tensor_reduce(blk_n[:, :], blk_g[:, :, :], AX_X, ALU.add))
            link(dve.tensor_copy(blk_end[:, 0:1], blk_n[:, 0:1]))
            for e in range(1, E):
                link(dve.tensor_tensor(blk_end[:, e:e + 1], blk_end[:, e - 1:e], blk_n[:, e:e + 1], ALU.add))
            link(dve.tensor_tensor(blk_ge[:, :, :], Bc("jtab", 1).unsqueeze(2).to_broadcast([1, NBLK, E]),
                                   blk_end[:, :].unsqueeze(1).to_broadcast([1, NBLK, E]), ALU.is_ge))
            link(dve.tensor_reduce(blk_e[:, :], blk_ge[:, :, :], AX_X, ALU.add))
            link(dve.tensor_tensor(blk_gn[:, :, :], blk_ge[:, :, :],
                                   blk_n[:, :].unsqueeze(1).to_broadcast([1, NBLK, E]), ALU.mult))
            link(dve.tensor_reduce(blk_s[:, :], blk_gn[:, :, :], AX_X, ALU.add))
            link(dve.tensor_tensor(blk_t[:, :], Bc("jtab", 1), blk_s[:, :], ALU.subtract))
            link(dve.tensor_scalar(blk_t2[:, :], blk_t[:, :], float(BLK), None, ALU.mult))
            link(dve.scalar_tensor_tensor(blk_s[:, :], blk_e[:, :], float(REG), blk_t2[:, :], ALU.mult, ALU.add))
            link(dve.tensor_scalar(blk_em[:, :], blk_e[:, :], float(E - 1), None, ALU.min))
            dve.tensor_copy(tab_r[:, :], blk_s[:, :]).then_inc(S["tab_ok"], 1)
            dve.tensor_copy(tab_e[:, :], blk_em[:, :]).then_inc(S["tab_ok"], 1)
            dve.wait_ge(S["tab_ok"], 2)

            def step(j, i, xt, hraw_, y):
                if xt:
                    dve.wait_ge(S["tr_ps"], j + 2)
                    dve.tensor_copy(xbT[(i + 1) % 2][:, :], RB0[:, 0:BLK]).then_inc(S["xb_ok"], 1)
                if hraw_:
                    dve.wait_ge(S["l1_ps"], j + 1)
                    if hraw_ > 1:
                        dve.wait_ge(S["htr_ps"], j - 1)
                    dve.tensor_copy(hraw[i % 2][:, :], s2b[:, i % 2, :]).then_inc(S["hraw_ok"], 1)
                if y:
                    k, n = i % 2, (i + 2) % 4
                    e = dve.value_load(tab_e[0:1, bass.ds(j - 2, 1)], min_val=0, max_val=E - 1)
                    dve.wait_ge(S["y_ps"], j - 1)
                    dve.tensor_tensor(ytmp[k][:, :], bank[2 + k][:, 0:D],
                                      rw[:, bass.ds(D * e + ROWS["b2"][0], D)], ALU.add).then_inc(S["ytmp_ok"], 1)
                    dve.wait_ge(S["ytmp_ok"], j - 1)
                    dve.scalar_tensor_tensor(yout[n][:, :], ytmp[k][:, :], rin[n][:, 2 * D:2 * D + 1], rin[n][:, 0:D],
                                             ALU.mult, ALU.add).then_inc(S["yo_ok"], 1)

            step(-1, 3, 1, 0, 0)
            step(0, 0, 1, 1, 0)
            step(1, 1, 1, 1, 0)
            step(2, 2, 1, 2, 1)
            step(3, 3, 1, 2, 1)
            with dve.Fori(1, NBLK // 4 - 1) as t:
                for i in range(4):
                    step(4 * t + i, i, 1, 2, 1)
            for j in range(NBLK - 4, NBLK + 2):
                step(j, j % 4, int(j + 1 < NBLK), 2 if j < NBLK else 0, 1)


def kernel(**inputs):
    import numpy as np
    import concourse.bacc as _bacc
    from concourse import mybir as _mybir
    from concourse.bass_utils import run_bass_kernel_spmd as _run

    x = {k: np.asarray(v) for k, v in inputs.items()}
    f32 = np.float32

    def columns(v):
        return v.reshape(-1, D).T

    def chunked(wt):
        return wt.reshape(-1, D, wt.shape[1]).transpose(1, 0, 2).reshape(D, -1)

    pos = np.zeros((D, D), f32)
    ang = np.arange(N)[:, None].astype(np.float64) / np.power(
        10000.0, 2 * (np.arange(D)[None, :] // 2) / np.float32(D))
    ang[:, 0::2] = np.sin(ang[:, 0::2])
    ang[:, 1::2] = np.cos(ang[:, 1::2])
    pos[:N] = ang
    p = np.arange(D)
    upper = np.zeros((D, N), f32)
    upper[:N] = np.arange(N)[:, None] < np.arange(N)[None, :]
    mask24 = np.zeros((D, H), f32)
    mask24[:3 * H] = (np.arange(3 * H)[:, None] % H) == np.arange(H)[None, :]

    def rowc(v):
        return np.broadcast_to(np.asarray(v, f32)[None, :], (D, len(v)))

    part_a = {
        "ident": np.eye(D, dtype=f32), "pos": pos, "wq": x["L0_tok_Wq"], "wk": x["L0_tok_Wk"], "wv": x["L0_tok_Wv"],
        "bq": columns(x["L0_tok_bq"]), "bk": columns(x["L0_tok_bk"]), "scale": columns(x["L0_tok_attn_scale"]),
        "iotap": p[:, None].astype(f32)}
    part_b = {
        "wo": x["L0_tok_Wo"], "w1": x["L0_tok_W1"], "w2": chunked(x["L0_tok_W2"]), "qw": x["L0_attn_q_w"].T,
        "kw": x["L0_attn_k_w"].T, "vw": x["L0_attn_v_w"].T, "ow": x["L0_attn_o_w"].T, "wr": x["L0_ffn_Wr"],
        "bv": columns(x["L0_tok_bv"]), "g1": columns(x["L0_tok_g1"]), "beta1": columns(x["L0_tok_beta1"]),
        "bf1": columns(x["L0_tok_bf1"]), "bf2": columns(x["L0_tok_bf2"]), "qb": columns(x["L0_attn_q_b"]),
        "kb": columns(x["L0_attn_k_b"]), "vb": columns(x["L0_attn_v_b"]), "b1": columns(x["L0_ffn_b1"].reshape(-1)),
        "hmask": (p[:, None] // HD == np.arange(H)[None, :]).astype(f32), "mask24": mask24,
        "base": rowc(np.arange(E) * REG), "wtab": rowc(E - np.arange(E)), "upper": upper,
        "id0": (p[:, None] + N * np.arange(GB)[None, :]).astype(f32), "jtab": rowc(np.arange(NBLK)),
        "k128": rowc(np.arange(B * N // BLK) * BLK)}
    pack = [np.ascontiguousarray(np.concatenate([part[k] for k in lay if k != "_"], axis=1))
            for part, lay in ((part_a, LAY_A), (part_b, LAY_B))]
    rows = np.concatenate([x["L0_tok_bo"], x["L0_tok_g2"], x["L0_tok_beta2"], x["L0_attn_o_b"], x["L0_ffn_br"],
                           x["L0_attn_eb_b"], x["L0_ffn_b2"].reshape(-1)])[None, :]
    arrays = {
        "tok": np.ascontiguousarray(x["x"].T), "emb": x["L0_tok_emb"], "pack_a": pack[0], "pack_b": pack[1],
        "rows": rows, "edges": x["L0_attn_edge_index"], "attr": x["L0_attn_edge_attr"],
        "ebw": np.ascontiguousarray(x["L0_attn_eb_w"].T), "w1m": x["L0_ffn_W1"], "w2m": x["L0_ffn_W2"]}

    nc = _bacc.Bacc("TRN2", target_bir_lowering=False, num_devices=1)
    args = [nc.dram_tensor(k, a.shape, _mybir.dt.from_np(a.dtype), kind="ExternalInput").ap()
            for k, a in arrays.items()]
    args.append(nc.dram_tensor("out", (B, N, D), F32, kind="ExternalOutput").ap())
    tower(nc, *args)
    r = _run(nc, [arrays], core_ids=[0])
    return r.results[0]["out"]
```

```python
from contextlib import ExitStack

import concourse.bass as bass
from concourse import mybir

F32 = mybir.dt.float32
BF16 = mybir.dt.bfloat16
I32 = mybir.dt.int32
U32 = mybir.dt.uint32
ALU = mybir.AluOpType
ACT = mybir.ActivationFunctionType
AX_X = mybir.AxisListType.X

B, N, D = 64, 96, 128
VOCAB = 8000
FF = 512
NC = FF // D
H, HD = 8, 16
E = 8
NE = 8192
GB = 4
G = B // GB
GT = GB * N
R = N // 4
RING = 8
UT = 4 * GT
POOL_UNITS = tuple(range(1, R, 3))
DVE_UNITS = tuple(r for r in range(R) if r not in POOL_UNITS)
NP, NV = len(POOL_UNITS), len(DVE_UNITS)
EPS_TOK, EPS_LN = 1e-6, 1e-5
BLK = 128
NBLK = B * N // BLK + E
REG = B * N + BLK
ROW = 2 * D + 2
FAR = 1 << 20
EC = NE // 8

BUF = 8

PE_AT = {"xT": -24, "qk": -24, "v": -18, "p1T": 26, "aT": 27, "wo": 29, "n1T": 34, "f1": (35, 37), "f2": 40, "r2": 43,
         "hnT": 51, "q2k2": 54, "v2": 57, "s2": (58, 62, 64, 71), "p2T": (63, 67, 70, 74), "pv": (64, 69, 72, 75),
         "a2T": 78, "o": 81, "xfT": 86, "lg": 87, "rank": 92}
ACT_AT = {"xT": -20, "qk": -16, "v": -13, "exp1": 27, "aT": 32, "x1T": 37, "relu": (38, 39), "hnT": 56, "q2k2": 59,
          "v2": 60, "exp2": (63, 66, 74, 76), "p2T": (65, 70, 75, 79), "a2T": 83, "xfT": 88, "gexp": 93}
DVE_AT = {"x0": -19, "nmax": 29, "rs1": 30, "pT": 33, "r1": 36, "n1": 39, "r2T": 48, "stats1": 49, "n2": 52, "stats2":
          55, "hn": 57, "mean": (38, 50, 56), "shift": (67, 69, 72, 78), "divide": (72, 75, 80, 83), "h2": 89, "xf":
          91, "router": 95, "place": 98}
POOL_AT = {"gather": -24, "bo": -9, "p1n": 31, "rsqrt0": 38, "rsqrt1": 49, "h": 53, "rsqrt2": 56, "kx": (62, 62, 67,
           70), "rsqrt3": 89, "lzero": 96, "scatter": 106}
DEPTH = max(s for table in (PE_AT, ACT_AT, DVE_AT, POOL_AT) for s in table.values() if isinstance(s, int)) // R

LAY_A, LAY_B = {}, {}
for _lay, _items in ((LAY_A, (("ident", D), ("pos", D), ("wq", D), ("wk", D), ("wv", D), ("bq", 1), ("bk", 1),
                              ("scale", 1), ("iotap", 1))),
                     (LAY_B, (("wo", D), ("w1", FF), ("w2", FF), ("qw", D), ("kw", D), ("vw", D), ("ow", D), ("wr", E),
                              ("bv", 1), ("g1", 1), ("beta1", 1), ("bf1", NC), ("bf2", 1), ("qb", 1), ("kb", 1),
                              ("vb", 1), ("b1", E * NC), ("hmask", H), ("mask24", H), ("base", E), ("wtab", E),
                              ("upper", N), ("jtab", NBLK), ("k128", B * N // BLK)))):
    _at = 0
    for _name, _n in _items:
        _lay[_name] = (_at, _n)
        _at += _n
    _lay["_"] = (_at, 0)
ROWS = {"bo": (0, D), "g2": (D, D), "beta2": (2 * D, D), "ob": (3 * D, D), "br": (4 * D, E), "ebb": (4 * D + E, H),
        "b2": (4 * D + E + H, E * D)}
ROWS_N = 4 * D + E + H + E * D


def tower(nc, tok, emb, pack_a, pack_b, rows, edges, attr, ebw, w1m, w2m, out):
    out_rows = out.rearrange("b n d -> (b n) d")
    sorted_rows = nc.dram_tensor("sorted_rows", (E * REG + E * BLK, ROW), F32, kind="Internal").ap()
    edge_keys = nc.dram_tensor("edge_keys", (128, NE // 128), F32, kind="Internal").ap()

    with ExitStack() as ctx:
        def sb(name, shape, dt=F32):
            return ctx.enter_context(nc.sbuf_tensor(name, shape, dt))

        def sem(name):
            return ctx.enter_context(nc.semaphore(name))

        ca = sb("pack_a_sb", [128, LAY_A["_"][0]])
        cb = sb("pack_b_sb", [128, LAY_B["_"][0]])
        rw = sb("rows_sb", [128, ROWS_N])

        def A(name, p=128):
            at, n = LAY_A[name]
            return ca[0:p, at:at + n]

        def Bc(name, p=128):
            at, n = LAY_B[name]
            return cb[0:p, at:at + n]

        def Rw(name, p=N):
            at, n = ROWS[name]
            return rw[0:p, at:at + n]

        ring = sb("ring", [128, RING, UT])
        tok_i = sb("tok_i", [N, B], I32)
        tok_f = sb("tok_f", [N, B])
        tok_n = sb("tok_n", [N, B])
        tok_u = sb("tok_u", [N, B], U32)
        tok_g = sb("tok_g", [N, GB], U32)
        bqk = sb("bqk", [128, 1])
        qb4 = sb("qb4", [128, 1])
        scale_win = sb("scale_win", [128, 63])
        emb_in = sb("emb_in", [N, GB, D])
        x0 = sb("x0", [N, GB, D])
        x0b = [sb(f"x0b_{p}", [N, GB, D]) for p in range(2)]
        xT = sb("xT", [128, GT])
        qS = [sb(f"qS_{p}", [128, GT]) for p in range(2)]
        kS = [sb(f"kS_{p}", [128, GT]) for p in range(2)]
        vS = [sb(f"vS_{p}", [N, GB, D]) for p in range(2)]
        nmax = sb("nmax", [128, GB])
        sum1 = sb("sum1", [128, GB])
        rs1 = sb("rs1", [128, GB])
        p1 = sb("p1", [128, GB, N])
        p1n = sb("p1n", [128, GB, N])
        pT = sb("pT", [N, GB, N])
        aT = sb("aT", [128, GT])
        r1 = sb("r1", [N, GB, D])
        st = [sb(f"st{k}", [N, GB, 6]) for k in range(4)]
        mv = [sb(f"mv{k}", [N, GB, 2]) for k in range(4)]
        ve = [sb(f"ve{k}", [N, GB]) for k in range(4)]
        rstd = [sb(f"rstd{k}", [N, GB]) for k in range(4)]
        mhalf = sb("mhalf", [N, GB])
        n1 = sb("n1", [N, GB, D])
        x1T = sb("x1T", [128, GT])
        hT = sb("hT", [128, NC, GT])
        r2T = sb("r2T", [128, GT])
        n2 = sb("n2", [N, GB, D])
        n2g = sb("n2g", [N, GB, D])
        h = sb("h", [N, GB, D])
        hb = [sb(f"hb_{p}", [N, GB, D]) for p in range(2)]
        hn = sb("hn", [N, GB, D])
        hnT = sb("hnT", [128, GT])
        q2T = sb("q2T", [128, GT])
        k2T = sb("k2T", [128, GT])
        v2 = sb("v2", [N, GB, H, HD + 1])
        kx = sb("kx", [128, GB, H, N])
        nm2 = [sb(f"nm2_{i}", [N, H]) for i in range(2)]
        p2 = [sb(f"p2_{i}", [N, H, N]) for i in range(2)]
        p2T = sb("p2T", [N, H, N])
        rd2 = [sb(f"rd2_{i}", [N, H]) for i in range(2)]
        a2 = sb("a2", [N, GB, H, HD])
        a2T = sb("a2T", [128, GT])
        row = [sb(f"row_{p}", [N, GB, ROW]) for p in range(2)]
        xfT = sb("xfT", [128, GT])
        lg = sb("lg", [N, GB, E])
        lmax = sb("lmax", [N, GB])
        lzero = sb("lzero", [N, GB])
        gexp = sb("gexp", [N, GB])
        ginv = sb("ginv", [N, GB])
        eqm = sb("eqm", [N, GB, E])
        eqw = sb("eqw", [N, GB, E])
        wsel = sb("wsel", [N, GB])
        oneh = sb("oneh", [N, GB, E], BF16)
        upper16 = sb("upper16", [N, N], BF16)
        ones16 = sb("ones16", [N, 128], BF16)
        posv = sb("posv", [N, GB, E])
        posm = sb("posm", [N, GB, E])
        posf = sb("posf", [N, GB])
        posu = [sb(f"posu_{p}", [N, GB], U32) for p in range(2)]
        cnt = [sb(f"cnt_{p}", [128, E]) for p in range(2)]
        ids = sb("ids", [N, B])
        key_e = sb("key_e", [128, 2, NE // 128], I32)
        key_f = sb("key_f", [128, 2, NE // 128])
        key_v = sb("key_v", [128, 2, NE // 128])
        key_w = sb("key_w", [128, 2, NE // 128])
        key_t = sb("key_t", [128, NE // 128])
        key_1 = sb("key_1", [128, NE // 128])
        cmax = sb("cmax", [N, 8])
        cpos = sb("cpos", [N, 8])
        coff = sb("coff", [N, 8])
        last1 = sb("last1", [N, 1])
        hit = sb("hit", [N, 1])
        last_f = sb("last_f", [N, 1])
        last_u = sb("last_u", [N, 1], U32)
        at_rows = sb("at_rows", [N, 3])
        atT = sb("atT", [3, N])
        ebw_sb = sb("ebw_sb", [3, H])
        cbias = sb("cbias", [N, H])
        cbh = sb("cbh", [N, H])
        cb16 = sb("cb16", [N, 3, H], BF16)
        cb32 = sb("cb32", [N, 3, H])
        crem = [sb(f"crem{i}", [N, H]) for i in range(2)]
        cbT = sb("cbT", [3 * H, N])
        cbx = sb("cbx", [3 * H, H, N], BF16)
        ones24 = sb("ones24", [3 * H, N], BF16)
        order = hT[0:N, :, :].rearrange("p c t -> p (c t)")[:, 0:EC]
        kx_flat = kx[0:N, :, :, :].rearrange("p b h n -> p (b h n)")
        ech = [kx_flat[:, i * EC:(i + 1) * EC] for i in range(2)]
        eprod = kx_flat[:, 2 * EC:3 * EC]
        w1s = ring[:, 0:RING // 2, :].rearrange("p a n -> p (a n)")[:, 0:E * FF]
        w2s = ring[:, RING // 2:RING, :].rearrange("p a n -> p (a n)")[:, 0:E * FF]
        padrow = sb("padrow", [BLK, ROW])
        padf = sb("padf", [BLK, E])
        padu = sb("padu", [BLK, E], U32)
        blk_n = sb("blk_n", [1, E])
        blk_g = sb("blk_g", [1, E, B * N // BLK])
        blk_c = sb("blk_c", [1, E])
        blk_end = sb("blk_end", [1, E])
        blk_ge = sb("blk_ge", [1, NBLK, E])
        blk_gn = sb("blk_gn", [1, NBLK, E])
        blk_e = sb("blk_e", [1, NBLK])
        blk_s = sb("blk_s", [1, NBLK])
        blk_t = sb("blk_t", [1, NBLK])
        blk_t2 = sb("blk_t2", [1, NBLK])
        blk_em = sb("blk_em", [1, NBLK])
        tab_e = sb("tab_e", [1, NBLK], I32)
        tab_r = sb("tab_r", [1, NBLK], I32)
        rin = [sb(f"rin{i}", [BLK, ROW]) for i in range(BUF)]
        yout = [sb(f"yout{i}", [BLK, D]) for i in range(BUF)]
        xbT = [sb(f"xbT{i}", [128, BLK]) for i in range(2)]
        hraw = [sb(f"hraw{i}", [BLK, FF]) for i in range(2)]
        hbT = [sb(f"hbT{i}", [128, NC, BLK]) for i in range(2)]
        ytmp = [sb(f"ytmp{i}", [BLK, D]) for i in range(2)]

        bank = [ctx.enter_context(nc.psum_tensor(f"bank{i}", [128, 512], F32)) for i in range(4)]
        s2b = ctx.enter_context(nc.psum_tensor("s2_banks", [128, 2, 512], F32))
        rbb = ctx.enter_context(nc.psum_tensor("rb_banks", [128, 2, 512], F32))
        QP, SC, RA0, RA1 = bank
        RB0, RB1 = rbb[:, 0, :], rbb[:, 1, :]
        S0, S1 = s2b[:, 0, :], s2b[:, 1, :]

        def feat(b):
            return b[:, 0:GT]

        def tokv(b):
            return b[0:N, :].rearrange("p (b d) -> p b d", b=GB)

        def cols(t, b):
            return t[:, b * N:(b + 1) * N]

        names = """ld_a ld_b ld_rows ld_tok ld_edge ld_ebw ld_keys ld_attr key_out ld_moe
            consts tok_ok tok_g_ok x0_ok xT_ps xT_ok q_ps q_ok k_ps k_ok v_ps v_ok x0b_ok
            qp_ok sum_dve sum_pool tanh_ok unit_used
            nmax_ok exp1_ok rs1_ok p1n_ok p1T_ps pT_ok aT_ps aT_ok wo_ps r1_ok n1_ok n1T_ps x1T_ok
            f1_ps hT_ok f2_ps r2T_ok r2_ps n2_ok n2g_ok h_ok hb_ok hn_ok hnT_ps hnT_ok
            q2_ps q2_ok k2_ps k2_ok v2_ps v2_ok kx_ok s2_ps nm2_ok p2_ok e2_ok p2T_ps p2T_ok pv_ps
            rd2_ok a2_ok a2T_ps a2T_ok o_ps h2_ok xf_ok xfT_ps xfT_ok lg_ps lg_ok chosen lzero_ok gexp_ok ginv_ok
            gate_ok rank_ps posv_ok placed pos_ok cnt_ok
            id_ok
            passed dve_seq bias_ok scale_ok upper_ok init_ok key_ok edge_p last_ok edge_at_ps atT_ok edge_cb_ps cb32_ok
            edge_cbT_ps cb_ok iota_ok pad_ok pad_out tab_ok
            tr_ps xb_ok l1_ps hraw_ok htr_ps hb_relu y_ps ytmp_ok yo_ok"""
        S = {n: sem(n) for n in names.split()}
        st_ok = [sem(f"st{k}_ok") for k in range(4)]
        mv_ok = [sem(f"mv{k}_ok") for k in range(4)]
        ve_ok = [sem(f"ve{k}_ok") for k in range(4)]
        rstd_ok = [sem(f"rstd{k}_ok") for k in range(4)]
        gathered = [sem(f"gathered_{p}") for p in range(2)]
        scattered = [sem(f"scattered_{p}") for p in range(2)]
        blk_in = [sem(f"blk_in{i}") for i in range(BUF)]
        blk_out = [sem(f"blk_out{i}") for i in range(BUF)]

        block = ctx.enter_context(nc.Block())

        def wait_apart(eng, s, value):
            eng.wait_ge(s, value)
            eng.sem_inc(S["passed"], 1)

        def windows(eng, window):
            window(-1, 1)
            for t in range(3):
                window(t, 0)
                window(t, 1)
            with eng.Fori(3, G // 2 - 1) as t:
                window(t, 0)
                window(t, 1)
            for w in range(G - 2, G + DEPTH):
                window(w // 2, w % 2)

        def due(t, p, r, slot):
            if slot % R != r:
                return ()
            k = slot // R
            gp = (p - k) % 2
            gt = t + (p - k - gp) // 2
            g = 2 * t + (p - k)
            if isinstance(t, int) and not 0 <= g < G:
                return ()
            return ((g, gp, gt),)

        def peeled(g):
            return isinstance(g, int)

        @block.sync
        def _(sp):
            sp.dma_start(tok_i[:, :], tok).then_inc(S["ld_tok"], 16)
            sp.dma_start(ca[:, :], pack_a).then_inc(S["ld_a"], 16)
            sp.dma_start(key_e[:, :, :], edges.rearrange("s (p f) -> p s f", p=128)).then_inc(S["ld_edge"], 16)
            sp.dma_start(cb[:, :], pack_b).then_inc(S["ld_b"], 16)
            sp.dma_start(rw[:, :], rows.to_broadcast([128, ROWS_N])).then_inc(S["ld_rows"], 16)
            sp.dma_start(ebw_sb[:, :], ebw).then_inc(S["ld_ebw"], 16)
            sp.wait_ge(S["key_ok"], 1)
            sp.dma_start(edge_keys, key_t[:, :]).then_inc(S["key_out"], 16)
            sp.wait_ge(S["key_out"], 16)
            flat = edge_keys.rearrange("p f -> (p f)").rearrange("(a n) -> a n", a=8)
            for c in range(8):
                if c >= 2:
                    sp.wait_ge(S["edge_p"], c - 1)
                sp.dma_start(ech[c % 2], flat[c:c + 1, :].to_broadcast([N, EC])).then_inc(S["ld_keys"], 16)
                sp.wait_ge(S["ld_keys"], 16 * (c + 1))
            sp.wait_ge(S["unit_used"], R * G)
            sp.dma_start(w1s.rearrange("p (e f) -> p e f", e=E), w1m.rearrange("e p f -> p e f")).then_inc(S["ld_moe"], 16)
            for e in range(E):
                sp.dma_start(w2s[:, e * FF:(e + 1) * FF].rearrange("p (c o) -> p c o", c=NC),
                             w2m[e].rearrange("(c p) o -> p c o", p=128)).then_inc(S["ld_moe"], 16)
            sp.wait_ge(S["tab_ok"], 2)
            sp.wait_ge(S["pad_out"], 16 * (E + 1))
            sp.wait_ge(scattered[0], 16 * GB * (G // 2))
            sp.wait_ge(scattered[1], 16 * GB * (G // 2))

            def load(j, i, first, t):
                if not first:
                    sp.wait_ge(blk_out[i], 16 * t)
                r = sp.value_load(tab_r[0:1, bass.ds(j, 1)], min_val=0, max_val=E * REG + (E - 1) * BLK)
                sp.dma_start(rin[i][:, :], sorted_rows[bass.ds(r, BLK), :]).then_inc(blk_in[i], 16)

            for i in range(BUF):
                load(i, i, True, 0)
            with sp.Fori(1, NBLK // BUF) as t:
                for i in range(BUF):
                    load(BUF * t + i, i, False, t)
            for i in range(BUF):
                sp.wait_ge(blk_out[i], 16 * (NBLK // BUF))

        @block.gpsimd
        def _(pool):
            pool.memset(mhalf[:, :], -0.5).then_inc(S["consts"], 1)
            pool.memset(v2[:, :, :, HD:HD + 1], 1.0).then_inc(S["consts"], 1)
            pool.memset(ones24[:, :], 1.0).then_inc(S["consts"], 1)
            pool.memset(ones16[:, :], 1.0).then_inc(S["consts"], 1)
            pool.memset(padrow[:, :], 0.0).then_inc(S["consts"], 1)
            pool.wait_ge(S["consts"], 5)
            pool.memset(padrow[:, 2 * D + 1:ROW].bitcast(I32), FAR).then_inc(S["consts"], 1)
            pool.wait_ge(S["consts"], 6)
            pool.dma_start(sorted_rows[E * REG:E * REG + E * BLK, :].rearrange("(k p) c -> p k c", p=BLK),
                           padrow[:, :].unsqueeze(1).to_broadcast([BLK, E, ROW])).then_inc(S["pad_out"], 16)
            pool.iota(order, [[1, EC]], base=1, channel_multiplier=0,
                      allow_small_or_imprecise_dtypes=True).then_inc(S["iota_ok"], 1)
            pool.iota(coff[:, :], [[EC, 8]], base=0, channel_multiplier=0,
                      allow_small_or_imprecise_dtypes=True).then_inc(S["iota_ok"], 1)
            pool.iota(ids[:, :], [[N, B]], base=0, channel_multiplier=1,
                      allow_small_or_imprecise_dtypes=True).then_inc(S["iota_ok"], 1)
            pool.wait_ge(S["iota_ok"], 3)
            pool.wait_ge(S["tok_ok"], 1)

            def rsqrt(k, g, eps):
                wait_apart(pool, mv_ok[k], g + 1)
                pool.tensor_scalar(ve[k][:, :], mv[k][:, :, 1], eps, None, ALU.add).then_inc(ve_ok[k], 1)
                pool.wait_ge(ve_ok[k], g + 1)
                pool.tensor_tensor(rstd[k][:, :], ve[k][:, :], mhalf[:, :], ALU.pow).then_inc(rstd_ok[k], 1)

            def window(t, p):
                w = 2 * t + p
                units = not isinstance(w, int) or 0 <= w < G
                for r in range(R):
                    if units and r in POOL_UNITS:
                        if r == POOL_UNITS[0]:
                            pool.wait_ge(S["q_ok"], w + 1)
                            pool.wait_ge(S["k_ok"], w + 1)
                        if not (isinstance(w, int) and w == 0 and r < RING):
                            pool.wait_ge(S["unit_used"], R * w + r - RING + 1)
                        pool.tensor_tensor(
                            ring[:, r % RING, :].rearrange("p (c b j) -> p c b j", c=4, b=GB),
                            kS[p][:, :].rearrange("p (b j) -> p b j", b=GB).unsqueeze(1).to_broadcast([128, 4, GB, N]),
                            qS[p][:, :].rearrange("p (b c r) -> p c b r", b=GB, c=4)[:, :, :, r].unsqueeze(3)
                            .to_broadcast([128, 4, GB, N]), ALU.add).then_inc(S["sum_pool"], 1)
                    if isinstance(w, int) and w == 0 and r == 15:
                        pool.wait_ge(S["last_ok"], 1)
                        pool.indirect_dma_start(
                            out=at_rows[:, :], out_offset=None, in_=attr,
                            in_offset=bass.IndirectOffsetOnAxis(ap=last_u[:, :], axis=0)).then_inc(S["ld_attr"], 16)
                    for g, gp, gt in due(t, p, r, POOL_AT["gather"]):
                        if not (peeled(g) and g == 0):
                            wait_apart(pool, S["x0_ok"], g)
                        pool.tensor_copy(tok_g[:, :], tok_u[:, bass.ds(GB * g, GB)]).then_inc(S["tok_g_ok"], 1)
                        wait_apart(pool, S["tok_g_ok"], g + 1)
                        for b in range(GB):
                            pool.indirect_dma_start(
                                out=emb_in[:, b, :], out_offset=None, in_=emb,
                                in_offset=bass.IndirectOffsetOnAxis(ap=tok_g[:, b:b + 1], axis=0))\
                                .then_inc(gathered[gp], 16)
                    for g, gp, gt in due(t, p, r, POOL_AT["rsqrt1"]):
                        rsqrt(1, g, EPS_TOK)
                    for g, gp, gt in due(t, p, r, POOL_AT["h"]):
                        pool.wait_ge(S["n2_ok"], g + 1)
                        pool.tensor_tensor(n2g[:, :, :], n2[:, :, :],
                                           Rw("g2").unsqueeze(1).to_broadcast([N, GB, D]), ALU.mult)\
                            .then_inc(S["n2g_ok"], 1)
                        pool.wait_ge(S["n2g_ok"], g + 1)
                        pool.tensor_tensor(h[:, :, :], n2g[:, :, :],
                                           Rw("beta2").unsqueeze(1).to_broadcast([N, GB, D]), ALU.add)\
                            .then_inc(S["h_ok"], 1)
                        pool.wait_ge(S["h_ok"], g + 1)
                        pool.tensor_tensor(hb[gp][:, :, :], h[:, :, :],
                                           Rw("ob").unsqueeze(1).to_broadcast([N, GB, D]), ALU.add)\
                            .then_inc(S["hb_ok"], 1)
                    for g, gp, gt in due(t, p, r, POOL_AT["rsqrt2"]):
                        rsqrt(2, g, EPS_LN)
                    for g, gp, gt in due(t, p, r, POOL_AT["p1n"]):
                        pool.wait_ge(S["rs1_ok"], g + 1)
                        pool.tensor_tensor(p1n[:, :, :], p1[:, :, :],
                                           rs1[:, :].unsqueeze(2).to_broadcast([128, GB, N]), ALU.mult)\
                            .then_inc(S["p1n_ok"], 1)
                    for g, gp, gt in due(t, p, r, POOL_AT["rsqrt0"]):
                        rsqrt(0, g, EPS_TOK)
                    for g, gp, gt in due(t, p, r, POOL_AT["rsqrt3"]):
                        rsqrt(3, g, EPS_LN)
                    for bb in range(GB):
                        for g, gp, gt in due(t, p, r, POOL_AT["kx"][bb]):
                            pool.wait_ge(S["k2_ok"], g + 1)
                            if not (peeled(g) and g == 0):
                                pool.wait_ge(S["s2_ps"], GB * g - GB + bb + 1)
                            pool.tensor_tensor(
                                kx[:, bb, :, :], cols(k2T, bb).unsqueeze(1).to_broadcast([128, H, N]),
                                Bc("hmask").unsqueeze(2).to_broadcast([128, H, N]), ALU.mult).then_inc(S["kx_ok"], 1)
                    for g, gp, gt in due(t, p, r, POOL_AT["bo"]):
                        if peeled(g) and g == 0:
                            pool.wait_ge(S["ld_b"], 16)
                            pool.wait_ge(S["ld_rows"], 16)
                        pool.wait_ge(S["x0_ok"], g + 1)
                        if not (peeled(g) and g < 2):
                            pool.wait_ge(S["r1_ok"], g - 1)
                        pool.tensor_tensor(x0b[gp][:, :, :], x0[:, :, :],
                                           Rw("bo").unsqueeze(1).to_broadcast([N, GB, D]), ALU.add)\
                            .then_inc(S["x0b_ok"], 1)
                    for g, gp, gt in due(t, p, r, POOL_AT["lzero"]):
                        pool.wait_ge(S["chosen"], 5 * g + 1)
                        pool.tensor_tensor(lzero[:, :], lmax[:, :], lmax[:, :], ALU.subtract).then_inc(S["lzero_ok"], 1)
                    for g, gp, gt in due(t, p, r, POOL_AT["scatter"]):
                        pool.wait_ge(S["xf_ok"], g + 1)
                        pool.tensor_copy(row[gp][:, :, 2 * D + 1].bitcast(I32), ids[:, bass.ds(GB * g, GB)])\
                            .then_inc(S["id_ok"], 1)
                        pool.wait_ge(S["pos_ok"], g + 1)
                        pool.wait_ge(S["gate_ok"], g + 1)
                        wait_apart(pool, S["id_ok"], g + 1)
                        for bb in range(GB):
                            pool.indirect_dma_start(
                                out=sorted_rows,
                                out_offset=bass.IndirectOffsetOnAxis(ap=posu[gp][:, bb:bb + 1], axis=0),
                                in_=row[gp][:, bb, :], in_offset=None).then_inc(scattered[gp], 16)

            windows(pool, window)

            pool.wait_ge(S["pad_ok"], 1)
            for e in range(E):
                pool.indirect_dma_start(
                    out=sorted_rows, out_offset=bass.IndirectOffsetOnAxis(ap=padu[:, e:e + 1], axis=0),
                    in_=padrow[:, :], in_offset=None).then_inc(S["pad_out"], 16)

            def store(j, i):
                wait_apart(pool, S["yo_ok"], j + 1)
                pool.indirect_dma_start(
                    out=out_rows, out_offset=bass.IndirectOffsetOnAxis(
                        ap=rin[i][:, 2 * D + 1:ROW].bitcast(U32), axis=0),
                    in_=yout[i][:, :], in_offset=None, bounds_check=B * N - 1, oob_is_err=False)\
                    .then_inc(blk_out[i], 16)

            with pool.Fori(0, NBLK // BUF) as t:
                for i in range(BUF):
                    store(BUF * t + i, i)

        @block.scalar
        def _(act):
            act.wait_ge(S["ld_a"], 16)
            act.wait_ge(S["ld_b"], 16)
            act.wait_ge(S["bias_ok"], 2)

            def window(t, p):
                w = 2 * t + p
                units = not isinstance(w, int) or 0 <= w < G
                for r in range(R):
                    if units:
                        if r in POOL_UNITS:
                            act.wait_ge(S["sum_pool"], NP * w + POOL_UNITS.index(r) + 1)
                        else:
                            act.wait_ge(S["sum_dve"], NV * w + DVE_UNITS.index(r) + 1)
                        act.activation(ring[:, r % RING, :], ring[:, r % RING, :], ACT.Tanh).then_inc(S["tanh_ok"], 1)
                    for g, gp, gt in due(t, p, r, ACT_AT["exp1"]):
                        act.wait_ge(S["nmax_ok"], g + 1)
                        for bb in range(GB):
                            act.activation(p1[:, bb, :], cols(SC, bb), ACT.Exp, bias=nmax[:, bb:bb + 1],
                                           accum_out=sum1[:, bb:bb + 1]).then_inc(S["exp1_ok"], 1)
                    for g, gp, gt in due(t, p, r, ACT_AT["xT"]):
                        act.wait_ge(S["xT_ps"], g + 1)
                        act.activation(xT[:, :], feat(RA1), ACT.Copy).then_inc(S["xT_ok"], 1)
                    for g, gp, gt in due(t, p, r, ACT_AT["qk"]):
                        act.wait_ge(S["q_ps"], g + 1)
                        act.activation(qS[gp][:, :], feat(S0), ACT.Copy).then_inc(S["q_ok"], 1)
                        act.wait_ge(S["k_ps"], g + 1)
                        act.activation(kS[gp][:, :], feat(S1), ACT.Identity, bias=bqk[:, 0:1]).then_inc(S["k_ok"], 1)
                    for g, gp, gt in due(t, p, r, ACT_AT["hnT"]):
                        act.wait_ge(S["hnT_ps"], g + 1)
                        act.activation(hnT[:, :], feat(RA0), ACT.Copy).then_inc(S["hnT_ok"], 1)
                    for g, gp, gt in due(t, p, r, ACT_AT["aT"]):
                        act.wait_ge(S["aT_ps"], g + 1)
                        act.activation(aT[:, :], feat(RA1), ACT.Identity, bias=Bc("bv")).then_inc(S["aT_ok"], 1)
                    for g, gp, gt in due(t, p, r, ACT_AT["q2k2"]):
                        act.wait_ge(S["q2_ps"], g + 1)
                        act.activation(q2T[:, :], feat(S0), ACT.Identity, bias=qb4[:, 0:1], scale=0.25)\
                            .then_inc(S["q2_ok"], 1)
                        act.wait_ge(S["k2_ps"], g + 1)
                        act.activation(k2T[:, :], feat(S1), ACT.Identity, bias=Bc("kb")).then_inc(S["k2_ok"], 1)
                    for g, gp, gt in due(t, p, r, ACT_AT["a2T"]):
                        act.wait_ge(S["a2T_ps"], g + 1)
                        act.activation(a2T[:, :], feat(RB1), ACT.Identity, bias=Bc("vb")).then_inc(S["a2T_ok"], 1)
                    for g, gp, gt in due(t, p, r, ACT_AT["v"]):
                        act.wait_ge(S["v_ps"], g + 1)
                        act.activation(vS[gp][:, :, :], tokv(RA1), ACT.Copy).then_inc(S["v_ok"], 1)
                    for g, gp, gt in due(t, p, r, ACT_AT["v2"]):
                        act.wait_ge(S["v2_ps"], g + 1)
                        act.activation(v2[:, :, :, 0:HD], tokv(S0).rearrange("p b (h d) -> p b h d", h=H), ACT.Copy)\
                            .then_inc(S["v2_ok"], 1)
                    for g, gp, gt in due(t, p, r, ACT_AT["x1T"]):
                        act.wait_ge(S["n1T_ps"], g + 1)
                        act.activation(x1T[:, :], feat(RA1), ACT.Identity, bias=Bc("beta1"), scale=Bc("g1"))\
                            .then_inc(S["x1T_ok"], 1)
                    for half in range(2):
                        for g, gp, gt in due(t, p, r, ACT_AT["relu"][half]):
                            for c in (2 * half, 2 * half + 1):
                                act.wait_ge(S["f1_ps"], NC * g + c + 1)
                                act.activation(hT[:, c, :], feat((RA0, RA1)[c % 2]), ACT.Relu,
                                               bias=Bc("bf1")[:, c:c + 1]).then_inc(S["hT_ok"], 1)
                    for g, gp, gt in due(t, p, r, ACT_AT["xfT"]):
                        act.wait_ge(S["xfT_ps"], g + 1)
                        act.activation(xfT[:, :], feat(RB1), ACT.Copy).then_inc(S["xfT_ok"], 1)
                    for bb in range(GB):
                        for g, gp, gt in due(t, p, r, ACT_AT["p2T"][bb]):
                            act.wait_ge(S["p2T_ps"], GB * g + bb + 1)
                            act.activation(p2T[:, :, :].rearrange("p (u v) m -> p u (v m)", u=2),
                                           rbb[0:N, :, 0:4 * N], ACT.Copy).then_inc(S["p2T_ok"], 1)
                        for g, gp, gt in due(t, p, r, ACT_AT["exp2"][bb]):
                            act.wait_ge(S["p2_ok"], GB * g + bb + 1)
                            act.activation(p2[bb % 2][:, :, :], p2[bb % 2][:, :, :], ACT.Exp).then_inc(S["e2_ok"], 1)
                    for g, gp, gt in due(t, p, r, ACT_AT["gexp"]):
                        act.wait_ge(S["lzero_ok"], g + 1)
                        act.activation(gexp[:, :], lzero[:, :], ACT.Exp).then_inc(S["gexp_ok"], 1)

            windows(act, window)

            act.wait_ge(S["tab_ok"], 2)

            def relu_block(j, i):
                e = act.value_load(tab_e[0:1, bass.ds(j, 1)], min_val=0, max_val=E - 1)
                act.wait_ge(S["htr_ps"], j + 1)
                for c in range(NC):
                    ins = act.activation(hbT[i % 2][:, c, :], bank[i % 2][:, c * BLK:(c + 1) * BLK], ACT.Relu,
                                         bias=Bc("b1")[:, bass.ds(NC * e + c, 1)])
                ins.then_inc(S["hb_relu"], 1)

            with act.Fori(0, NBLK // 4) as t:
                for i in range(4):
                    relu_block(4 * t + i, i)

        @block.tensor
        def _(pe):
            pe.wait_ge(S["ld_a"], 16)
            pe.wait_ge(S["scale_ok"], 1)
            pe.wait_ge(S["upper_ok"], 1)
            pe.wait_ge(S["consts"], 6)
            ident = A("ident")

            def window(t, p):
                w = 2 * t + p
                units = not isinstance(w, int) or 0 <= w < G
                if isinstance(w, int) and w == 0:
                    pe.wait_ge(S["ld_ebw"], 16)
                    pe.wait_ge(S["ld_b"], 16)
                for r in range(R):
                    if units:
                        if r == 0 and not (isinstance(w, int) and w == 0):
                            pe.wait_ge(S["exp1_ok"], GB * w)
                        pe.wait_ge(S["tanh_ok"], R * w + r + 1)
                        for c in range(4):
                            ins = pe.matmul(SC[32 * c:32 * c + 32, 0:GT], scale_win[:, 31 - r:63 - r],
                                            ring[:, r % RING, c * GT:(c + 1) * GT], start=(r == 0), stop=(r == R - 1))
                        ins.then_inc(S["unit_used"], 1)
                    if isinstance(w, int) and w == 0:
                        if r == 18:
                            pe.wait_ge(S["ld_attr"], 16)
                            pe.transpose(RB0[0:3, 0:N], at_rows[:, :], ident[0:N, 0:N]).then_inc(S["edge_at_ps"], 1)
                        if r == 20:
                            pe.wait_ge(S["atT_ok"], 1)
                            pe.matmul(RB1[0:N, 0:H], atT[:, :], ebw_sb[:, :], start=True, stop=True)\
                                .then_inc(S["edge_cb_ps"], 1)
                        if r == 22:
                            pe.wait_ge(S["cb32_ok"], 1)
                            pe.transpose(RB0[0:3 * H, 0:N], cb32[:, :, :].rearrange("p s h -> p (s h)"),
                                         ident[0:N, 0:N]).then_inc(S["edge_cbT_ps"], 1)
                    for g, gp, gt in due(t, p, r, PE_AT["xT"]):
                        pe.wait_ge(S["x0_ok"], g + 1)
                        if not (peeled(g) and g < 3):
                            pe.wait_ge(S["n2_ok"], g - 2)
                        for b in range(GB):
                            ins = pe.transpose(cols(RA1, b), x0[:, b, :], ident[0:N, 0:N])
                        ins.then_inc(S["xT_ps"], 1)
                    for g, gp, gt in due(t, p, r, PE_AT["qk"]):
                        pe.wait_ge(S["xT_ok"], g + 1)
                        if not (peeled(g) and g < 4):
                            pe.wait_ge(S["p2_ok"], GB * (g - 3))
                        pe.matmul(feat(S0), A("wq"), xT[:, :], start=True, stop=True).then_inc(S["q_ps"], 1)
                        pe.matmul(feat(S1), A("wk"), xT[:, :], start=True, stop=True).then_inc(S["k_ps"], 1)
                    for g, gp, gt in due(t, p, r, PE_AT["v"]):
                        if not (peeled(g) and g < 2):
                            pe.wait_ge(S["aT_ok"], g - 1)
                        for b in range(GB):
                            ins = pe.matmul(tokv(RA1)[:, b, :], cols(xT, b), A("wv"), start=True, stop=True)
                        ins.then_inc(S["v_ps"], 1)
                    for g, gp, gt in due(t, p, r, PE_AT["p1T"]):
                        pe.wait_ge(S["p1n_ok"], g + 1)
                        if not (peeled(g) and g < 3):
                            pe.wait_ge(S["cnt_ok"], g - 2)
                        for bb in range(GB):
                            ins = pe.transpose(RA0[0:N, bb * 128:(bb + 1) * 128], p1n[:, bb, :], ident)
                        ins.then_inc(S["p1T_ps"], 1)
                    for g, gp, gt in due(t, p, r, PE_AT["aT"]):
                        pe.wait_ge(S["pT_ok"], g + 1)
                        if peeled(g) and g + 2 >= G:
                            pe.wait_ge(S["n2_ok"], g)
                            pe.wait_ge(S["v_ok"], g + 1)
                        else:
                            pe.wait_ge(S["xT_ok"], g + 3)
                            pe.wait_ge(S["v_ok"], g + 1)
                        for bb in range(GB):
                            ins = pe.matmul(cols(RA1, bb), vS[gp][:, bb, :], pT[:, bb, :], start=True, stop=True)
                        ins.then_inc(S["aT_ps"], 1)
                    for g, gp, gt in due(t, p, r, PE_AT["wo"]):
                        pe.wait_ge(S["aT_ok"], g + 1)
                        if not (peeled(g) and g == 0):
                            pe.wait_ge(S["hnT_ok"], g)
                        for bb in range(GB):
                            ins = pe.matmul(tokv(RA0)[:, bb, :], cols(aT, bb), Bc("wo"), start=True, stop=True)
                        ins.then_inc(S["wo_ps"], 1)
                    for g, gp, gt in due(t, p, r, PE_AT["n1T"]):
                        pe.wait_ge(S["n1_ok"], g + 1)
                        if not (peeled(g) and g + 2 >= G):
                            pe.wait_ge(S["v_ok"], g + 3)
                        for bb in range(GB):
                            ins = pe.transpose(cols(RA1, bb), n1[:, bb, :], ident[0:N, 0:N])
                        ins.then_inc(S["n1T_ps"], 1)
                    for half in range(2):
                        for g, gp, gt in due(t, p, r, PE_AT["f1"][half]):
                            for c in (2 * half, 2 * half + 1):
                                if c == 0:
                                    pe.wait_ge(S["x1T_ok"], g + 1)
                                if c >= 2:
                                    pe.wait_ge(S["hT_ok"], NC * g + c - 1)
                                pe.matmul(feat((RA0, RA1)[c % 2]), Bc("w1")[:, c * D:(c + 1) * D], x1T[:, :],
                                          start=True, stop=True).then_inc(S["f1_ps"], 1)
                    for g, gp, gt in due(t, p, r, PE_AT["f2"]):
                        pe.wait_ge(S["hT_ok"], NC * g + NC)
                        for c in range(NC):
                            ins = pe.matmul(feat(RA0), Bc("w2")[:, c * D:(c + 1) * D], hT[:, c, :],
                                            start=(c == 0), stop=(c == NC - 1))
                        ins.then_inc(S["f2_ps"], 1)
                    for g, gp, gt in due(t, p, r, PE_AT["r2"]):
                        pe.wait_ge(S["r2T_ok"], g + 1)
                        if not (peeled(g) and g < 2):
                            pe.wait_ge(S["lg_ok"], g - 1)
                        for bb in range(GB):
                            ins = pe.transpose(tokv(RA1)[:, bb, :], cols(r2T, bb), ident)
                        ins.then_inc(S["r2_ps"], 1)
                    for g, gp, gt in due(t, p, r, PE_AT["hnT"]):
                        pe.wait_ge(S["hn_ok"], g + 1)
                        if not (peeled(g) and g == G - 1):
                            pe.wait_ge(S["pT_ok"], g + 2)
                        else:
                            pe.wait_ge(S["cnt_ok"], g - 1)
                        for bb in range(GB):
                            ins = pe.transpose(cols(RA0, bb), hn[:, bb, :], ident[0:N, 0:N])
                        ins.then_inc(S["hnT_ps"], 1)
                    for g, gp, gt in due(t, p, r, PE_AT["q2k2"]):
                        pe.wait_ge(S["hnT_ok"], g + 1)
                        if not (peeled(g) and g + 3 >= G):
                            pe.wait_ge(S["k_ok"], g + 4)
                        else:
                            pe.wait_ge(S["p2_ok"], GB * g)
                        pe.matmul(feat(S0), Bc("qw"), hnT[:, :], start=True, stop=True).then_inc(S["q2_ps"], 1)
                        pe.matmul(feat(S1), Bc("kw"), hnT[:, :], start=True, stop=True).then_inc(S["k2_ps"], 1)
                    for g, gp, gt in due(t, p, r, PE_AT["v2"]):
                        pe.wait_ge(S["q2_ok"], g + 1)
                        for bb in range(GB):
                            ins = pe.matmul(tokv(S0)[:, bb, :], cols(hnT, bb), Bc("vw"), start=True, stop=True)
                        ins.then_inc(S["v2_ps"], 1)
                    for bb in range(GB):
                        for g, gp, gt in due(t, p, r, PE_AT["pv"][bb]):
                            pe.wait_ge(S["p2T_ok"], GB * g + bb + 1)
                            for hh in range(H):
                                ins = pe.matmul(RB0[0:N, hh * (HD + 1):(hh + 1) * (HD + 1)], p2T[:, hh, :],
                                                v2[:, bb, hh, :], start=True, stop=True)
                            ins.then_inc(S["pv_ps"], 1)
                        for g, gp, gt in due(t, p, r, PE_AT["s2"][bb]):
                            pe.wait_ge(S["kx_ok"], GB * g + bb + 1)
                            if bb == 0:
                                pe.wait_ge(S["cb_ok"], 1)
                                pe.wait_ge(S["v2_ok"], g + 1)
                            else:
                                pe.wait_ge(S["p2_ok"], GB * g + bb)
                            for u in range(2):
                                pe.matmul(s2b[0:N, u, 0:4 * N], cols(q2T, bb),
                                          kx[:, bb, 4 * u:4 * u + 4, :].rearrange("p h m -> p (h m)"),
                                          start=True, stop=False)
                                ins = pe.matmul(s2b[0:N, u, 0:4 * N], ones24[:, :],
                                                cbx[:, 4 * u:4 * u + 4, :].rearrange("p h m -> p (h m)"),
                                                start=False, stop=True)
                            ins.then_inc(S["s2_ps"], 1)
                        for g, gp, gt in due(t, p, r, PE_AT["p2T"][bb]):
                            pe.wait_ge(S["e2_ok"], GB * g + bb + 1)
                            if bb > 0:
                                pe.wait_ge(S["a2_ok"], GB * g + bb)
                            elif not (peeled(g) and g == 0):
                                pe.wait_ge(S["xfT_ok"], g)
                            for hh in range(H):
                                ins = pe.transpose(rbb[0:N, hh // 4, (hh % 4) * N:(hh % 4 + 1) * N],
                                                   p2[bb % 2][:, hh, :], ident[0:N, 0:N])
                            ins.then_inc(S["p2T_ps"], 1)
                    for g, gp, gt in due(t, p, r, PE_AT["a2T"]):
                        pe.wait_ge(S["a2_ok"], GB * g + GB)
                        for bb in range(GB):
                            ins = pe.transpose(cols(RB1, bb), a2[:, bb, :, :].rearrange("p h d -> p (h d)"),
                                               ident[0:N, 0:N])
                        ins.then_inc(S["a2T_ps"], 1)
                    for g, gp, gt in due(t, p, r, PE_AT["o"]):
                        pe.wait_ge(S["a2T_ok"], g + 1)
                        for bb in range(GB):
                            ins = pe.matmul(tokv(RB0)[:, bb, :], cols(a2T, bb), Bc("ow"), start=True, stop=True)
                        ins.then_inc(S["o_ps"], 1)
                    for g, gp, gt in due(t, p, r, PE_AT["xfT"]):
                        pe.wait_ge(S["xf_ok"], g + 1)
                        for bb in range(GB):
                            ins = pe.transpose(cols(RB1, bb), row[gp][:, bb, D:2 * D], ident[0:N, 0:N])
                        ins.then_inc(S["xfT_ps"], 1)
                    for g, gp, gt in due(t, p, r, PE_AT["lg"]):
                        pe.wait_ge(S["xfT_ok"], g + 1)
                        if not (peeled(g) and g + 2 >= G):
                            pe.wait_ge(S["hT_ok"], NC * g + 3 * NC)
                        else:
                            pe.wait_ge(S["n2_ok"], min(G, g + 2))
                        for bb in range(GB):
                            ins = pe.matmul(RA1[0:N, bb * E:(bb + 1) * E], cols(xfT, bb), Bc("wr"), start=True, stop=True)
                        ins.then_inc(S["lg_ps"], 1)
                    for g, gp, gt in due(t, p, r, PE_AT["rank"]):
                        pe.wait_ge(S["chosen"], 5 * g + 5)
                        if not (peeled(g) and g + 2 >= G):
                            pe.wait_ge(S["r2T_ok"], g + 3)
                        else:
                            pe.wait_ge(S["hnT_ok"], min(G, g + 2))
                        for b in range(GB):
                            pe.matmul(RA0[0:N, b * E:(b + 1) * E], upper16[:, :], oneh[:, b, :], start=True, stop=(b == 0))
                            for c in range(b):
                                pe.matmul(RA0[0:N, b * E:(b + 1) * E], ones16[:, 0:N], oneh[:, c, :], start=False,
                                          stop=(c == b - 1))
                        for b in range(GB):
                            ins = pe.matmul(RA0[:, GB * E:GB * E + E], ones16[:, :], oneh[:, b, :], start=(b == 0),
                                            stop=(b == GB - 1))
                        ins.then_inc(S["rank_ps"], 1)

            windows(pe, window)

            pe.wait_ge(S["tab_ok"], 2)
            pe.wait_ge(S["ld_moe"], 16 * (E + 1))

            def step(j, i, tr, l1, htr, l2, t=None, tr0=False):
                t = j // BUF if t is None else t
                if l1:
                    e1 = pe.value_load(tab_e[0:1, bass.ds(j, 1)], min_val=0, max_val=E - 1)
                if l2:
                    e2 = pe.value_load(tab_e[0:1, bass.ds(j - 2, 1)], min_val=0, max_val=E - 1)
                if tr:
                    n = (i + 1) % BUF
                    pe.wait_ge(blk_in[n], 16 * (t + (1 if i < BUF - 1 else 2)))
                    if not tr0:
                        pe.wait_ge(S["xb_ok"], j + 1)
                    pe.transpose(RB0[:, 0:BLK], rin[n][:, D:2 * D], ident).then_inc(S["tr_ps"], 1)
                if l1:
                    pe.wait_ge(S["xb_ok"], j + 1)
                    if l1 > 1:
                        pe.wait_ge(S["hraw_ok"], j - 1)
                    pe.matmul(s2b[:, i % 2, :], xbT[i % 2][:, :], w1s[:, bass.ds(FF * e1, FF)], start=True, stop=True)\
                        .then_inc(S["l1_ps"], 1)
                if htr:
                    pe.wait_ge(S["hraw_ok"], j)
                    if htr > 1:
                        pe.wait_ge(S["hb_relu"], j - 2)
                    k = (i + 1) % 2
                    for c in range(NC):
                        ins = pe.transpose(bank[k][:, c * BLK:(c + 1) * BLK], hraw[k][:, c * BLK:(c + 1) * BLK], ident)
                    ins.then_inc(S["htr_ps"], 1)
                if l2:
                    k = i % 2
                    pe.wait_ge(S["hb_relu"], j - 1)
                    if l2 > 1:
                        pe.wait_ge(S["ytmp_ok"], j - 3)
                    for c in range(NC):
                        ins = pe.matmul(bank[2 + k][:, 0:D], hbT[k][:, c, :], w2s[:, bass.ds(FF * e2 + c * D, D)],
                                        start=(c == 0), stop=(c == NC - 1))
                    ins.then_inc(S["y_ps"], 1)

            step(-1, BUF - 1, 1, 0, 0, 0, tr0=True)
            step(0, 0, 1, 1, 0, 0)
            step(1, 1, 1, 1, 1, 0)
            step(2, 2, 1, 2, 1, 1)
            step(3, 3, 1, 2, 2, 1)
            for j in range(4, BUF):
                step(j, j, 1, 2, 2, 2)
            with pe.Fori(1, NBLK // BUF - 1) as t:
                for i in range(BUF):
                    step(BUF * t + i, i, 1, 2, 2, 2, t)
            for j in range(NBLK - BUF, NBLK + 2):
                step(j, j % BUF, int(j + 1 < NBLK), 2 if j < NBLK else 0, 2 if j - 1 < NBLK else 0, 2)

        @block.vector
        def _(dve):
            linked = [0]

            def link(ins):
                linked[0] += 1
                ins.then_inc(S["dve_seq"], 1)
                dve.wait_ge(S["dve_seq"], linked[0])

            link(dve.memset(scale_win[:, :], 0.0))
            dve.wait_ge(S["ld_tok"], 16)
            link(dve.tensor_copy(tok_f[:, :], tok_i[:, :]))
            link(dve.tensor_scalar(tok_n[:, :], tok_f[:, :], 0.0, float(VOCAB), ALU.is_lt, ALU.mult))
            link(dve.tensor_tensor(tok_f[:, :], tok_n[:, :], tok_f[:, :], ALU.add))
            dve.tensor_scalar(tok_u[:, :], tok_f[:, :], float(VOCAB - 1), 0.0, ALU.min, ALU.max)\
                .then_inc(S["tok_ok"], 1)
            dve.wait_ge(S["ld_a"], 16)
            dve.tensor_tensor(bqk[:, :], A("bq"), A("bk"), ALU.add).then_inc(S["bias_ok"], 1)
            dve.tensor_copy(scale_win[:, 31:32], A("scale")).then_inc(S["scale_ok"], 1)
            dve.wait_ge(S["ld_b"], 16)
            dve.tensor_scalar(qb4[:, :], Bc("qb"), 0.25, None, ALU.mult).then_inc(S["bias_ok"], 1)
            dve.tensor_copy(upper16[:, :], Bc("upper", N)).then_inc(S["upper_ok"], 1)
            link(dve.tensor_copy(cnt[1][:, :], Bc("base")))

            def stats(k, g, src):
                for b in range(GB):
                    ins = dve.bn_stats(st[k][:, b, :], src[:, b, 0:D])
                ins.then_inc(st_ok[k], 1)

            def means(k):
                for b in range(GB):
                    ins = dve.bn_aggr(mv[k][:, b, :], st[k][:, b, :])
                ins.then_inc(mv_ok[k], 1)

            def edge_keys_in():
                dve.wait_ge(S["ld_edge"], 16)
                link(dve.tensor_copy(key_f[:, :, :], key_e[:, :, :]))
                link(dve.tensor_scalar(key_v[:, :, :], key_f[:, :, :], 0.0, None, ALU.is_ge))
                link(dve.scalar_tensor_tensor(key_w[:, :, :], key_f[:, :, :], float(N), key_v[:, :, :], ALU.is_lt, ALU.mult))
                link(dve.scalar_tensor_tensor(key_1[:, :], key_f[:, 1, :], 1.0, key_w[:, 0, :], ALU.add, ALU.mult))
                link(dve.tensor_tensor(key_v[:, 0, :], key_1[:, :], key_w[:, 1, :], ALU.mult))
                dve.tensor_scalar(key_t[:, :], key_v[:, 0, :], -1.0, None, ALU.add).then_inc(S["key_ok"], 1)

            def edges_in(r):
                if 4 <= r < 12:
                    c = r - 4
                    if c == 0:
                        dve.wait_ge(S["iota_ok"], 2)
                    dve.wait_ge(S["ld_keys"], 16 * (c + 1))
                    link(dve.scalar_tensor_tensor(eprod, ech[c % 2], A("iotap", N), order, ALU.is_equal, ALU.mult))
                    dve.tensor_reduce(cmax[:, c:c + 1], eprod, AX_X, ALU.max).then_inc(S["edge_p"], 1)
                    dve.wait_ge(S["edge_p"], c + 1)
                if r == 13:
                    link(dve.tensor_tensor(cpos[:, :], cmax[:, :], coff[:, :], ALU.add))
                    link(dve.scalar_tensor_tensor(coff[:, :], cmax[:, :], 0.0, cpos[:, :], ALU.is_gt, ALU.mult))
                    link(dve.tensor_reduce(last1[:, :], coff[:, :], AX_X, ALU.max))
                    link(dve.tensor_scalar(hit[:, :], last1[:, :], 0.0, None, ALU.is_gt))
                    dve.tensor_scalar(last_u[:, :], last1[:, :], -1.0, 0.0, ALU.add, ALU.max).then_inc(S["last_ok"], 1)
                if r == 19:
                    dve.wait_ge(S["edge_at_ps"], 1)
                    dve.tensor_copy(atT[:, :], RB0[0:3, 0:N]).then_inc(S["atT_ok"], 1)
                if r == 21:
                    dve.wait_ge(S["edge_cb_ps"], 1)
                    link(dve.tensor_tensor(cbias[:, :], RB1[0:N, 0:H], Rw("ebb"), ALU.add))
                    link(dve.tensor_scalar(cbh[:, :], cbias[:, :], hit[:, 0:1], None, ALU.mult))
                    link(dve.tensor_copy(cb16[:, 0, :], cbh[:, :]))
                    link(dve.tensor_tensor(crem[0][:, :], cbh[:, :], cb16[:, 0, :], ALU.subtract))
                    link(dve.tensor_copy(cb16[:, 1, :], crem[0][:, :]))
                    link(dve.tensor_tensor(crem[1][:, :], crem[0][:, :], cb16[:, 1, :], ALU.subtract))
                    link(dve.tensor_copy(cb16[:, 2, :], crem[1][:, :]))
                    dve.tensor_copy(cb32[:, :, :], cb16[:, :, :]).then_inc(S["cb32_ok"], 1)
                if r == 23:
                    dve.wait_ge(S["edge_cbT_ps"], 1)
                    link(dve.tensor_copy(cbT[:, :], RB0[0:3 * H, 0:N]))
                    dve.tensor_tensor(cbx[:, :, :], cbT[:, :].unsqueeze(1).to_broadcast([3 * H, H, N]),
                                      Bc("mask24", 3 * H).unsqueeze(2).to_broadcast([3 * H, H, N]), ALU.mult)\
                        .then_inc(S["cb_ok"], 1)

            dve.wait_ge(S["ld_rows"], 16)

            def window(t, p):
                w = 2 * t + p
                units = not isinstance(w, int) or 0 <= w < G
                first = isinstance(w, int) and w == 0
                for r in range(R):
                    if units and r == 0:
                        dve.wait_ge(S["q_ok"], w + 1)
                        dve.wait_ge(S["k_ok"], w + 1)
                        if not first:
                            dve.wait_ge(S["sum_dve"], NV * w)
                        dve.tensor_copy(feat(QP), qS[p][:, :]).then_inc(S["qp_ok"], 1)
                        dve.wait_ge(S["qp_ok"], w + 1)
                    for k in range(3):
                        for g, gp, gt in due(t, p, r, DVE_AT["mean"][k]):
                            dve.wait_ge(st_ok[k], g + 1)
                    if units and r in DVE_UNITS:
                        if not (first and r < RING):
                            dve.wait_ge(S["unit_used"], R * w + r - RING + 1)
                        dve.tensor_tensor(
                            ring[:, r % RING, :].rearrange("p (c b j) -> p c b j", c=4, b=GB),
                            kS[p][:, :].rearrange("p (b j) -> p b j", b=GB).unsqueeze(1).to_broadcast([128, 4, GB, N]),
                            feat(QP).rearrange("p (b c r) -> p c b r", b=GB, c=4)[:, :, :, r].unsqueeze(3)
                            .to_broadcast([128, 4, GB, N]), ALU.add).then_inc(S["sum_dve"], 1)
                    if first:
                        edges_in(r)
                    if isinstance(w, int) and w == -1 and r == R - 1:
                        edge_keys_in()
                    for k in range(3):
                        for g, gp, gt in due(t, p, r, DVE_AT["mean"][k]):
                            means(k)
                    for g, gp, gt in due(t, p, r, DVE_AT["x0"]):
                        dve.wait_ge(gathered[gp], 16 * GB * gt + 16 * GB)
                        if not (peeled(g) and g == 0):
                            dve.wait_ge(S["xT_ps"], g)
                            dve.wait_ge(S["x0b_ok"], g)
                        dve.scalar_tensor_tensor(x0[:, :, :], emb_in[:, :, :], float(D) ** 0.5,
                                                 A("pos", N).unsqueeze(1).to_broadcast([N, GB, D]), ALU.mult, ALU.add)\
                            .then_inc(S["x0_ok"], 1)
                    for g, gp, gt in due(t, p, r, DVE_AT["nmax"]):
                        dve.wait_ge(S["unit_used"], R * g + R)
                        dve.tensor_reduce(nmax[:, :], feat(SC).rearrange("p (b j) -> p b j", b=GB), AX_X, ALU.max,
                                          negate=True).then_inc(S["nmax_ok"], 1)
                    for g, gp, gt in due(t, p, r, DVE_AT["rs1"]):
                        dve.wait_ge(S["exp1_ok"], GB * g + GB)
                        dve.reciprocal(rs1[:, :], sum1[:, :]).then_inc(S["rs1_ok"], 1)
                    for g, gp, gt in due(t, p, r, DVE_AT["pT"]):
                        dve.wait_ge(S["p1T_ps"], g + 1)
                        dve.tensor_copy(pT[:, :, :].rearrange("p b (c r) -> p b c r", c=4),
                                        RA0[0:N, :].rearrange("p (b c r) -> p b c r", b=GB, c=4)[:, :, :, 0:R])\
                            .then_inc(S["pT_ok"], 1)
                    for g, gp, gt in due(t, p, r, DVE_AT["r1"]):
                        dve.wait_ge(S["wo_ps"], g + 1)
                        dve.wait_ge(S["x0b_ok"], g + 1)
                        dve.tensor_tensor(r1[:, :, :], tokv(RA0), x0b[gp][:, :, :], ALU.add).then_inc(S["r1_ok"], 1)
                        dve.wait_ge(S["r1_ok"], g + 1)
                        stats(0, g, r1)
                    for g, gp, gt in due(t, p, r, DVE_AT["n1"]):
                        dve.wait_ge(rstd_ok[0], g + 1)
                        for bb in range(GB):
                            ins = dve.tensor_scalar(n1[:, bb, :], r1[:, bb, :], mv[0][:, bb, 0:1],
                                                    rstd[0][:, bb:bb + 1], ALU.subtract, ALU.mult)
                        ins.then_inc(S["n1_ok"], 1)
                    for g, gp, gt in due(t, p, r, DVE_AT["r2T"]):
                        dve.wait_ge(S["f2_ps"], g + 1)
                        dve.scalar_tensor_tensor(r2T[:, :], feat(RA0), Bc("bf2"), x1T[:, :], ALU.add, ALU.add)\
                            .then_inc(S["r2T_ok"], 1)
                    for g, gp, gt in due(t, p, r, DVE_AT["stats1"]):
                        dve.wait_ge(S["r2_ps"], g + 1)
                        stats(1, g, tokv(RA1))
                    for g, gp, gt in due(t, p, r, DVE_AT["n2"]):
                        dve.wait_ge(rstd_ok[1], g + 1)
                        for bb in range(GB):
                            ins = dve.tensor_scalar(n2[:, bb, :], tokv(RA1)[:, bb, :], mv[1][:, bb, 0:1],
                                                    rstd[1][:, bb:bb + 1], ALU.subtract, ALU.mult)
                        ins.then_inc(S["n2_ok"], 1)
                    for g, gp, gt in due(t, p, r, DVE_AT["stats2"]):
                        dve.wait_ge(S["h_ok"], g + 1)
                        stats(2, g, h)
                    for g, gp, gt in due(t, p, r, DVE_AT["hn"]):
                        dve.wait_ge(rstd_ok[2], g + 1)
                        for bb in range(GB):
                            ins = dve.tensor_scalar(hn[:, bb, :], h[:, bb, :], mv[2][:, bb, 0:1],
                                                    rstd[2][:, bb:bb + 1], ALU.subtract, ALU.mult)
                        ins.then_inc(S["hn_ok"], 1)
                    for bb in range(GB):
                        for g, gp, gt in due(t, p, r, DVE_AT["divide"][bb]):
                            n = GB * g + bb + 1
                            o = RB0[0:N, 0:H * (HD + 1)].rearrange("p (h d) -> p h d", h=H)
                            dve.wait_ge(S["pv_ps"], n)
                            dve.reciprocal(rd2[bb % 2][:, :], o[:, :, HD]).then_inc(S["rd2_ok"], 1)
                            dve.wait_ge(S["rd2_ok"], n)
                            dve.tensor_tensor(a2[:, bb, :, :], o[:, :, 0:HD],
                                              rd2[bb % 2][:, :].unsqueeze(2).to_broadcast([N, H, HD]), ALU.mult)\
                                .then_inc(S["a2_ok"], 1)
                        for g, gp, gt in due(t, p, r, DVE_AT["shift"][bb]):
                            n = GB * g + bb + 1
                            s = s2b[0:N, :, 0:4 * N].rearrange("p u (v m) -> p u v m", v=4)
                            dve.wait_ge(S["s2_ps"], n)
                            dve.tensor_reduce(nm2[bb % 2][:, :].rearrange("p (u v) -> p u v", u=2), s, AX_X, ALU.max,
                                              negate=True).then_inc(S["nm2_ok"], 1)
                            dve.wait_ge(S["nm2_ok"], n)
                            dve.tensor_tensor(p2[bb % 2][:, :, :].rearrange("p (u v) m -> p u v m", u=2), s,
                                              nm2[bb % 2][:, :].rearrange("p (u v) -> p u v", u=2).unsqueeze(3)
                                              .to_broadcast([N, 2, 4, N]), ALU.add).then_inc(S["p2_ok"], 1)
                    for g, gp, gt in due(t, p, r, DVE_AT["h2"]):
                        dve.wait_ge(S["o_ps"], g + 1)
                        dve.wait_ge(S["hb_ok"], g + 1)
                        if not (peeled(g) and g < 2):
                            dve.wait_ge(scattered[gp], 16 * GB * gt)
                        dve.tensor_tensor(row[gp][:, :, 0:D], tokv(RB0), hb[gp][:, :, :], ALU.add)\
                            .then_inc(S["h2_ok"], 1)
                        dve.wait_ge(S["h2_ok"], g + 1)
                        stats(3, g, row[gp])
                        wait_apart(dve, st_ok[3], g + 1)
                        means(3)
                    for g, gp, gt in due(t, p, r, DVE_AT["xf"]):
                        dve.wait_ge(rstd_ok[3], g + 1)
                        for bb in range(GB):
                            ins = dve.tensor_scalar(row[gp][:, bb, D:2 * D], row[gp][:, bb, 0:D], mv[3][:, bb, 0:1],
                                                    rstd[3][:, bb:bb + 1], ALU.subtract, ALU.mult)
                        ins.then_inc(S["xf_ok"], 1)
                    for g, gp, gt in due(t, p, r, DVE_AT["place"]):
                        dve.wait_ge(S["rank_ps"], g + 1)
                        dve.tensor_tensor(posv[:, :, :], RA0[0:N, 0:GB * E].rearrange("p (b e) -> p b e", b=GB),
                                          cnt[1 - gp][0:N, :].unsqueeze(1).to_broadcast([N, GB, E]), ALU.add)\
                            .then_inc(S["posv_ok"], 1)
                        dve.tensor_tensor(cnt[gp][:, :], cnt[1 - gp][:, :], RA0[:, GB * E:GB * E + E], ALU.add)\
                            .then_inc(S["cnt_ok"], 1)
                        dve.wait_ge(S["posv_ok"], g + 1)
                        dve.tensor_tensor(posm[:, :, :], posv[:, :, :], oneh[:, :, :], ALU.mult).then_inc(S["placed"], 1)
                        dve.wait_ge(S["gexp_ok"], g + 1)
                        dve.reciprocal(ginv[:, :], gexp[:, :]).then_inc(S["ginv_ok"], 1)
                        dve.wait_ge(S["placed"], 2 * g + 1)
                        dve.tensor_reduce(posf[:, :], posm[:, :, :], AX_X, ALU.add).then_inc(S["placed"], 1)
                        dve.wait_ge(S["placed"], 2 * g + 2)
                        dve.tensor_copy(posu[gp][:, :], posf[:, :]).then_inc(S["pos_ok"], 1)
                        dve.wait_ge(S["ginv_ok"], g + 1)
                        dve.tensor_tensor(row[gp][:, :, 2 * D], gexp[:, :], ginv[:, :], ALU.mult).then_inc(S["gate_ok"], 1)
                        dve.wait_ge(S["cnt_ok"], g + 1)
                    for g, gp, gt in due(t, p, r, DVE_AT["router"]):
                        dve.wait_ge(S["lg_ps"], g + 1)
                        dve.tensor_tensor(lg[:, :, :], RA1[0:N, 0:GB * E].rearrange("p (b e) -> p b e", b=GB),
                                          Rw("br").unsqueeze(1).to_broadcast([N, GB, E]), ALU.add).then_inc(S["lg_ok"], 1)
                        dve.wait_ge(S["lg_ok"], g + 1)
                        dve.tensor_reduce(lmax[:, :], lg[:, :, :], AX_X, ALU.max).then_inc(S["chosen"], 1)
                        dve.wait_ge(S["chosen"], 5 * g + 1)
                        dve.tensor_tensor(eqm[:, :, :], lg[:, :, :], lmax[:, :].unsqueeze(2).to_broadcast([N, GB, E]),
                                          ALU.is_equal).then_inc(S["chosen"], 1)
                        dve.wait_ge(S["chosen"], 5 * g + 2)
                        dve.tensor_tensor(eqw[:, :, :], eqm[:, :, :],
                                          Bc("wtab", N).unsqueeze(1).to_broadcast([N, GB, E]), ALU.mult)\
                            .then_inc(S["chosen"], 1)
                        dve.wait_ge(S["chosen"], 5 * g + 3)
                        dve.tensor_reduce(wsel[:, :], eqw[:, :, :], AX_X, ALU.max).then_inc(S["chosen"], 1)
                        dve.wait_ge(S["chosen"], 5 * g + 4)
                        dve.tensor_tensor(oneh[:, :, :], Bc("wtab", N).unsqueeze(1).to_broadcast([N, GB, E]),
                                          wsel[:, :].unsqueeze(2).to_broadcast([N, GB, E]), ALU.is_equal)\
                            .then_inc(S["chosen"], 1)

            windows(dve, window)

            last = cnt[1]
            KB = B * N // BLK
            link(dve.tensor_scalar(padf[:, :], last[:, :], A("iotap"), None, ALU.add))
            dve.tensor_copy(padu[:, :], padf[:, :]).then_inc(S["pad_ok"], 1)
            link(dve.tensor_tensor(blk_c[:, :], last[0:1, :], Bc("base", 1), ALU.subtract))
            link(dve.tensor_tensor(blk_g[:, :, :], blk_c[:, :].unsqueeze(2).to_broadcast([1, E, KB]),
                                   Bc("k128", 1).unsqueeze(1).to_broadcast([1, E, KB]), ALU.is_gt))
            link(dve.tensor_reduce(blk_n[:, :], blk_g[:, :, :], AX_X, ALU.add))
            link(dve.tensor_copy(blk_end[:, 0:1], blk_n[:, 0:1]))
            for e in range(1, E):
                link(dve.tensor_tensor(blk_end[:, e:e + 1], blk_end[:, e - 1:e], blk_n[:, e:e + 1], ALU.add))
            link(dve.tensor_tensor(blk_ge[:, :, :], Bc("jtab", 1).unsqueeze(2).to_broadcast([1, NBLK, E]),
                                   blk_end[:, :].unsqueeze(1).to_broadcast([1, NBLK, E]), ALU.is_ge))
            link(dve.tensor_reduce(blk_e[:, :], blk_ge[:, :, :], AX_X, ALU.add))
            link(dve.tensor_tensor(blk_gn[:, :, :], blk_ge[:, :, :],
                                   blk_n[:, :].unsqueeze(1).to_broadcast([1, NBLK, E]), ALU.mult))
            link(dve.tensor_reduce(blk_s[:, :], blk_gn[:, :, :], AX_X, ALU.add))
            link(dve.tensor_tensor(blk_t[:, :], Bc("jtab", 1), blk_s[:, :], ALU.subtract))
            link(dve.tensor_scalar(blk_t2[:, :], blk_t[:, :], float(BLK), None, ALU.mult))
            link(dve.scalar_tensor_tensor(blk_s[:, :], blk_e[:, :], float(REG), blk_t2[:, :], ALU.mult, ALU.add))
            link(dve.tensor_scalar(blk_em[:, :], blk_e[:, :], float(E - 1), None, ALU.min))
            dve.tensor_copy(tab_r[:, :], blk_s[:, :]).then_inc(S["tab_ok"], 1)
            dve.tensor_copy(tab_e[:, :], blk_em[:, :]).then_inc(S["tab_ok"], 1)
            dve.wait_ge(S["tab_ok"], 2)

            def step(j, i, xt, hraw_, y):
                if xt:
                    dve.wait_ge(S["tr_ps"], j + 2)
                    dve.tensor_copy(xbT[(i + 1) % 2][:, :], RB0[:, 0:BLK]).then_inc(S["xb_ok"], 1)
                if hraw_:
                    dve.wait_ge(S["l1_ps"], j + 1)
                    if hraw_ > 1:
                        dve.wait_ge(S["htr_ps"], j - 1)
                    dve.tensor_copy(hraw[i % 2][:, :], s2b[:, i % 2, :]).then_inc(S["hraw_ok"], 1)
                if y:
                    k, n = i % 2, (i - 2) % BUF
                    e = dve.value_load(tab_e[0:1, bass.ds(j - 2, 1)], min_val=0, max_val=E - 1)
                    dve.wait_ge(S["y_ps"], j - 1)
                    dve.tensor_tensor(ytmp[k][:, :], bank[2 + k][:, 0:D],
                                      rw[:, bass.ds(D * e + ROWS["b2"][0], D)], ALU.add).then_inc(S["ytmp_ok"], 1)
                    dve.wait_ge(S["ytmp_ok"], j - 1)
                    dve.scalar_tensor_tensor(yout[n][:, :], ytmp[k][:, :], rin[n][:, 2 * D:2 * D + 1], rin[n][:, 0:D],
                                             ALU.mult, ALU.add).then_inc(S["yo_ok"], 1)

            step(-1, BUF - 1, 1, 0, 0)
            step(0, 0, 1, 1, 0)
            step(1, 1, 1, 1, 0)
            for j in range(2, BUF):
                step(j, j, 1, 2, 1)
            with dve.Fori(1, NBLK // BUF - 1) as t:
                for i in range(BUF):
                    step(BUF * t + i, i, 1, 2, 1)
            for j in range(NBLK - BUF, NBLK + 2):
                step(j, j % BUF, int(j + 1 < NBLK), 2 if j < NBLK else 0, 1)


def kernel(**inputs):
    import numpy as np
    import concourse.bacc as _bacc
    from concourse import mybir as _mybir
    from concourse.bass_utils import run_bass_kernel_spmd as _run

    x = {k: np.asarray(v) for k, v in inputs.items()}
    f32 = np.float32

    def columns(v):
        return v.reshape(-1, D).T

    def chunked(wt):
        return wt.reshape(-1, D, wt.shape[1]).transpose(1, 0, 2).reshape(D, -1)

    pos = np.zeros((D, D), f32)
    ang = np.arange(N)[:, None].astype(np.float64) / np.power(
        10000.0, 2 * (np.arange(D)[None, :] // 2) / np.float32(D))
    ang[:, 0::2] = np.sin(ang[:, 0::2])
    ang[:, 1::2] = np.cos(ang[:, 1::2])
    pos[:N] = ang
    p = np.arange(D)
    upper = np.zeros((D, N), f32)
    upper[:N] = np.arange(N)[:, None] < np.arange(N)[None, :]
    mask24 = np.zeros((D, H), f32)
    mask24[:3 * H] = (np.arange(3 * H)[:, None] % H) == np.arange(H)[None, :]

    def rowc(v):
        return np.broadcast_to(np.asarray(v, f32)[None, :], (D, len(v)))

    part_a = {
        "ident": np.eye(D, dtype=f32), "pos": pos, "wq": x["L0_tok_Wq"], "wk": x["L0_tok_Wk"], "wv": x["L0_tok_Wv"],
        "bq": columns(x["L0_tok_bq"]), "bk": columns(x["L0_tok_bk"]), "scale": columns(x["L0_tok_attn_scale"]),
        "iotap": p[:, None].astype(f32)}
    part_b = {
        "wo": x["L0_tok_Wo"], "w1": x["L0_tok_W1"], "w2": chunked(x["L0_tok_W2"]), "qw": x["L0_attn_q_w"].T,
        "kw": x["L0_attn_k_w"].T, "vw": x["L0_attn_v_w"].T, "ow": x["L0_attn_o_w"].T, "wr": x["L0_ffn_Wr"],
        "bv": columns(x["L0_tok_bv"]), "g1": columns(x["L0_tok_g1"]), "beta1": columns(x["L0_tok_beta1"]),
        "bf1": columns(x["L0_tok_bf1"]), "bf2": columns(x["L0_tok_bf2"]), "qb": columns(x["L0_attn_q_b"]),
        "kb": columns(x["L0_attn_k_b"]), "vb": columns(x["L0_attn_v_b"]), "b1": columns(x["L0_ffn_b1"].reshape(-1)),
        "hmask": (p[:, None] // HD == np.arange(H)[None, :]).astype(f32), "mask24": mask24,
        "base": rowc(np.arange(E) * REG), "wtab": rowc(E - np.arange(E)), "upper": upper,
        "jtab": rowc(np.arange(NBLK)),
        "k128": rowc(np.arange(B * N // BLK) * BLK)}
    pack = [np.ascontiguousarray(np.concatenate([part[k] for k in lay if k != "_"], axis=1))
            for part, lay in ((part_a, LAY_A), (part_b, LAY_B))]
    rows = np.concatenate([x["L0_tok_bo"], x["L0_tok_g2"], x["L0_tok_beta2"], x["L0_attn_o_b"], x["L0_ffn_br"],
                           x["L0_attn_eb_b"], x["L0_ffn_b2"].reshape(-1)])[None, :]
    arrays = {
        "tok": np.ascontiguousarray(x["x"].T), "emb": x["L0_tok_emb"], "pack_a": pack[0], "pack_b": pack[1],
        "rows": rows, "edges": x["L0_attn_edge_index"], "attr": x["L0_attn_edge_attr"],
        "ebw": np.ascontiguousarray(x["L0_attn_eb_w"].T), "w1m": x["L0_ffn_W1"], "w2m": x["L0_ffn_W2"]}

    nc = _bacc.Bacc("TRN2", target_bir_lowering=False, num_devices=1)
    args = [nc.dram_tensor(k, a.shape, _mybir.dt.from_np(a.dtype), kind="ExternalInput").ap()
            for k, a in arrays.items()]
    args.append(nc.dram_tensor("out", (B, N, D), F32, kind="ExternalOutput").ap())
    tower(nc, *args)
    r = _run(nc, [arrays], core_ids=[0])
    return r.results[0]["out"]
```

```python
from contextlib import ExitStack

import concourse.bass as bass
from concourse import mybir

F32 = mybir.dt.float32
BF16 = mybir.dt.bfloat16
I32 = mybir.dt.int32
U32 = mybir.dt.uint32
ALU = mybir.AluOpType
ACT = mybir.ActivationFunctionType
AX_X = mybir.AxisListType.X

B, N, D = 64, 96, 128
VOCAB = 8000
FF = 512
NC = FF // D
H, HD = 8, 16
HH = H // 2
E = 8
NE = 8192
GB = 4
G = B // GB
GT = GB * N
R = N // 4
RING = 8
UT = 4 * GT
POOL_UNITS = (1, 3, 6, 8, 11, 13, 16, 18, 21, 23)
DVE_UNITS = tuple(r for r in range(R) if r not in POOL_UNITS)
NP, NV = len(POOL_UNITS), len(DVE_UNITS)
EPS_TOK, EPS_LN = 1e-6, 1e-5
BLK = 128
NBLK = B * N // BLK + E
REG = B * N + BLK
ROW = 2 * D + 2
FAR = 1 << 20
EC = NE // 8

BUF = 8

PE_AT = {"xT": -21, "qk": -19, "v": -15, "p1T": 27, "aT": 28, "wo": 32, "n1T": 36, "f1": (37, 39), "f2": 42, "r2": 43,
         "hnT": 55, "q2k2": 57, "v2": 60, "s2": (61, 63, 67, 71), "p2T": (66, 68, 73, 75), "pv": (67, 71, 74, 76),
         "a2T": 80, "o": 82, "xfT": 87, "lg": 89, "rank": 93}
ACT_AT = {"xT": -19, "qk": -16, "v": -12, "exp1": 25, "aT": 31, "x1T": 37, "relu": (39, 42), "hnT": 56, "q2k2": 60,
          "v2": 62, "exp2": (66, 67, 73, 75), "p2T": (68, 72, 75, 77), "a2T": 82, "xfT": 90, "gexp": 95, "pT": 29}
DVE_AT = {"x0": -19, "nmax": 27, "rs1": 28, "r1": 36, "n1": 39, "r2T": 46, "stats1": 48, "n2": 51, "stats2": 54, "hn":
          58, "mean": (38, 50, 55, 91), "shift": (67, 69, 74, 76), "divide": (73, 76, 77, 82), "h2": 87, "xf": 91,
          "router": 93, "place": 98}
POOL_AT = {"gather": -24, "bo": -8, "p1n": 31, "rsqrt0": 40, "rsqrt1": 53, "h": 55, "rsqrt2": 59, "kx": 64, "rsqrt3":
           91, "lzero": 97, "scatter": 108}
EDGE_AT = {"chunk": (4, 7, 10, 13, 16, 19, 31, 34), "last": 35, "gather": 37, "rows": 40, "rows_out": 45,
           "product": 43, "parts": 48, "turn": 46, "spread": 51}
DEPTH = max(s for table in (PE_AT, ACT_AT, DVE_AT, POOL_AT) for s in table.values() if isinstance(s, int)) // R

LAY_A, LAY_B = {}, {}
for _lay, _items in ((LAY_A, (("ident", D), ("pos", D), ("wq", D), ("wk", D), ("wv", D), ("bq", 1), ("bk", 1),
                              ("scale", 1), ("iotap", 1))),
                     (LAY_B, (("wo", D), ("w1", FF), ("w2", FF), ("qw", D), ("kw", D), ("vw", D), ("ow", D), ("wr", E),
                              ("bv", 1), ("g1", 1), ("beta1", 1), ("bf1", NC), ("bf2", 1), ("qb", 1), ("kb", 1),
                              ("vb", 1), ("b1", E * NC), ("hmask", HH), ("bmask", HH), ("base", E), ("wtab", E),
                              ("upper", N), ("jtab", NBLK), ("k128", B * N // BLK)))):
    _at = 0
    for _name, _n in _items:
        _lay[_name] = (_at, _n)
        _at += _n
    _lay["_"] = (_at, 0)
ROWS = {"bo": (0, D), "g2": (D, D), "beta2": (2 * D, D), "ob": (3 * D, D), "br": (4 * D, E), "ebb": (4 * D + E, H),
        "b2": (4 * D + E + H, E * D)}
ROWS_N = 4 * D + E + H + E * D


def tower(nc, tok, emb, pack_a, pack_b, rows, edges, attr, ebw, w1m, w2m, out):
    out_rows = out.rearrange("b n d -> (b n) d")
    sorted_rows = nc.dram_tensor("sorted_rows", (E * REG + E * BLK, ROW), F32, kind="Internal").ap()
    edge_keys = nc.dram_tensor("edge_keys", (128, NE // 128), F32, kind="Internal").ap()

    with ExitStack() as ctx:
        def sb(name, shape, dt=F32):
            return ctx.enter_context(nc.sbuf_tensor(name, shape, dt))

        def sem(name):
            return ctx.enter_context(nc.semaphore(name))

        ca = sb("pack_a_sb", [128, LAY_A["_"][0]])
        cb = sb("pack_b_sb", [128, LAY_B["_"][0]])
        rw = sb("rows_sb", [128, ROWS_N])

        def A(name, p=128):
            at, n = LAY_A[name]
            return ca[0:p, at:at + n]

        def Bc(name, p=128):
            at, n = LAY_B[name]
            return cb[0:p, at:at + n]

        def Rw(name, p=N):
            at, n = ROWS[name]
            return rw[0:p, at:at + n]

        ring = sb("ring", [128, RING, UT])
        tok_i = sb("tok_i", [N, B], I32)
        tok_f = sb("tok_f", [N, B])
        tok_n = sb("tok_n", [N, B])
        tok_u = sb("tok_u", [N, B], U32)
        tok_g = sb("tok_g", [N, GB], U32)
        bqk = sb("bqk", [128, 1])
        qb4 = sb("qb4", [128, 1])
        scale_win = sb("scale_win", [128, 63])
        emb_in = sb("emb_in", [N, GB, D])
        x0 = sb("x0", [N, GB, D])
        x0b = [sb(f"x0b_{p}", [N, GB, D]) for p in range(2)]
        xT = sb("xT", [128, GT])
        qS = [sb(f"qS_{p}", [128, GT]) for p in range(2)]
        kS = [sb(f"kS_{p}", [128, GT]) for p in range(2)]
        vS = [sb(f"vS_{p}", [N, GB, D]) for p in range(2)]
        nmax = sb("nmax", [128, GB])
        sum1 = sb("sum1", [128, GB])
        rs1 = sb("rs1", [128, GB])
        p1 = sb("p1", [128, GB, N])
        p1n = sb("p1n", [128, GB, N])
        pT = sb("pT", [N, GB, N])
        aT = sb("aT", [128, GT])
        r1 = sb("r1", [N, GB, D])
        st = [sb(f"st{k}", [N, GB, 6]) for k in range(4)]
        mv = [sb(f"mv{k}", [N, GB, 2]) for k in range(4)]
        ve = [sb(f"ve{k}", [N, GB]) for k in range(4)]
        rstd = [sb(f"rstd{k}", [N, GB]) for k in range(4)]
        mhalf = sb("mhalf", [N, GB])
        n1 = sb("n1", [N, GB, D])
        x1T = sb("x1T", [128, GT])
        hT = sb("hT", [128, NC, GT])
        r2T = sb("r2T", [128, GT])
        n2 = sb("n2", [N, GB, D])
        n2g = sb("n2g", [N, GB, D])
        h = [sb(f"h_{p}", [N, GB, D]) for p in range(2)]
        hn = sb("hn", [N, GB, D])
        hnT = sb("hnT", [128, GT])
        q2T = sb("q2T", [128, GT])
        k2T = sb("k2T", [128, GT])
        v2 = sb("v2", [N, GB, H, HD + 1])
        kx = sb("kx", [128, GB, HH, N])
        nm2 = [sb(f"nm2_{i}", [N, H]) for i in range(2)]
        p2 = [sb(f"p2_{i}", [N, H, N]) for i in range(2)]
        p2T = sb("p2T", [N, H, N])
        rd2 = [sb(f"rd2_{i}", [N, H]) for i in range(2)]
        a2 = sb("a2", [N, GB, H, HD])
        a2T = sb("a2T", [128, GT])
        row = [sb(f"row_{p}", [N, GB, ROW]) for p in range(2)]
        xfT = sb("xfT", [128, GT])
        lg = sb("lg", [N, GB, E])
        lmax = sb("lmax", [N, GB])
        lzero = sb("lzero", [N, GB])
        gexp = sb("gexp", [N, GB])
        ginv = sb("ginv", [N, GB])
        eqm = sb("eqm", [N, GB, E])
        eqw = sb("eqw", [N, GB, E])
        wsel = sb("wsel", [N, GB])
        oneh = sb("oneh", [N, GB, E], BF16)
        upper16 = sb("upper16", [N, N], BF16)
        ones16 = sb("ones16", [N, 128], BF16)
        posv = sb("posv", [N, GB, E])
        posm = sb("posm", [N, GB, E])
        posf = sb("posf", [N, GB])
        posu = [sb(f"posu_{p}", [N, GB], U32) for p in range(2)]
        cnt = [sb(f"cnt_{p}", [128, E]) for p in range(2)]
        ids = sb("ids", [N, B])
        key_e = sb("key_e", [128, 2, NE // 128], I32)
        key_f = sb("key_f", [128, 2, NE // 128])
        key_v = sb("key_v", [128, 2, NE // 128])
        key_w = sb("key_w", [128, 2, NE // 128])
        key_t = sb("key_t", [128, NE // 128])
        key_1 = sb("key_1", [128, NE // 128])
        cmax = sb("cmax", [N, 8])
        cpos = sb("cpos", [N, 8])
        coff = sb("coff", [N, 8])
        last1 = sb("last1", [N, 1])
        hit = sb("hit", [N, 1])
        last_f = sb("last_f", [N, 1])
        last_u = sb("last_u", [N, 1], U32)
        at_rows = sb("at_rows", [N, 3])
        atT = sb("atT", [3, N])
        ebw_sb = sb("ebw_sb", [3, H])
        cbias = sb("cbias", [N, H])
        cbh = sb("cbh", [N, H])
        cb16 = sb("cb16", [N, 3, H], BF16)
        cb32 = sb("cb32", [N, 128])
        crem = [sb(f"crem{i}", [N, H]) for i in range(2)]
        cbT = sb("cbT", [128, N])
        cbx = sb("cbx", [128, HH, N], BF16)
        ones1 = sb("ones1", [1, N])
        ones_b = sb("ones_b", [128, N], BF16)
        edge_buf = sb("edge_buf", [N, 3, EC])
        order = hT[0:N, :, :].rearrange("p c t -> p (c t)")[:, 0:EC]
        ech = [edge_buf[:, i, :] for i in range(2)]
        eprod = edge_buf[:, 2, :]
        w1s = ring[:, 0:RING // 2, :].rearrange("p a n -> p (a n)")[:, 0:E * FF]
        w2s = ring[:, RING // 2:RING, :].rearrange("p a n -> p (a n)")[:, 0:E * FF]
        padrow = sb("padrow", [BLK, ROW])
        padf = sb("padf", [BLK, E])
        padu = sb("padu", [BLK, E], U32)
        blk_n = sb("blk_n", [1, E])
        blk_g = sb("blk_g", [1, E, B * N // BLK])
        blk_c = sb("blk_c", [1, E])
        blk_end = sb("blk_end", [1, E])
        blk_ge = sb("blk_ge", [1, NBLK, E])
        blk_gn = sb("blk_gn", [1, NBLK, E])
        blk_e = sb("blk_e", [1, NBLK])
        blk_s = sb("blk_s", [1, NBLK])
        blk_t = sb("blk_t", [1, NBLK])
        blk_t2 = sb("blk_t2", [1, NBLK])
        blk_em = sb("blk_em", [1, NBLK])
        tab_e = sb("tab_e", [1, NBLK], I32)
        tab_r = sb("tab_r", [1, NBLK], I32)
        tab_p = sb("tab_p", [1, E], I32)
        rin = [sb(f"rin{i}", [BLK, ROW]) for i in range(BUF)]
        yout = [sb(f"yout{i}", [BLK, D]) for i in range(BUF)]
        xbT = [sb(f"xbT{i}", [128, BLK]) for i in range(2)]
        w1b = [sb(f"w1b{i}", [D, FF]) for i in range(2)]
        hbT = [sb(f"hbT{i}", [128, NC, BLK]) for i in range(2)]
        ytmp = [sb(f"ytmp{i}", [BLK, D]) for i in range(2)]

        bank = [ctx.enter_context(nc.psum_tensor(f"bank{i}", [128, 512], F32)) for i in range(4)]
        s2b = ctx.enter_context(nc.psum_tensor("s2_banks", [128, 2, 512], F32))
        rbb = ctx.enter_context(nc.psum_tensor("rb_banks", [128, 2, 512], F32))
        QP, SC, RA0, RA1 = bank
        RB0, RB1 = rbb[:, 0, :], rbb[:, 1, :]
        S0, S1 = s2b[:, 0, :], s2b[:, 1, :]

        def feat(b):
            return b[:, 0:GT]

        def tokv(b):
            return b[0:N, :].rearrange("p (b d) -> p b d", b=GB)

        def cols(t, b):
            return t[:, b * N:(b + 1) * N]

        names = """ld_a ld_b ld_rows ld_tok ld_edge ld_ebw ld_keys ld_attr key_out ld_moe
            consts tok_ok tok_g_ok x0_ok xT_ps xT_ok q_ps q_ok k_ps k_ok v_ps v_ok x0b_ok
            qp_ok sum_dve sum_pool tanh_ok unit_used
            nmax_ok exp1_ok rs1_ok p1n_ok p1T_ps pT_ok aT_ps aT_ok wo_ps r1_ok n1_ok n1T_ps x1T_ok
            f1_ps hT_ok f2_ps r2T_ok r2_ps n2_ok n2g_ok h_ok hn_ok hnT_ps hnT_ok
            q2_ps q2_ok k2_ps k2_ok v2_ps v2_ok kx_ok s2_ps nm2_ok p2_ok e2_ok p2T_ps p2T_ok pv_ps
            rd2_ok a2_ok a2T_ps a2T_ok o_ps h2_ok xf_ok xfT_ps xfT_ok lg_ps lg_ok chosen lzero_ok gexp_ok ginv_ok
            gate_ok rank_ps posv_ok placed pos_ok cnt_ok
            id_ok
            passed dve_seq bias_ok scale_ok upper_ok init_ok key_ok edge_p last_ok edge_at_ps atT_ok edge_cb_ps cb32_ok
            edge_cbT_ps cb_ok iota_ok pad_ok pad_out pad_out_sp tab_ok
            tr_ps xb_ok l1_ps  hb_relu y_ps ytmp_ok yo_ok"""
        S = {n: sem(n) for n in names.split()}
        st_ok = [sem(f"st{k}_ok") for k in range(4)]
        mv_ok = [sem(f"mv{k}_ok") for k in range(4)]
        ve_ok = [sem(f"ve{k}_ok") for k in range(4)]
        rstd_ok = [sem(f"rstd{k}_ok") for k in range(4)]
        gathered = [sem(f"gathered_{p}") for p in range(2)]
        scattered = [sem(f"scattered_{p}") for p in range(2)]
        blk_in = [sem(f"blk_in{i}") for i in range(BUF)]
        blk_out = [sem(f"blk_out{i}") for i in range(BUF)]

        block = ctx.enter_context(nc.Block())

        def wait_apart(eng, s, value):
            eng.wait_ge(s, value)
            eng.sem_inc(S["passed"], 1)

        def windows(eng, window):
            window(-1, 1)
            for t in range(3):
                window(t, 0)
                window(t, 1)
            with eng.Fori(3, G // 2 - 1) as t:
                window(t, 0)
                window(t, 1)
            for w in range(G - 2, G + DEPTH):
                window(w // 2, w % 2)

        def due(t, p, r, slot):
            if slot % R != r:
                return ()
            k = slot // R
            gp = (p - k) % 2
            gt = t + (p - k - gp) // 2
            g = 2 * t + (p - k)
            if isinstance(t, int) and not 0 <= g < G:
                return ()
            return ((g, gp, gt),)

        def peeled(g):
            return isinstance(g, int)

        @block.sync
        def _(sp):
            sp.dma_start(tok_i[:, :], tok).then_inc(S["ld_tok"], 16)
            sp.dma_start(ca[:, :], pack_a).then_inc(S["ld_a"], 16)
            sp.dma_start(key_e[:, :, :], edges.rearrange("s (p f) -> p s f", p=128)).then_inc(S["ld_edge"], 16)
            sp.dma_start(cb[:, :], pack_b).then_inc(S["ld_b"], 16)
            sp.dma_start(rw[:, :], rows.to_broadcast([128, ROWS_N])).then_inc(S["ld_rows"], 16)
            sp.dma_start(ebw_sb[:, :], ebw).then_inc(S["ld_ebw"], 16)
            sp.wait_ge(S["key_ok"], 1)
            sp.dma_start(edge_keys, key_t[:, :]).then_inc(S["key_out"], 16)
            sp.wait_ge(S["key_out"], 16)
            flat = edge_keys.rearrange("p f -> (p f)").rearrange("(a n) -> a n", a=8)
            for c in range(8):
                if c >= 2:
                    sp.wait_ge(S["edge_p"], c - 1)
                sp.dma_start(ech[c % 2], flat[c:c + 1, :].to_broadcast([N, EC])).then_inc(S["ld_keys"], 16)
                sp.wait_ge(S["ld_keys"], 16 * (c + 1))
            sp.wait_ge(S["unit_used"], R * G)
            sp.dma_start(w1s.rearrange("p (e f) -> p e f", e=E), w1m.rearrange("e p f -> p e f")).then_inc(S["ld_moe"], 16)
            for e in range(E):
                sp.dma_start(w2s[:, e * FF:(e + 1) * FF].rearrange("p (c o) -> p c o", c=NC),
                             w2m[e].rearrange("(c p) o -> p c o", p=128)).then_inc(S["ld_moe"], 16)
            sp.wait_ge(S["pad_ok"], 1)
            for e in range(E // 2, E):
                r = sp.value_load(tab_p[0:1, e:e + 1], min_val=0, max_val=E * REG)
                sp.dma_start(sorted_rows[bass.ds(r, BLK), :], padrow[:, :]).then_inc(S["pad_out_sp"], 16)
            sp.wait_ge(S["tab_ok"], 2)
            sp.wait_ge(S["pad_out"], 16 * (E // 2 + 1))
            sp.wait_ge(S["pad_out_sp"], 16 * (E // 2))
            sp.wait_ge(scattered[0], 16 * GB * (G // 2))
            sp.wait_ge(scattered[1], 16 * GB * (G // 2))

            def load(j, i, first, t):
                if not first:
                    sp.wait_ge(blk_out[i], 16 * t)
                r = sp.value_load(tab_r[0:1, bass.ds(j, 1)], min_val=0, max_val=E * REG + (E - 1) * BLK)
                sp.dma_start(rin[i][:, :], sorted_rows[bass.ds(r, BLK), :]).then_inc(blk_in[i], 16)

            for i in range(BUF):
                load(i, i, True, 0)
            with sp.Fori(1, NBLK // BUF) as t:
                for i in range(BUF):
                    load(BUF * t + i, i, False, t)
            for i in range(BUF):
                sp.wait_ge(blk_out[i], 16 * (NBLK // BUF))

        @block.gpsimd
        def _(pool):
            pool.memset(mhalf[:, :], -0.5).then_inc(S["consts"], 1)
            pool.memset(v2[:, :, :, HD:HD + 1], 1.0).then_inc(S["consts"], 1)
            pool.memset(ones_b[:, :], 1.0).then_inc(S["consts"], 1)
            pool.memset(ones1[:, :], 1.0).then_inc(S["consts"], 1)
            pool.memset(ones16[:, :], 1.0).then_inc(S["consts"], 1)
            pool.memset(padrow[:, :], 0.0).then_inc(S["consts"], 1)
            pool.wait_ge(S["consts"], 6)
            pool.memset(padrow[:, 2 * D + 1:ROW].bitcast(I32), FAR).then_inc(S["consts"], 1)
            pool.wait_ge(S["consts"], 7)
            pool.dma_start(sorted_rows[E * REG:E * REG + E * BLK, :].rearrange("(k p) c -> p k c", p=BLK),
                           padrow[:, :].unsqueeze(1).to_broadcast([BLK, E, ROW])).then_inc(S["pad_out"], 16)
            pool.iota(order, [[1, EC]], base=1, channel_multiplier=0,
                      allow_small_or_imprecise_dtypes=True).then_inc(S["iota_ok"], 1)
            pool.iota(coff[:, :], [[EC, 8]], base=0, channel_multiplier=0,
                      allow_small_or_imprecise_dtypes=True).then_inc(S["iota_ok"], 1)
            pool.iota(ids[:, :], [[N, B]], base=0, channel_multiplier=1,
                      allow_small_or_imprecise_dtypes=True).then_inc(S["iota_ok"], 1)
            pool.wait_ge(S["iota_ok"], 3)
            pool.wait_ge(S["tok_ok"], 1)

            def rsqrt(k, g, eps):
                wait_apart(pool, mv_ok[k], g + 1)
                pool.tensor_scalar(ve[k][:, :], mv[k][:, :, 1], eps, None, ALU.add).then_inc(ve_ok[k], 1)
                pool.wait_ge(ve_ok[k], g + 1)
                pool.tensor_tensor(rstd[k][:, :], ve[k][:, :], mhalf[:, :], ALU.pow).then_inc(rstd_ok[k], 1)

            def window(t, p):
                w = 2 * t + p
                units = not isinstance(w, int) or 0 <= w < G
                for r in range(R):
                    if units and r in POOL_UNITS:
                        if r == POOL_UNITS[0]:
                            pool.wait_ge(S["q_ok"], w + 1)
                            pool.wait_ge(S["k_ok"], w + 1)
                        if not (isinstance(w, int) and w == 0 and r < RING):
                            pool.wait_ge(S["unit_used"], R * w + r - RING + 1)
                        pool.tensor_tensor(
                            ring[:, r % RING, :].rearrange("p (c b j) -> p c b j", c=4, b=GB),
                            kS[p][:, :].rearrange("p (b j) -> p b j", b=GB).unsqueeze(1).to_broadcast([128, 4, GB, N]),
                            qS[p][:, :].rearrange("p (b c r) -> p c b r", b=GB, c=4)[:, :, :, r].unsqueeze(3)
                            .to_broadcast([128, 4, GB, N]), ALU.add).then_inc(S["sum_pool"], 1)
                    if isinstance(w, int) and R * w + r == EDGE_AT["gather"]:
                        pool.wait_ge(S["last_ok"], 1)
                        pool.indirect_dma_start(
                            out=at_rows[:, :], out_offset=None, in_=attr,
                            in_offset=bass.IndirectOffsetOnAxis(ap=last_u[:, :], axis=0)).then_inc(S["ld_attr"], 16)
                    for g, gp, gt in due(t, p, r, POOL_AT["gather"]):
                        if not (peeled(g) and g == 0):
                            wait_apart(pool, S["x0_ok"], g)
                        pool.tensor_copy(tok_g[:, :], tok_u[:, bass.ds(GB * g, GB)]).then_inc(S["tok_g_ok"], 1)
                        wait_apart(pool, S["tok_g_ok"], g + 1)
                        for b in range(GB):
                            pool.indirect_dma_start(
                                out=emb_in[:, b, :], out_offset=None, in_=emb,
                                in_offset=bass.IndirectOffsetOnAxis(ap=tok_g[:, b:b + 1], axis=0))\
                                .then_inc(gathered[gp], 16)
                    for g, gp, gt in due(t, p, r, POOL_AT["rsqrt1"]):
                        rsqrt(1, g, EPS_TOK)
                    for g, gp, gt in due(t, p, r, POOL_AT["h"]):
                        pool.wait_ge(S["n2_ok"], g + 1)
                        pool.tensor_tensor(n2g[:, :, :], n2[:, :, :],
                                           Rw("g2").unsqueeze(1).to_broadcast([N, GB, D]), ALU.mult)\
                            .then_inc(S["n2g_ok"], 1)
                        pool.wait_ge(S["n2g_ok"], g + 1)
                        pool.tensor_tensor(h[gp][:, :, :], n2g[:, :, :],
                                           Rw("beta2").unsqueeze(1).to_broadcast([N, GB, D]), ALU.add)\
                            .then_inc(S["h_ok"], 1)
                    for g, gp, gt in due(t, p, r, POOL_AT["rsqrt2"]):
                        rsqrt(2, g, EPS_LN)
                    for g, gp, gt in due(t, p, r, POOL_AT["p1n"]):
                        pool.wait_ge(S["rs1_ok"], g + 1)
                        pool.tensor_tensor(p1n[:, :, :], p1[:, :, :],
                                           rs1[:, :].unsqueeze(2).to_broadcast([128, GB, N]), ALU.mult)\
                            .then_inc(S["p1n_ok"], 1)
                    for g, gp, gt in due(t, p, r, POOL_AT["rsqrt0"]):
                        rsqrt(0, g, EPS_TOK)
                    for g, gp, gt in due(t, p, r, POOL_AT["rsqrt3"]):
                        rsqrt(3, g, EPS_LN)
                    for g, gp, gt in due(t, p, r, POOL_AT["kx"]):
                        pool.wait_ge(S["k2_ok"], g + 1)
                        if not (peeled(g) and g == 0):
                            pool.wait_ge(S["s2_ps"], GB * g)
                        pool.tensor_tensor(
                            kx[:, :, :, :],
                            k2T[:, :].rearrange("p (b m) -> p b m", b=GB).unsqueeze(2).to_broadcast([128, GB, HH, N]),
                            Bc("hmask").unsqueeze(1).unsqueeze(3).to_broadcast([128, GB, HH, N]), ALU.mult)\
                            .then_inc(S["kx_ok"], 1)
                    for g, gp, gt in due(t, p, r, POOL_AT["bo"]):
                        if peeled(g) and g == 0:
                            pool.wait_ge(S["ld_b"], 16)
                            pool.wait_ge(S["ld_rows"], 16)
                        pool.wait_ge(S["x0_ok"], g + 1)
                        if not (peeled(g) and g < 2):
                            pool.wait_ge(S["r1_ok"], g - 1)
                        pool.tensor_tensor(x0b[gp][:, :, :], x0[:, :, :],
                                           Rw("bo").unsqueeze(1).to_broadcast([N, GB, D]), ALU.add)\
                            .then_inc(S["x0b_ok"], 1)
                    for g, gp, gt in due(t, p, r, POOL_AT["lzero"]):
                        pool.wait_ge(S["chosen"], 5 * g + 1)
                        pool.tensor_tensor(lzero[:, :], lmax[:, :], lmax[:, :], ALU.subtract).then_inc(S["lzero_ok"], 1)
                    for g, gp, gt in due(t, p, r, POOL_AT["scatter"]):
                        pool.wait_ge(S["xf_ok"], g + 1)
                        pool.tensor_copy(row[gp][:, :, 2 * D + 1].bitcast(I32), ids[:, bass.ds(GB * g, GB)])\
                            .then_inc(S["id_ok"], 1)
                        pool.wait_ge(S["pos_ok"], g + 1)
                        pool.wait_ge(S["gate_ok"], g + 1)
                        wait_apart(pool, S["id_ok"], g + 1)
                        for bb in range(GB):
                            pool.indirect_dma_start(
                                out=sorted_rows,
                                out_offset=bass.IndirectOffsetOnAxis(ap=posu[gp][:, bb:bb + 1], axis=0),
                                in_=row[gp][:, bb, :], in_offset=None).then_inc(scattered[gp], 16)

            windows(pool, window)

            pool.wait_ge(S["pad_ok"], 1)
            for e in range(E // 2):
                pool.indirect_dma_start(
                    out=sorted_rows, out_offset=bass.IndirectOffsetOnAxis(ap=padu[:, e:e + 1], axis=0),
                    in_=padrow[:, :], in_offset=None).then_inc(S["pad_out"], 16)

            def store(j, i):
                wait_apart(pool, S["yo_ok"], j + 1)
                pool.indirect_dma_start(
                    out=out_rows, out_offset=bass.IndirectOffsetOnAxis(
                        ap=rin[i][:, 2 * D + 1:ROW].bitcast(U32), axis=0),
                    in_=yout[i][:, :], in_offset=None, bounds_check=B * N - 1, oob_is_err=False)\
                    .then_inc(blk_out[i], 16)

            with pool.Fori(0, NBLK // BUF) as t:
                for i in range(BUF):
                    store(BUF * t + i, i)

        @block.scalar
        def _(act):
            act.wait_ge(S["ld_a"], 16)
            act.wait_ge(S["ld_b"], 16)
            act.wait_ge(S["bias_ok"], 2)

            def window(t, p):
                w = 2 * t + p
                units = not isinstance(w, int) or 0 <= w < G
                for r in range(R):
                    if units:
                        if r in POOL_UNITS:
                            act.wait_ge(S["sum_pool"], NP * w + POOL_UNITS.index(r) + 1)
                        else:
                            act.wait_ge(S["sum_dve"], NV * w + DVE_UNITS.index(r) + 1)
                        act.activation(ring[:, r % RING, :], ring[:, r % RING, :], ACT.Tanh).then_inc(S["tanh_ok"], 1)
                    for g, gp, gt in due(t, p, r, ACT_AT["exp1"]):
                        act.wait_ge(S["nmax_ok"], g + 1)
                        for bb in range(GB):
                            act.activation(p1[:, bb, :], cols(SC, bb), ACT.Exp, bias=nmax[:, bb:bb + 1],
                                           accum_out=sum1[:, bb:bb + 1]).then_inc(S["exp1_ok"], 1)
                    for g, gp, gt in due(t, p, r, ACT_AT["pT"]):
                        act.wait_ge(S["p1T_ps"], g + 1)
                        act.activation(pT[:, :, :].rearrange("p b (c r) -> p b c r", c=4),
                                       RA0[0:N, :].rearrange("p (b c r) -> p b c r", b=GB, c=4)[:, :, :, 0:R],
                                       ACT.Copy).then_inc(S["pT_ok"], 1)
                    for g, gp, gt in due(t, p, r, ACT_AT["xT"]):
                        act.wait_ge(S["xT_ps"], g + 1)
                        act.activation(xT[:, :], feat(RA1), ACT.Copy).then_inc(S["xT_ok"], 1)
                    for g, gp, gt in due(t, p, r, ACT_AT["qk"]):
                        act.wait_ge(S["q_ps"], g + 1)
                        act.activation(qS[gp][:, :], feat(S0), ACT.Copy).then_inc(S["q_ok"], 1)
                        act.wait_ge(S["k_ps"], g + 1)
                        act.activation(kS[gp][:, :], feat(S1), ACT.Identity, bias=bqk[:, 0:1]).then_inc(S["k_ok"], 1)
                    for g, gp, gt in due(t, p, r, ACT_AT["hnT"]):
                        act.wait_ge(S["hnT_ps"], g + 1)
                        act.activation(hnT[:, :], feat(RA0), ACT.Copy).then_inc(S["hnT_ok"], 1)
                    for g, gp, gt in due(t, p, r, ACT_AT["aT"]):
                        act.wait_ge(S["aT_ps"], g + 1)
                        act.activation(aT[:, :], feat(RA1), ACT.Identity, bias=Bc("bv")).then_inc(S["aT_ok"], 1)
                    for g, gp, gt in due(t, p, r, ACT_AT["q2k2"]):
                        act.wait_ge(S["q2_ps"], g + 1)
                        act.activation(q2T[:, :], feat(S0), ACT.Identity, bias=qb4[:, 0:1], scale=0.25)\
                            .then_inc(S["q2_ok"], 1)
                        act.wait_ge(S["k2_ps"], g + 1)
                        act.activation(k2T[:, :], feat(S1), ACT.Identity, bias=Bc("kb")).then_inc(S["k2_ok"], 1)
                    for g, gp, gt in due(t, p, r, ACT_AT["a2T"]):
                        act.wait_ge(S["a2T_ps"], g + 1)
                        act.activation(a2T[:, :], feat(RB1), ACT.Identity, bias=Bc("vb")).then_inc(S["a2T_ok"], 1)
                    for g, gp, gt in due(t, p, r, ACT_AT["v"]):
                        act.wait_ge(S["v_ps"], g + 1)
                        act.activation(vS[gp][:, :, :], tokv(RA1), ACT.Copy).then_inc(S["v_ok"], 1)
                    for g, gp, gt in due(t, p, r, ACT_AT["v2"]):
                        act.wait_ge(S["v2_ps"], g + 1)
                        act.activation(v2[:, :, :, 0:HD], tokv(S0).rearrange("p b (h d) -> p b h d", h=H), ACT.Copy)\
                            .then_inc(S["v2_ok"], 1)
                    for g, gp, gt in due(t, p, r, ACT_AT["x1T"]):
                        act.wait_ge(S["n1T_ps"], g + 1)
                        act.activation(x1T[:, :], feat(RA1), ACT.Identity, bias=Bc("beta1"), scale=Bc("g1"))\
                            .then_inc(S["x1T_ok"], 1)
                    for half in range(2):
                        for g, gp, gt in due(t, p, r, ACT_AT["relu"][half]):
                            for c in (2 * half, 2 * half + 1):
                                act.wait_ge(S["f1_ps"], NC * g + c + 1)
                                act.activation(hT[:, c, :], feat((RA0, RA1)[c % 2]), ACT.Relu,
                                               bias=Bc("bf1")[:, c:c + 1]).then_inc(S["hT_ok"], 1)
                    for g, gp, gt in due(t, p, r, ACT_AT["xfT"]):
                        act.wait_ge(S["xfT_ps"], g + 1)
                        act.activation(xfT[:, :], feat(RB1), ACT.Copy).then_inc(S["xfT_ok"], 1)
                    for bb in range(GB):
                        for g, gp, gt in due(t, p, r, ACT_AT["p2T"][bb]):
                            act.wait_ge(S["p2T_ps"], GB * g + bb + 1)
                            act.activation(p2T[:, :, :].rearrange("p (u v) m -> p u (v m)", u=2),
                                           rbb[0:N, :, 0:4 * N], ACT.Copy).then_inc(S["p2T_ok"], 1)
                        for g, gp, gt in due(t, p, r, ACT_AT["exp2"][bb]):
                            act.wait_ge(S["p2_ok"], GB * g + bb + 1)
                            act.activation(p2[bb % 2][:, :, :], p2[bb % 2][:, :, :], ACT.Exp).then_inc(S["e2_ok"], 1)
                    for g, gp, gt in due(t, p, r, ACT_AT["gexp"]):
                        act.wait_ge(S["lzero_ok"], g + 1)
                        act.activation(gexp[:, :], lzero[:, :], ACT.Exp).then_inc(S["gexp_ok"], 1)

            windows(act, window)

            act.wait_ge(S["tab_ok"], 2)

            def relu_block(j, i):
                e = act.value_load(tab_e[0:1, bass.ds(j, 1)], min_val=0, max_val=E - 1)
                act.wait_ge(S["l1_ps"], j + 1)
                for c in range(NC):
                    ins = act.activation(hbT[i % 2][:, c, :], bank[i % 2][:, c * BLK:(c + 1) * BLK], ACT.Relu,
                                         bias=Bc("b1")[:, bass.ds(NC * e + c, 1)])
                ins.then_inc(S["hb_relu"], 1)

            with act.Fori(0, NBLK // 4) as t:
                for i in range(4):
                    relu_block(4 * t + i, i)

        @block.tensor
        def _(pe):
            pe.wait_ge(S["ld_a"], 16)
            pe.wait_ge(S["scale_ok"], 1)
            pe.wait_ge(S["upper_ok"], 1)
            pe.wait_ge(S["consts"], 7)
            ident = A("ident")

            def window(t, p):
                w = 2 * t + p
                units = not isinstance(w, int) or 0 <= w < G
                if isinstance(w, int) and w == 0:
                    pe.wait_ge(S["ld_ebw"], 16)
                    pe.wait_ge(S["ld_b"], 16)
                    pe.wait_ge(S["ld_rows"], 16)
                for r in range(R):
                    if units:
                        if r == 0 and not (isinstance(w, int) and w == 0):
                            pe.wait_ge(S["exp1_ok"], GB * w)
                        pe.wait_ge(S["tanh_ok"], R * w + r + 1)
                        for c in range(4):
                            ins = pe.matmul(SC[32 * c:32 * c + 32, 0:GT], scale_win[:, 31 - r:63 - r],
                                            ring[:, r % RING, c * GT:(c + 1) * GT], start=(r == 0), stop=(r == R - 1))
                        ins.then_inc(S["unit_used"], 1)
                    if isinstance(w, int) and 1 <= w < 3:
                        if R * w + r == EDGE_AT["rows"]:
                            pe.wait_ge(S["ld_attr"], 16)
                            pe.transpose(RB0[0:3, 0:N], at_rows[:, :], ident[0:N, 0:N]).then_inc(S["edge_at_ps"], 1)
                        if R * w + r == EDGE_AT["product"]:
                            pe.wait_ge(S["atT_ok"], 1)
                            pe.matmul(RB1[0:N, 0:H], atT[:, :], ebw_sb[:, :], start=True, stop=True)\
                                .then_inc(S["edge_cb_ps"], 1)
                        if R * w + r == EDGE_AT["turn"]:
                            pe.wait_ge(S["cb32_ok"], 2)
                            pe.transpose(RB0[:, 0:N], cb32[:, :], ident[0:N, 0:N]).then_inc(S["edge_cbT_ps"], 1)
                    for g, gp, gt in due(t, p, r, PE_AT["xT"]):
                        pe.wait_ge(S["x0_ok"], g + 1)
                        if not (peeled(g) and g < 3):
                            pe.wait_ge(S["n2_ok"], g - 2)
                        for b in range(GB):
                            ins = pe.transpose(cols(RA1, b), x0[:, b, :], ident[0:N, 0:N])
                        ins.then_inc(S["xT_ps"], 1)
                    for g, gp, gt in due(t, p, r, PE_AT["qk"]):
                        pe.wait_ge(S["xT_ok"], g + 1)
                        if not (peeled(g) and g < 4):
                            pe.wait_ge(S["p2_ok"], GB * (g - 3))
                        pe.matmul(feat(S0), A("wq"), xT[:, :], start=True, stop=True).then_inc(S["q_ps"], 1)
                        pe.matmul(feat(S1), A("wk"), xT[:, :], start=True, stop=True).then_inc(S["k_ps"], 1)
                    for g, gp, gt in due(t, p, r, PE_AT["v"]):
                        if not (peeled(g) and g < 2):
                            pe.wait_ge(S["aT_ok"], g - 1)
                        for b in range(GB):
                            ins = pe.matmul(tokv(RA1)[:, b, :], cols(xT, b), A("wv"), start=True, stop=True)
                        ins.then_inc(S["v_ps"], 1)
                    for g, gp, gt in due(t, p, r, PE_AT["p1T"]):
                        pe.wait_ge(S["p1n_ok"], g + 1)
                        if not (peeled(g) and g < 3):
                            pe.wait_ge(S["cnt_ok"], g - 2)
                        for bb in range(GB):
                            ins = pe.transpose(RA0[0:N, bb * 128:(bb + 1) * 128], p1n[:, bb, :], ident)
                        ins.then_inc(S["p1T_ps"], 1)
                    for g, gp, gt in due(t, p, r, PE_AT["aT"]):
                        pe.wait_ge(S["pT_ok"], g + 1)
                        if peeled(g) and g + 2 >= G:
                            pe.wait_ge(S["n2_ok"], g)
                            pe.wait_ge(S["v_ok"], g + 1)
                        else:
                            pe.wait_ge(S["xT_ok"], g + 3)
                            pe.wait_ge(S["v_ok"], g + 1)
                        for bb in range(GB):
                            ins = pe.matmul(cols(RA1, bb), vS[gp][:, bb, :], pT[:, bb, :], start=True, stop=True)
                        ins.then_inc(S["aT_ps"], 1)
                    for g, gp, gt in due(t, p, r, PE_AT["wo"]):
                        pe.wait_ge(S["aT_ok"], g + 1)
                        if not (peeled(g) and g == 0):
                            pe.wait_ge(S["hnT_ok"], g)
                        for bb in range(GB):
                            ins = pe.matmul(tokv(RA0)[:, bb, :], cols(aT, bb), Bc("wo"), start=True, stop=True)
                        ins.then_inc(S["wo_ps"], 1)
                    for g, gp, gt in due(t, p, r, PE_AT["n1T"]):
                        pe.wait_ge(S["n1_ok"], g + 1)
                        if not (peeled(g) and g + 2 >= G):
                            pe.wait_ge(S["v_ok"], g + 3)
                        for bb in range(GB):
                            ins = pe.transpose(cols(RA1, bb), n1[:, bb, :], ident[0:N, 0:N])
                        ins.then_inc(S["n1T_ps"], 1)
                    for half in range(2):
                        for g, gp, gt in due(t, p, r, PE_AT["f1"][half]):
                            for c in (2 * half, 2 * half + 1):
                                if c == 0:
                                    pe.wait_ge(S["x1T_ok"], g + 1)
                                if c >= 2:
                                    pe.wait_ge(S["hT_ok"], NC * g + c - 1)
                                pe.matmul(feat((RA0, RA1)[c % 2]), Bc("w1")[:, c * D:(c + 1) * D], x1T[:, :],
                                          start=True, stop=True).then_inc(S["f1_ps"], 1)
                    for g, gp, gt in due(t, p, r, PE_AT["f2"]):
                        pe.wait_ge(S["hT_ok"], NC * g + NC)
                        for c in range(NC):
                            ins = pe.matmul(feat(RA0), Bc("w2")[:, c * D:(c + 1) * D], hT[:, c, :],
                                            start=(c == 0), stop=(c == NC - 1))
                        ins.then_inc(S["f2_ps"], 1)
                    for g, gp, gt in due(t, p, r, PE_AT["r2"]):
                        pe.wait_ge(S["r2T_ok"], g + 1)
                        if not (peeled(g) and g < 2):
                            pe.wait_ge(S["lg_ok"], g - 1)
                        for bb in range(GB):
                            ins = pe.transpose(tokv(RA1)[:, bb, :], cols(r2T, bb), ident)
                        ins.then_inc(S["r2_ps"], 1)
                    for g, gp, gt in due(t, p, r, PE_AT["hnT"]):
                        pe.wait_ge(S["hn_ok"], g + 1)
                        if not (peeled(g) and g == G - 1):
                            pe.wait_ge(S["pT_ok"], g + 2)
                        else:
                            pe.wait_ge(S["cnt_ok"], g - 1)
                        for bb in range(GB):
                            ins = pe.transpose(cols(RA0, bb), hn[:, bb, :], ident[0:N, 0:N])
                        ins.then_inc(S["hnT_ps"], 1)
                    for g, gp, gt in due(t, p, r, PE_AT["q2k2"]):
                        pe.wait_ge(S["hnT_ok"], g + 1)
                        if not (peeled(g) and g + 3 >= G):
                            pe.wait_ge(S["k_ok"], g + 4)
                        else:
                            pe.wait_ge(S["p2_ok"], GB * g)
                        pe.matmul(feat(S0), Bc("qw"), hnT[:, :], start=True, stop=True).then_inc(S["q2_ps"], 1)
                        pe.matmul(feat(S1), Bc("kw"), hnT[:, :], start=True, stop=True).then_inc(S["k2_ps"], 1)
                    for g, gp, gt in due(t, p, r, PE_AT["v2"]):
                        pe.wait_ge(S["q2_ok"], g + 1)
                        for bb in range(GB):
                            ins = pe.matmul(tokv(S0)[:, bb, :], cols(hnT, bb), Bc("vw"), start=True, stop=True)
                        ins.then_inc(S["v2_ps"], 1)
                    for bb in range(GB):
                        for g, gp, gt in due(t, p, r, PE_AT["pv"][bb]):
                            pe.wait_ge(S["p2T_ok"], GB * g + bb + 1)
                            for hh in range(H):
                                ins = pe.matmul(RB0[0:N, hh * (HD + 1):(hh + 1) * (HD + 1)], p2T[:, hh, :],
                                                v2[:, bb, hh, :], start=True, stop=True)
                            ins.then_inc(S["pv_ps"], 1)
                        for g, gp, gt in due(t, p, r, PE_AT["s2"][bb]):
                            if bb == 0:
                                pe.wait_ge(S["kx_ok"], g + 1)
                                pe.wait_ge(S["cb_ok"], 1)
                                pe.wait_ge(S["v2_ok"], g + 1)
                            else:
                                pe.wait_ge(S["p2_ok"], GB * g + bb)
                            for u in range(2):
                                half = slice(64 * u, 64 * u + 64)
                                pe.matmul(s2b[0:N, u, 0:4 * N], q2T[half, bb * N:(bb + 1) * N],
                                          kx[half, bb, :, :].rearrange("p h m -> p (h m)"), start=True, stop=False)
                                ins = pe.matmul(s2b[0:N, u, 0:4 * N], ones_b[half, :],
                                                cbx[half, :, :].rearrange("p h m -> p (h m)"), start=False, stop=True)
                            ins.then_inc(S["s2_ps"], 1)
                        for g, gp, gt in due(t, p, r, PE_AT["p2T"][bb]):
                            pe.wait_ge(S["e2_ok"], GB * g + bb + 1)
                            if bb > 0:
                                pe.wait_ge(S["a2_ok"], GB * g + bb)
                            elif not (peeled(g) and g == 0):
                                pe.wait_ge(S["xfT_ok"], g)
                            for hh in range(H):
                                ins = pe.transpose(rbb[0:N, hh // 4, (hh % 4) * N:(hh % 4 + 1) * N],
                                                   p2[bb % 2][:, hh, :], ident[0:N, 0:N])
                            ins.then_inc(S["p2T_ps"], 1)
                    for g, gp, gt in due(t, p, r, PE_AT["a2T"]):
                        pe.wait_ge(S["a2_ok"], GB * g + GB)
                        for bb in range(GB):
                            ins = pe.transpose(cols(RB1, bb), a2[:, bb, :, :].rearrange("p h d -> p (h d)"),
                                               ident[0:N, 0:N])
                        ins.then_inc(S["a2T_ps"], 1)
                    for g, gp, gt in due(t, p, r, PE_AT["o"]):
                        pe.wait_ge(S["a2T_ok"], g + 1)
                        for bb in range(GB):
                            pe.matmul(tokv(RB0)[:, bb, :], cols(a2T, bb), Bc("ow"), start=True, stop=False)
                            ins = pe.matmul(tokv(RB0)[:, bb, :], ones1[:, :], Rw("ob", 1), start=False, stop=True)
                        ins.then_inc(S["o_ps"], 1)
                    for g, gp, gt in due(t, p, r, PE_AT["xfT"]):
                        pe.wait_ge(S["xf_ok"], g + 1)
                        for bb in range(GB):
                            ins = pe.transpose(cols(RB1, bb), row[gp][:, bb, D:2 * D], ident[0:N, 0:N])
                        ins.then_inc(S["xfT_ps"], 1)
                    for g, gp, gt in due(t, p, r, PE_AT["lg"]):
                        pe.wait_ge(S["xfT_ok"], g + 1)
                        if not (peeled(g) and g + 2 >= G):
                            pe.wait_ge(S["hT_ok"], NC * g + 3 * NC)
                        else:
                            pe.wait_ge(S["n2_ok"], min(G, g + 2))
                        for bb in range(GB):
                            ins = pe.matmul(RA1[0:N, bb * E:(bb + 1) * E], cols(xfT, bb), Bc("wr"), start=True, stop=True)
                        ins.then_inc(S["lg_ps"], 1)
                    for g, gp, gt in due(t, p, r, PE_AT["rank"]):
                        pe.wait_ge(S["chosen"], 5 * g + 5)
                        if not (peeled(g) and g + 2 >= G):
                            pe.wait_ge(S["r2T_ok"], g + 3)
                        else:
                            pe.wait_ge(S["hnT_ok"], min(G, g + 2))
                        for b in range(GB):
                            pe.matmul(RA0[0:N, b * E:(b + 1) * E], upper16[:, :], oneh[:, b, :], start=True, stop=(b == 0))
                            for c in range(b):
                                pe.matmul(RA0[0:N, b * E:(b + 1) * E], ones16[:, 0:N], oneh[:, c, :], start=False,
                                          stop=(c == b - 1))
                        for b in range(GB):
                            ins = pe.matmul(RA0[:, GB * E:GB * E + E], ones16[:, :], oneh[:, b, :], start=(b == 0),
                                            stop=(b == GB - 1))
                        ins.then_inc(S["rank_ps"], 1)

            windows(pe, window)

            pe.wait_ge(S["tab_ok"], 2)
            pe.wait_ge(S["ld_moe"], 16 * (E + 1))

            def step(j, i, tr, l1, l2, t=None, tr0=False):
                t = j // BUF if t is None else t
                if l2:
                    e2 = pe.value_load(tab_e[0:1, bass.ds(j - 2, 1)], min_val=0, max_val=E - 1)
                if tr:
                    n = (i + 1) % BUF
                    pe.wait_ge(blk_in[n], 16 * (t + (1 if i < BUF - 1 else 2)))
                    if not tr0:
                        pe.wait_ge(S["xb_ok"], j + 1)
                    pe.transpose(RB0[:, 0:BLK], rin[n][:, D:2 * D], ident).then_inc(S["tr_ps"], 1)
                if l2:
                    k = i % 2
                    pe.wait_ge(S["hb_relu"], j - 1)
                    if l2 > 1:
                        pe.wait_ge(S["ytmp_ok"], j - 3)
                    for c in range(NC):
                        ins = pe.matmul(bank[2 + k][:, 0:D], hbT[k][:, c, :], w2s[:, bass.ds(FF * e2 + c * D, D)],
                                        start=(c == 0), stop=(c == NC - 1))
                    ins.then_inc(S["y_ps"], 1)
                if l1:
                    pe.wait_ge(S["xb_ok"], j + 1)
                    for c in range(NC):
                        ins = pe.matmul(bank[i % 2][:, c * BLK:(c + 1) * BLK], w1b[i % 2][:, c * D:(c + 1) * D],
                                        xbT[i % 2][:, :], start=True, stop=True)
                    ins.then_inc(S["l1_ps"], 1)

            step(-1, BUF - 1, 1, 0, 0, tr0=True)
            step(0, 0, 1, 1, 0)
            step(1, 1, 1, 1, 0)
            step(2, 2, 1, 1, 1)
            step(3, 3, 1, 1, 1)
            for j in range(4, BUF):
                step(j, j, 1, 1, 2)
            with pe.Fori(1, NBLK // BUF - 1) as t:
                for i in range(BUF):
                    step(BUF * t + i, i, 1, 1, 2, t)
            for j in range(NBLK - BUF, NBLK + 2):
                step(j, j % BUF, int(j + 1 < NBLK), int(j < NBLK), 2)

        @block.vector
        def _(dve):
            linked = [0]

            def link(ins):
                linked[0] += 1
                ins.then_inc(S["dve_seq"], 1)
                dve.wait_ge(S["dve_seq"], linked[0])

            link(dve.memset(scale_win[:, :], 0.0))
            dve.wait_ge(S["ld_tok"], 16)
            link(dve.tensor_copy(tok_f[:, :], tok_i[:, :]))
            link(dve.tensor_scalar(tok_n[:, :], tok_f[:, :], 0.0, float(VOCAB), ALU.is_lt, ALU.mult))
            link(dve.tensor_tensor(tok_f[:, :], tok_n[:, :], tok_f[:, :], ALU.add))
            dve.tensor_scalar(tok_u[:, :], tok_f[:, :], float(VOCAB - 1), 0.0, ALU.min, ALU.max)\
                .then_inc(S["tok_ok"], 1)
            dve.wait_ge(S["ld_a"], 16)
            dve.tensor_tensor(bqk[:, :], A("bq"), A("bk"), ALU.add).then_inc(S["bias_ok"], 1)
            dve.tensor_copy(scale_win[:, 31:32], A("scale")).then_inc(S["scale_ok"], 1)
            dve.wait_ge(S["ld_b"], 16)
            dve.tensor_scalar(qb4[:, :], Bc("qb"), 0.25, None, ALU.mult).then_inc(S["bias_ok"], 1)
            dve.tensor_copy(upper16[:, :], Bc("upper", N)).then_inc(S["upper_ok"], 1)
            link(dve.tensor_copy(cnt[1][:, :], Bc("base")))

            def stats(k, g, src):
                for b in range(GB):
                    ins = dve.bn_stats(st[k][:, b, :], src[:, b, 0:D])
                ins.then_inc(st_ok[k], 1)

            def means(k):
                for b in range(GB):
                    ins = dve.bn_aggr(mv[k][:, b, :], st[k][:, b, :])
                ins.then_inc(mv_ok[k], 1)

            def edge_keys_in():
                dve.wait_ge(S["ld_edge"], 16)
                link(dve.tensor_copy(key_f[:, :, :], key_e[:, :, :]))
                link(dve.tensor_scalar(key_v[:, :, :], key_f[:, :, :], 0.0, None, ALU.is_ge))
                link(dve.scalar_tensor_tensor(key_w[:, :, :], key_f[:, :, :], float(N), key_v[:, :, :], ALU.is_lt, ALU.mult))
                link(dve.scalar_tensor_tensor(key_1[:, :], key_f[:, 1, :], 1.0, key_w[:, 0, :], ALU.add, ALU.mult))
                link(dve.tensor_tensor(key_v[:, 0, :], key_1[:, :], key_w[:, 1, :], ALU.mult))
                dve.tensor_scalar(key_t[:, :], key_v[:, 0, :], -1.0, None, ALU.add).then_inc(S["key_ok"], 1)

            def edges_in(r):
                if r in EDGE_AT["chunk"]:
                    c = EDGE_AT["chunk"].index(r)
                    if c == 0:
                        dve.wait_ge(S["iota_ok"], 2)
                    dve.wait_ge(S["ld_keys"], 16 * (c + 1))
                    link(dve.scalar_tensor_tensor(eprod, ech[c % 2], A("iotap", N), order, ALU.is_equal, ALU.mult))
                    dve.tensor_reduce(cmax[:, c:c + 1], eprod, AX_X, ALU.max).then_inc(S["edge_p"], 1)
                    dve.wait_ge(S["edge_p"], c + 1)
                if r == EDGE_AT["last"]:
                    link(dve.tensor_tensor(cpos[:, :], cmax[:, :], coff[:, :], ALU.add))
                    link(dve.scalar_tensor_tensor(coff[:, :], cmax[:, :], 0.0, cpos[:, :], ALU.is_gt, ALU.mult))
                    link(dve.tensor_reduce(last1[:, :], coff[:, :], AX_X, ALU.max))
                    link(dve.tensor_scalar(hit[:, :], last1[:, :], 0.0, None, ALU.is_gt))
                    dve.tensor_scalar(last_u[:, :], last1[:, :], -1.0, 0.0, ALU.add, ALU.max).then_inc(S["last_ok"], 1)
                if r == EDGE_AT["rows_out"]:
                    dve.wait_ge(S["edge_at_ps"], 1)
                    dve.tensor_copy(atT[:, :], RB0[0:3, 0:N]).then_inc(S["atT_ok"], 1)
                if r == EDGE_AT["parts"]:
                    dve.wait_ge(S["edge_cb_ps"], 1)
                    link(dve.tensor_tensor(cbias[:, :], RB1[0:N, 0:H], Rw("ebb"), ALU.add))
                    link(dve.tensor_scalar(cbh[:, :], cbias[:, :], hit[:, 0:1], None, ALU.mult))
                    link(dve.tensor_copy(cb16[:, 0, :], cbh[:, :]))
                    link(dve.tensor_tensor(crem[0][:, :], cbh[:, :], cb16[:, 0, :], ALU.subtract))
                    link(dve.tensor_copy(cb16[:, 1, :], crem[0][:, :]))
                    link(dve.tensor_tensor(crem[1][:, :], crem[0][:, :], cb16[:, 1, :], ALU.subtract))
                    link(dve.tensor_copy(cb16[:, 2, :], crem[1][:, :]))
                    link(dve.memset(cb32[:, :], 0.0))
                    for u in range(2):
                        dve.tensor_copy(cb32[:, 64 * u:64 * u + 3 * H], cb16[:, :, :].rearrange("p s h -> p (s h)"))\
                            .then_inc(S["cb32_ok"], 1)
                if r == EDGE_AT["spread"]:
                    dve.wait_ge(S["edge_cbT_ps"], 1)
                    link(dve.tensor_copy(cbT[:, :], RB0[:, 0:N]))
                    dve.tensor_tensor(cbx[:, :, :], cbT[:, :].unsqueeze(1).to_broadcast([128, HH, N]),
                                      Bc("bmask").unsqueeze(2).to_broadcast([128, HH, N]), ALU.mult)\
                        .then_inc(S["cb_ok"], 1)

            dve.wait_ge(S["ld_rows"], 16)

            def window(t, p):
                w = 2 * t + p
                units = not isinstance(w, int) or 0 <= w < G
                first = isinstance(w, int) and w == 0
                for r in range(R):
                    if units and r == 0:
                        dve.wait_ge(S["q_ok"], w + 1)
                        dve.wait_ge(S["k_ok"], w + 1)
                        if not first:
                            dve.wait_ge(S["sum_dve"], NV * w)
                        dve.tensor_copy(feat(QP), qS[p][:, :]).then_inc(S["qp_ok"], 1)
                        dve.wait_ge(S["qp_ok"], w + 1)
                    for k in range(4):
                        for g, gp, gt in due(t, p, r, DVE_AT["mean"][k]):
                            dve.wait_ge(st_ok[k], g + 1)
                    if units and r in DVE_UNITS:
                        if not (first and r < RING):
                            dve.wait_ge(S["unit_used"], R * w + r - RING + 1)
                        dve.tensor_tensor(
                            ring[:, r % RING, :].rearrange("p (c b j) -> p c b j", c=4, b=GB),
                            kS[p][:, :].rearrange("p (b j) -> p b j", b=GB).unsqueeze(1).to_broadcast([128, 4, GB, N]),
                            feat(QP).rearrange("p (b c r) -> p c b r", b=GB, c=4)[:, :, :, r].unsqueeze(3)
                            .to_broadcast([128, 4, GB, N]), ALU.add).then_inc(S["sum_dve"], 1)
                    if isinstance(w, int) and 0 <= w < 3:
                        edges_in(R * w + r)
                    if isinstance(w, int) and w == -1 and r == R - 1:
                        edge_keys_in()
                    for k in range(4):
                        for g, gp, gt in due(t, p, r, DVE_AT["mean"][k]):
                            means(k)
                    for g, gp, gt in due(t, p, r, DVE_AT["x0"]):
                        dve.wait_ge(gathered[gp], 16 * GB * gt + 16 * GB)
                        if not (peeled(g) and g == 0):
                            dve.wait_ge(S["xT_ps"], g)
                            dve.wait_ge(S["x0b_ok"], g)
                        dve.scalar_tensor_tensor(x0[:, :, :], emb_in[:, :, :], float(D) ** 0.5,
                                                 A("pos", N).unsqueeze(1).to_broadcast([N, GB, D]), ALU.mult, ALU.add)\
                            .then_inc(S["x0_ok"], 1)
                    for g, gp, gt in due(t, p, r, DVE_AT["nmax"]):
                        dve.wait_ge(S["unit_used"], R * g + R)
                        dve.tensor_reduce(nmax[:, :], feat(SC).rearrange("p (b j) -> p b j", b=GB), AX_X, ALU.max,
                                          negate=True).then_inc(S["nmax_ok"], 1)
                    for g, gp, gt in due(t, p, r, DVE_AT["rs1"]):
                        dve.wait_ge(S["exp1_ok"], GB * g + GB)
                        dve.reciprocal(rs1[:, :], sum1[:, :]).then_inc(S["rs1_ok"], 1)
                    for g, gp, gt in due(t, p, r, DVE_AT["r1"]):
                        dve.wait_ge(S["wo_ps"], g + 1)
                        dve.wait_ge(S["x0b_ok"], g + 1)
                        dve.tensor_tensor(r1[:, :, :], tokv(RA0), x0b[gp][:, :, :], ALU.add).then_inc(S["r1_ok"], 1)
                        dve.wait_ge(S["r1_ok"], g + 1)
                        stats(0, g, r1)
                    for g, gp, gt in due(t, p, r, DVE_AT["n1"]):
                        dve.wait_ge(rstd_ok[0], g + 1)
                        for bb in range(GB):
                            ins = dve.tensor_scalar(n1[:, bb, :], r1[:, bb, :], mv[0][:, bb, 0:1],
                                                    rstd[0][:, bb:bb + 1], ALU.subtract, ALU.mult)
                        ins.then_inc(S["n1_ok"], 1)
                    for g, gp, gt in due(t, p, r, DVE_AT["r2T"]):
                        dve.wait_ge(S["f2_ps"], g + 1)
                        dve.scalar_tensor_tensor(r2T[:, :], feat(RA0), Bc("bf2"), x1T[:, :], ALU.add, ALU.add)\
                            .then_inc(S["r2T_ok"], 1)
                    for g, gp, gt in due(t, p, r, DVE_AT["stats1"]):
                        dve.wait_ge(S["r2_ps"], g + 1)
                        stats(1, g, tokv(RA1))
                    for g, gp, gt in due(t, p, r, DVE_AT["n2"]):
                        dve.wait_ge(rstd_ok[1], g + 1)
                        for bb in range(GB):
                            ins = dve.tensor_scalar(n2[:, bb, :], tokv(RA1)[:, bb, :], mv[1][:, bb, 0:1],
                                                    rstd[1][:, bb:bb + 1], ALU.subtract, ALU.mult)
                        ins.then_inc(S["n2_ok"], 1)
                    for g, gp, gt in due(t, p, r, DVE_AT["stats2"]):
                        dve.wait_ge(S["h_ok"], g + 1)
                        stats(2, g, h[gp])
                    for g, gp, gt in due(t, p, r, DVE_AT["hn"]):
                        dve.wait_ge(rstd_ok[2], g + 1)
                        for bb in range(GB):
                            ins = dve.tensor_scalar(hn[:, bb, :], h[gp][:, bb, :], mv[2][:, bb, 0:1],
                                                    rstd[2][:, bb:bb + 1], ALU.subtract, ALU.mult)
                        ins.then_inc(S["hn_ok"], 1)
                    for bb in range(GB):
                        for g, gp, gt in due(t, p, r, DVE_AT["divide"][bb]):
                            n = GB * g + bb + 1
                            o = RB0[0:N, 0:H * (HD + 1)].rearrange("p (h d) -> p h d", h=H)
                            dve.wait_ge(S["pv_ps"], n)
                            dve.reciprocal(rd2[bb % 2][:, :], o[:, :, HD]).then_inc(S["rd2_ok"], 1)
                            dve.wait_ge(S["rd2_ok"], n)
                            dve.tensor_tensor(a2[:, bb, :, :], o[:, :, 0:HD],
                                              rd2[bb % 2][:, :].unsqueeze(2).to_broadcast([N, H, HD]), ALU.mult)\
                                .then_inc(S["a2_ok"], 1)
                        for g, gp, gt in due(t, p, r, DVE_AT["shift"][bb]):
                            n = GB * g + bb + 1
                            s = s2b[0:N, :, 0:4 * N].rearrange("p u (v m) -> p u v m", v=4)
                            dve.wait_ge(S["s2_ps"], n)
                            dve.tensor_reduce(nm2[bb % 2][:, :].rearrange("p (u v) -> p u v", u=2), s, AX_X, ALU.max,
                                              negate=True).then_inc(S["nm2_ok"], 1)
                            dve.wait_ge(S["nm2_ok"], n)
                            dve.tensor_tensor(p2[bb % 2][:, :, :].rearrange("p (u v) m -> p u v m", u=2), s,
                                              nm2[bb % 2][:, :].rearrange("p (u v) -> p u v", u=2).unsqueeze(3)
                                              .to_broadcast([N, 2, 4, N]), ALU.add).then_inc(S["p2_ok"], 1)
                    for g, gp, gt in due(t, p, r, DVE_AT["h2"]):
                        dve.wait_ge(S["o_ps"], g + 1)
                        if not (peeled(g) and g < 2):
                            dve.wait_ge(scattered[gp], 16 * GB * gt)
                        dve.tensor_tensor(row[gp][:, :, 0:D], tokv(RB0), h[gp][:, :, :], ALU.add)\
                            .then_inc(S["h2_ok"], 1)
                        dve.wait_ge(S["h2_ok"], g + 1)
                        stats(3, g, row[gp])
                    for g, gp, gt in due(t, p, r, DVE_AT["xf"]):
                        dve.wait_ge(rstd_ok[3], g + 1)
                        for bb in range(GB):
                            ins = dve.tensor_scalar(row[gp][:, bb, D:2 * D], row[gp][:, bb, 0:D], mv[3][:, bb, 0:1],
                                                    rstd[3][:, bb:bb + 1], ALU.subtract, ALU.mult)
                        ins.then_inc(S["xf_ok"], 1)
                    for g, gp, gt in due(t, p, r, DVE_AT["place"]):
                        dve.wait_ge(S["rank_ps"], g + 1)
                        dve.tensor_tensor(posv[:, :, :], RA0[0:N, 0:GB * E].rearrange("p (b e) -> p b e", b=GB),
                                          cnt[1 - gp][0:N, :].unsqueeze(1).to_broadcast([N, GB, E]), ALU.add)\
                            .then_inc(S["posv_ok"], 1)
                        dve.tensor_tensor(cnt[gp][:, :], cnt[1 - gp][:, :], RA0[:, GB * E:GB * E + E], ALU.add)\
                            .then_inc(S["cnt_ok"], 1)
                        dve.wait_ge(S["posv_ok"], g + 1)
                        dve.tensor_tensor(posm[:, :, :], posv[:, :, :], oneh[:, :, :], ALU.mult).then_inc(S["placed"], 1)
                        dve.wait_ge(S["gexp_ok"], g + 1)
                        dve.reciprocal(ginv[:, :], gexp[:, :]).then_inc(S["ginv_ok"], 1)
                        dve.wait_ge(S["placed"], 2 * g + 1)
                        dve.tensor_reduce(posf[:, :], posm[:, :, :], AX_X, ALU.add).then_inc(S["placed"], 1)
                        dve.wait_ge(S["placed"], 2 * g + 2)
                        dve.tensor_copy(posu[gp][:, :], posf[:, :]).then_inc(S["pos_ok"], 1)
                        dve.wait_ge(S["ginv_ok"], g + 1)
                        dve.tensor_tensor(row[gp][:, :, 2 * D], gexp[:, :], ginv[:, :], ALU.mult).then_inc(S["gate_ok"], 1)
                        dve.wait_ge(S["cnt_ok"], g + 1)
                    for g, gp, gt in due(t, p, r, DVE_AT["router"]):
                        dve.wait_ge(S["lg_ps"], g + 1)
                        dve.tensor_tensor(lg[:, :, :], RA1[0:N, 0:GB * E].rearrange("p (b e) -> p b e", b=GB),
                                          Rw("br").unsqueeze(1).to_broadcast([N, GB, E]), ALU.add).then_inc(S["lg_ok"], 1)
                        dve.wait_ge(S["lg_ok"], g + 1)
                        dve.tensor_reduce(lmax[:, :], lg[:, :, :], AX_X, ALU.max).then_inc(S["chosen"], 1)
                        dve.wait_ge(S["chosen"], 5 * g + 1)
                        dve.tensor_tensor(eqm[:, :, :], lg[:, :, :], lmax[:, :].unsqueeze(2).to_broadcast([N, GB, E]),
                                          ALU.is_equal).then_inc(S["chosen"], 1)
                        dve.wait_ge(S["chosen"], 5 * g + 2)
                        dve.tensor_tensor(eqw[:, :, :], eqm[:, :, :],
                                          Bc("wtab", N).unsqueeze(1).to_broadcast([N, GB, E]), ALU.mult)\
                            .then_inc(S["chosen"], 1)
                        dve.wait_ge(S["chosen"], 5 * g + 3)
                        dve.tensor_reduce(wsel[:, :], eqw[:, :, :], AX_X, ALU.max).then_inc(S["chosen"], 1)
                        dve.wait_ge(S["chosen"], 5 * g + 4)
                        dve.tensor_tensor(oneh[:, :, :], Bc("wtab", N).unsqueeze(1).to_broadcast([N, GB, E]),
                                          wsel[:, :].unsqueeze(2).to_broadcast([N, GB, E]), ALU.is_equal)\
                            .then_inc(S["chosen"], 1)

            windows(dve, window)

            last = cnt[1]
            KB = B * N // BLK
            link(dve.tensor_scalar(padf[:, :], last[:, :], A("iotap"), None, ALU.add))
            link(dve.tensor_copy(tab_p[:, :], last[0:1, :]))
            dve.tensor_copy(padu[:, :], padf[:, :]).then_inc(S["pad_ok"], 1)
            link(dve.tensor_tensor(blk_c[:, :], last[0:1, :], Bc("base", 1), ALU.subtract))
            link(dve.tensor_tensor(blk_g[:, :, :], blk_c[:, :].unsqueeze(2).to_broadcast([1, E, KB]),
                                   Bc("k128", 1).unsqueeze(1).to_broadcast([1, E, KB]), ALU.is_gt))
            link(dve.tensor_reduce(blk_n[:, :], blk_g[:, :, :], AX_X, ALU.add))
            link(dve.tensor_copy(blk_end[:, 0:1], blk_n[:, 0:1]))
            for e in range(1, E):
                link(dve.tensor_tensor(blk_end[:, e:e + 1], blk_end[:, e - 1:e], blk_n[:, e:e + 1], ALU.add))
            link(dve.tensor_tensor(blk_ge[:, :, :], Bc("jtab", 1).unsqueeze(2).to_broadcast([1, NBLK, E]),
                                   blk_end[:, :].unsqueeze(1).to_broadcast([1, NBLK, E]), ALU.is_ge))
            link(dve.tensor_reduce(blk_e[:, :], blk_ge[:, :, :], AX_X, ALU.add))
            link(dve.tensor_tensor(blk_gn[:, :, :], blk_ge[:, :, :],
                                   blk_n[:, :].unsqueeze(1).to_broadcast([1, NBLK, E]), ALU.mult))
            link(dve.tensor_reduce(blk_s[:, :], blk_gn[:, :, :], AX_X, ALU.add))
            link(dve.tensor_tensor(blk_t[:, :], Bc("jtab", 1), blk_s[:, :], ALU.subtract))
            link(dve.tensor_scalar(blk_t2[:, :], blk_t[:, :], float(BLK), None, ALU.mult))
            link(dve.scalar_tensor_tensor(blk_s[:, :], blk_e[:, :], float(REG), blk_t2[:, :], ALU.mult, ALU.add))
            link(dve.tensor_scalar(blk_em[:, :], blk_e[:, :], float(E - 1), None, ALU.min))
            dve.tensor_copy(tab_r[:, :], blk_s[:, :]).then_inc(S["tab_ok"], 1)
            dve.tensor_copy(tab_e[:, :], blk_em[:, :]).then_inc(S["tab_ok"], 1)
            dve.wait_ge(S["tab_ok"], 2)
            dve.wait_ge(S["ld_moe"], 16 * (E + 1))

            def step(j, i, xt, y):
                if xt:
                    e1 = dve.value_load(tab_e[0:1, bass.ds(j + 1, 1)], min_val=0, max_val=E - 1)
                    dve.wait_ge(S["tr_ps"], j + 2)
                    dve.tensor_copy(w1b[(i + 1) % 2][:, :], w1s[:, bass.ds(FF * e1, FF)])
                    dve.tensor_copy(xbT[(i + 1) % 2][:, :], RB0[:, 0:BLK]).then_inc(S["xb_ok"], 1)
                if y:
                    k, n = i % 2, (i - 2) % BUF
                    e = dve.value_load(tab_e[0:1, bass.ds(j - 2, 1)], min_val=0, max_val=E - 1)
                    dve.wait_ge(S["y_ps"], j - 1)
                    dve.tensor_tensor(ytmp[k][:, :], bank[2 + k][:, 0:D],
                                      rw[:, bass.ds(D * e + ROWS["b2"][0], D)], ALU.add).then_inc(S["ytmp_ok"], 1)
                    dve.wait_ge(S["ytmp_ok"], j - 1)
                    dve.scalar_tensor_tensor(yout[n][:, :], ytmp[k][:, :], rin[n][:, 2 * D:2 * D + 1], rin[n][:, 0:D],
                                             ALU.mult, ALU.add).then_inc(S["yo_ok"], 1)

            step(-1, BUF - 1, 1, 0)
            step(0, 0, 1, 0)
            step(1, 1, 1, 0)
            for j in range(2, BUF):
                step(j, j, 1, 1)
            with dve.Fori(1, NBLK // BUF - 1) as t:
                for i in range(BUF):
                    step(BUF * t + i, i, 1, 1)
            for j in range(NBLK - BUF, NBLK + 2):
                step(j, j % BUF, int(j + 1 < NBLK), 1)


def kernel(**inputs):
    import numpy as np
    import concourse.bacc as _bacc
    from concourse import mybir as _mybir
    from concourse.bass_utils import run_bass_kernel_spmd as _run

    x = {k: np.asarray(v) for k, v in inputs.items()}
    f32 = np.float32

    def columns(v):
        return v.reshape(-1, D).T

    def chunked(wt):
        return wt.reshape(-1, D, wt.shape[1]).transpose(1, 0, 2).reshape(D, -1)

    pos = np.zeros((D, D), f32)
    ang = np.arange(N)[:, None].astype(np.float64) / np.power(
        10000.0, 2 * (np.arange(D)[None, :] // 2) / np.float32(D))
    ang[:, 0::2] = np.sin(ang[:, 0::2])
    ang[:, 1::2] = np.cos(ang[:, 1::2])
    pos[:N] = ang
    p = np.arange(D)
    upper = np.zeros((D, N), f32)
    upper[:N] = np.arange(N)[:, None] < np.arange(N)[None, :]
    bmask = np.zeros((D, HH), f32)
    for u in range(2):
        bmask[64 * u:64 * u + 3 * H] = (np.arange(3 * H)[:, None] % H) == HH * u + np.arange(HH)[None, :]

    def rowc(v):
        return np.broadcast_to(np.asarray(v, f32)[None, :], (D, len(v)))

    part_a = {
        "ident": np.eye(D, dtype=f32), "pos": pos, "wq": x["L0_tok_Wq"], "wk": x["L0_tok_Wk"], "wv": x["L0_tok_Wv"],
        "bq": columns(x["L0_tok_bq"]), "bk": columns(x["L0_tok_bk"]), "scale": columns(x["L0_tok_attn_scale"]),
        "iotap": p[:, None].astype(f32)}
    part_b = {
        "wo": x["L0_tok_Wo"], "w1": x["L0_tok_W1"], "w2": chunked(x["L0_tok_W2"]), "qw": x["L0_attn_q_w"].T,
        "kw": x["L0_attn_k_w"].T, "vw": x["L0_attn_v_w"].T, "ow": x["L0_attn_o_w"].T, "wr": x["L0_ffn_Wr"],
        "bv": columns(x["L0_tok_bv"]), "g1": columns(x["L0_tok_g1"]), "beta1": columns(x["L0_tok_beta1"]),
        "bf1": columns(x["L0_tok_bf1"]), "bf2": columns(x["L0_tok_bf2"]), "qb": columns(x["L0_attn_q_b"]),
        "kb": columns(x["L0_attn_k_b"]), "vb": columns(x["L0_attn_v_b"]), "b1": columns(x["L0_ffn_b1"].reshape(-1)),
        "hmask": (p[:, None] // HD % HH == np.arange(HH)[None, :]).astype(f32), "bmask": bmask,
        "base": rowc(np.arange(E) * REG), "wtab": rowc(E - np.arange(E)), "upper": upper,
        "jtab": rowc(np.arange(NBLK)),
        "k128": rowc(np.arange(B * N // BLK) * BLK)}
    pack = [np.ascontiguousarray(np.concatenate([part[k] for k in lay if k != "_"], axis=1))
            for part, lay in ((part_a, LAY_A), (part_b, LAY_B))]
    rows = np.concatenate([x["L0_tok_bo"], x["L0_tok_g2"], x["L0_tok_beta2"], x["L0_attn_o_b"], x["L0_ffn_br"],
                           x["L0_attn_eb_b"], x["L0_ffn_b2"].reshape(-1)])[None, :]
    arrays = {
        "tok": np.ascontiguousarray(x["x"].T), "emb": x["L0_tok_emb"], "pack_a": pack[0], "pack_b": pack[1],
        "rows": rows, "edges": x["L0_attn_edge_index"], "attr": x["L0_attn_edge_attr"],
        "ebw": np.ascontiguousarray(x["L0_attn_eb_w"].T), "w1m": x["L0_ffn_W1"], "w2m": x["L0_ffn_W2"]}

    nc = _bacc.Bacc("TRN2", target_bir_lowering=False, num_devices=1)
    args = [nc.dram_tensor(k, a.shape, _mybir.dt.from_np(a.dtype), kind="ExternalInput").ap()
            for k, a in arrays.items()]
    args.append(nc.dram_tensor("out", (B, N, D), F32, kind="ExternalOutput").ap())
    tower(nc, *args)
    r = _run(nc, [arrays], core_ids=[0])
    return r.results[0]["out"]
```
